# Optimizing a Trainium2 kernel written in Bass

```python
import numpy as np
import jax
import jax.numpy as jnp

def _softmax(x, axis=-1):
    return jax.nn.softmax(x, axis=axis)

def _gelu(x):
    return jax.nn.gelu(x, approximate=True)

def _silu(x):
    return jax.nn.silu(x)

def _sigmoid(x):
    return jax.nn.sigmoid(x)

def _layernorm(x, axis=-1, eps=1e-05):
    m = jnp.mean(x, axis=axis, keepdims=True)
    v = jnp.var(x, axis=axis, keepdims=True)
    return (x - m) / jnp.sqrt(v + eps)

def _scatter_add(tgt, idx, src, axis=0):
    return tgt.at[idx].add(src)

def _segment_sum(src, seg, n):
    return jax.ops.segment_sum(src, seg, n)
kernel_name = 'mk_gnn_ffn_d2_gnn_r32_354527'

def setup_inputs(seed: int=0):
    np.random.seed(seed)
    _w = jnp.asarray

    def _rec_inputs():
        import jax
        import jax.numpy as jnp
        _gk = jax.random.key(seed)
        x = -0.0002117 + 1 * jax.random.normal(jax.random.fold_in(_gk, 1), (3125, 256), jnp.float32)
        _s = jax.random.randint(jax.random.fold_in(_gk, 2), (25000,), 0, 3125, jnp.int32)
        _d = jax.random.randint(jax.random.fold_in(_gk, 3), (25000,), 0, 3125, jnp.int32)
        _loop = jnp.arange(3125, dtype=jnp.int32)
        src = jnp.concatenate([_s, _d, _loop])
        dst = jnp.concatenate([_d, _s, _loop])
        _o = jnp.argsort(dst, stable=True)
        src = src[_o]
        dst = dst[_o]
        edge_attr_64 = 0.000102155 + 1.00015 * jax.random.normal(jax.random.fold_in(_gk, 12), (53125, 64), jnp.float32)
        edge_weight = jax.random.uniform(jax.random.fold_in(_gk, 14), (53125,), jnp.float32, 0.0, 1)
        return (x, src, dst, edge_attr_64, edge_weight)
    x, src, dst, edge_attr_64, edge_weight = _rec_inputs()

    def _L0_gnn_setup():
        import jax, jax.numpy as jnp
        import numpy as np
        N_NODES = 3125
        N_EDGES = 100000
        D_IN = 256
        D_OUT = 256
        key = jax.random.key(seed)
        k1, k2, k3, k4, k5 = jax.random.split(key, 5)
        inputs = jax.random.normal(k1, (N_NODES, D_IN), dtype=jnp.float32)
        init_range = np.sqrt(6.0 / (D_IN + D_OUT)).astype(np.float32)
        weight = jax.random.uniform(k2, (D_IN, D_OUT), dtype=jnp.float32, minval=-init_range, maxval=init_range)
        edge_src = jax.random.randint(k3, (N_EDGES,), 0, N_NODES, dtype=jnp.int32)
        edge_dst = jax.random.randint(k4, (N_EDGES,), 0, N_NODES, dtype=jnp.int32)
        edge_vals = jax.random.uniform(k5, (N_EDGES,), dtype=jnp.float32)
        return {'inputs': inputs, 'weight': weight, 'edge_src': edge_src, 'edge_dst': edge_dst, 'edge_vals': edge_vals}
    _L0_gnn_all = _L0_gnn_setup()
    _L0_gnn_in = {k: v for k, v in _L0_gnn_all.items() if k in ('weight',)}
    del _L0_gnn_all

    def _L0_ffn_setup():
        import math
        import jax, jax.numpy as jnp
        import numpy as np
        CAPACITY_FACTOR = 1.25
        key = jax.random.key(seed)
        ks = jax.random.split(key, 5)
        B, L, D, F, E = (8, 256, 256, 1024, 8)
        h = jax.random.normal(ks[0], (B, L, D), dtype=jnp.float32)
        gate_w = jax.random.normal(ks[1], (D, E), dtype=jnp.float32) * 0.02
        gate_b = jnp.zeros((E,), dtype=jnp.float32)
        w1 = jax.random.normal(ks[2], (E, D, F), dtype=jnp.float32) * (1.0 / math.sqrt(D))
        b1 = jnp.zeros((E, F), dtype=jnp.float32)
        w2 = jax.random.normal(ks[3], (E, F, D), dtype=jnp.float32) * (1.0 / math.sqrt(F))
        b2 = jnp.zeros((E, D), dtype=jnp.float32)
        return {'h': h, 'gate_w': gate_w, 'gate_b': gate_b, 'w1': w1, 'b1': b1, 'w2': w2, 'b2': b2}
    _L0_ffn_all = _L0_ffn_setup()
    _L0_ffn_in = {k: v for k, v in _L0_ffn_all.items() if k in ('gate_w', 'gate_b', 'w1', 'b1', 'w2', 'b2')}
    del _L0_ffn_all

    def _L1_gnn_setup():
        import jax, jax.numpy as jnp
        import numpy as np
        N_NODES = 50000
        N_EDGES = 15625
        HDIM = 256
        EDIM = 64
        MSG_H = 512
        UPD_H = 512
        LN_EPS = 1e-05

        def _mlp(x, W1, b1, W2, b2):
            return jax.nn.relu(x @ W1 + b1) @ W2 + b2

        def _layer_norm(x, gamma, beta):
            mu = jnp.mean(x, axis=-1, keepdims=True)
            var = jnp.mean(jnp.square(x - mu), axis=-1, keepdims=True)
            return (x - mu) * jax.lax.rsqrt(var + LN_EPS) * gamma + beta
        key = jax.random.key(seed)
        ks = jax.random.split(key, 12)

        def lin_init(k, fan_in, fan_out):
            bound = 1.0 / np.sqrt(fan_in)
            return jax.random.uniform(k, (fan_in, fan_out), jnp.float32, -bound, bound)
        h = jax.random.normal(ks[0], (N_NODES, HDIM), jnp.float32)
        edge_index = jax.random.randint(ks[1], (2, N_EDGES), 0, N_NODES, jnp.int64)
        edge_attr = jax.random.normal(ks[2], (N_EDGES, EDIM), jnp.float32)
        eW1 = lin_init(ks[3], 2 * HDIM + EDIM, MSG_H)
        eb1 = jnp.zeros((MSG_H,), jnp.float32)
        eW2 = lin_init(ks[4], MSG_H, HDIM)
        eb2 = jnp.zeros((HDIM,), jnp.float32)
        nW1 = lin_init(ks[5], 2 * HDIM, UPD_H)
        nb1 = jnp.zeros((UPD_H,), jnp.float32)
        nW2 = lin_init(ks[6], UPD_H, HDIM)
        nb2 = jnp.zeros((HDIM,), jnp.float32)
        ln_gamma = jnp.ones((HDIM,), jnp.float32)
        ln_beta = jnp.zeros((HDIM,), jnp.float32)
        return {'h': h, 'edge_index': edge_index, 'edge_attr': edge_attr, 'eW1': eW1, 'eb1': eb1, 'eW2': eW2, 'eb2': eb2, 'nW1': nW1, 'nb1': nb1, 'nW2': nW2, 'nb2': nb2, 'ln_gamma': ln_gamma, 'ln_beta': ln_beta}
    _L1_gnn_all = _L1_gnn_setup()
    _L1_gnn_in = {k: v for k, v in _L1_gnn_all.items() if k in ('eW1', 'eb1', 'eW2', 'eb2', 'nW1', 'nb1', 'nW2', 'nb2', 'ln_gamma', 'ln_beta')}
    del _L1_gnn_all

    def _L1_ffn_setup():
        import jax, jax.numpy as jnp
        import numpy as np
        E = 8
        K = 2
        D = 256
        H = 512
        DOUT = 256
        EPS = 1e-05
        key = jax.random.key(seed)
        ks = jax.random.split(key, 9)
        s = 0.02
        return {'x': jax.random.normal(ks[0], (4, 256, D), jnp.float32), 'gamma': 1.0 + 0.05 * jax.random.normal(ks[1], (D,), jnp.float32), 'beta': 0.05 * jax.random.normal(ks[2], (D,), jnp.float32), 'Wr': 0.01 * jax.random.normal(ks[3], (D, E), jnp.float32), 'br': jnp.zeros((E,), jnp.float32), 'W1': s * jax.random.normal(ks[4], (E, D, H), jnp.float32), 'b1': s * jax.random.normal(ks[5], (E, H), jnp.float32), 'W2': s * jax.random.normal(ks[6], (E, H, DOUT), jnp.float32), 'b2': s * jax.random.normal(ks[7], (E, DOUT), jnp.float32)}
    _L1_ffn_all = _L1_ffn_setup()
    _L1_ffn_in = {k: v for k, v in _L1_ffn_all.items() if k in ('gamma', 'beta', 'Wr', 'br', 'W1', 'b1', 'W2', 'b2')}
    del _L1_ffn_all
    return {'x': x, 'src': src, 'dst': dst, 'edge_attr_64': edge_attr_64, 'edge_weight': edge_weight, 'L0_gnn_weight': _L0_gnn_in['weight'], 'L0_ffn_gate_w': _L0_ffn_in['gate_w'], 'L0_ffn_gate_b': _L0_ffn_in['gate_b'], 'L0_ffn_w1': _L0_ffn_in['w1'], 'L0_ffn_b1': _L0_ffn_in['b1'], 'L0_ffn_w2': _L0_ffn_in['w2'], 'L0_ffn_b2': _L0_ffn_in['b2'], 'L1_gnn_eW1': _L1_gnn_in['eW1'], 'L1_gnn_eb1': _L1_gnn_in['eb1'], 'L1_gnn_eW2': _L1_gnn_in['eW2'], 'L1_gnn_eb2': _L1_gnn_in['eb2'], 'L1_gnn_nW1': _L1_gnn_in['nW1'], 'L1_gnn_nb1': _L1_gnn_in['nb1'], 'L1_gnn_nW2': _L1_gnn_in['nW2'], 'L1_gnn_nb2': _L1_gnn_in['nb2'], 'L1_gnn_ln_gamma': _L1_gnn_in['ln_gamma'], 'L1_gnn_ln_beta': _L1_gnn_in['ln_beta'], 'L1_ffn_gamma': _L1_ffn_in['gamma'], 'L1_ffn_beta': _L1_ffn_in['beta'], 'L1_ffn_Wr': _L1_ffn_in['Wr'], 'L1_ffn_br': _L1_ffn_in['br'], 'L1_ffn_W1': _L1_ffn_in['W1'], 'L1_ffn_b1': _L1_ffn_in['b1'], 'L1_ffn_W2': _L1_ffn_in['W2'], 'L1_ffn_b2': _L1_ffn_in['b2']}

def reference(x, src, dst, edge_attr_64, edge_weight, L0_gnn_weight, L0_ffn_gate_w, L0_ffn_gate_b, L0_ffn_w1, L0_ffn_b1, L0_ffn_w2, L0_ffn_b2, L1_gnn_eW1, L1_gnn_eb1, L1_gnn_eW2, L1_gnn_eb2, L1_gnn_nW1, L1_gnn_nb1, L1_gnn_nW2, L1_gnn_nb2, L1_gnn_ln_gamma, L1_gnn_ln_beta, L1_ffn_gamma, L1_ffn_beta, L1_ffn_Wr, L1_ffn_br, L1_ffn_W1, L1_ffn_b1, L1_ffn_W2, L1_ffn_b2):
    import jax
    import jax.numpy as jnp

    def _L0_gnn_ref(inputs, weight, edge_src, edge_dst, edge_vals):
        import jax, jax.numpy as jnp
        import numpy as np
        N_NODES = 3125
        N_EDGES = 100000
        D_IN = 256
        D_OUT = 256
        x = inputs @ weight
        msgs = edge_vals[:, None] * x[edge_src]
        out = jax.ops.segment_sum(msgs, edge_dst, num_segments=inputs.shape[0])
        return jax.nn.relu(out)

    def _L0_ffn_ref(h, gate_w, gate_b, w1, b1, w2, b2):
        import math
        import jax, jax.numpy as jnp
        import numpy as np
        CAPACITY_FACTOR = 1.25
        B, L, D = h.shape
        E = gate_w.shape[1]
        T = B * L
        C = max(1, math.ceil(CAPACITY_FACTOR * T / E))
        x = h.reshape(T, D)
        logits = x @ gate_w + gate_b
        probs = jax.nn.softmax(logits, axis=-1)
        idx = jnp.argmax(probs, axis=-1)
        prb = jnp.take_along_axis(probs, idx[:, None], axis=1)[:, 0]
        one_hot = jax.nn.one_hot(idx, E, dtype=jnp.float32)
        pos = (jnp.cumsum(one_hot, axis=0) * one_hot).sum(-1).astype(jnp.int32) - 1
        kept = pos < C
        pos_safe = jnp.where(kept, pos, C)
        buf = jnp.zeros((E, C, D), dtype=h.dtype).at[idx, pos_safe].set(x, mode='drop')
        hmid = jax.nn.relu(jnp.einsum('ecd,edf->ecf', buf, w1) + b1[:, None, :])
        ybuf = jnp.einsum('ecf,efd->ecd', hmid, w2) + b2[:, None, :]
        pos_g = jnp.minimum(pos, C - 1)
        y_tok = ybuf[idx, pos_g] * (prb * kept)[:, None]
        y = y_tok.reshape(B, L, D)
        y = jnp.nan_to_num(y, nan=0.0, posinf=10000.0, neginf=-10000.0)
        return y

    def _L1_gnn_ref(h, edge_index, edge_attr, eW1, eb1, eW2, eb2, nW1, nb1, nW2, nb2, ln_gamma, ln_beta):
        import jax, jax.numpy as jnp
        import numpy as np
        N_NODES = 50000
        N_EDGES = 15625
        HDIM = 256
        EDIM = 64
        MSG_H = 512
        UPD_H = 512
        LN_EPS = 1e-05

        def _mlp(x, W1, b1, W2, b2):
            return jax.nn.relu(x @ W1 + b1) @ W2 + b2

        def _layer_norm(x, gamma, beta):
            mu = jnp.mean(x, axis=-1, keepdims=True)
            var = jnp.mean(jnp.square(x - mu), axis=-1, keepdims=True)
            return (x - mu) * jax.lax.rsqrt(var + LN_EPS) * gamma + beta
        src = edge_index[0]
        dst = edge_index[1]
        m_in = jnp.concatenate([h[src], h[dst], edge_attr], axis=1)
        m = _mlp(m_in, eW1, eb1, eW2, eb2)
        agg = jax.ops.segment_sum(m, dst, num_segments=h.shape[0])
        h_upd = _mlp(jnp.concatenate([h, agg], axis=1), nW1, nb1, nW2, nb2)
        return _layer_norm(h + h_upd, ln_gamma, ln_beta)

    def _L1_ffn_ref(x, gamma, beta, Wr, br, W1, b1, W2, b2):
        import jax, jax.numpy as jnp
        import numpy as np
        E = 8
        K = 2
        D = 256
        H = 512
        DOUT = 256
        EPS = 1e-05
        mu = jnp.mean(x, axis=-1, keepdims=True)
        var = jnp.mean(jnp.square(x - mu), axis=-1, keepdims=True)
        xn = (x - mu) * jax.lax.rsqrt(var + EPS) * gamma + beta
        logits = jnp.einsum('bsd,de->bse', xn, Wr) + br
        top_vals, top_idx = jax.lax.top_k(logits, K)
        w = jax.nn.softmax(top_vals, axis=-1)
        w_full = jnp.einsum('bsk,bske->bse', w, jax.nn.one_hot(top_idx, E, dtype=w.dtype))
        y = jnp.zeros(x.shape[:-1] + (DOUT,), x.dtype)
        for e in range(E):
            h = jax.nn.gelu(jnp.einsum('bsd,dh->bsh', xn, W1[e]) + b1[e], approximate=False)
            y_e = jnp.einsum('bsh,hd->bsd', h, W2[e]) + b2[e]
            y = y + y_e * w_full[..., e, None]
        return y
    edge_index = jnp.stack([src, dst])
    x = x + _L0_gnn_ref(_layernorm(x, axis=-1), L0_gnn_weight, src, dst, edge_weight)
    x = x + _L0_ffn_ref(_layernorm(x, axis=-1)[None], L0_ffn_gate_w, L0_ffn_gate_b, L0_ffn_w1, L0_ffn_b1, L0_ffn_w2, L0_ffn_b2)[0]
    x = x + _L1_gnn_ref(_layernorm(x, axis=-1), edge_index, edge_attr_64, L1_gnn_eW1, L1_gnn_eb1, L1_gnn_eW2, L1_gnn_eb2, L1_gnn_nW1, L1_gnn_nb1, L1_gnn_nW2, L1_gnn_nb2, L1_gnn_ln_gamma, L1_gnn_ln_beta)
    x = x + _L1_ffn_ref(_layernorm(x, axis=-1)[None], L1_ffn_gamma, L1_ffn_beta, L1_ffn_Wr, L1_ffn_br, L1_ffn_W1, L1_ffn_b1, L1_ffn_W2, L1_ffn_b2)[0]
    return x

_drawn_inputs = setup_inputs


def setup_inputs(seed=0):
    import zlib

    import numpy as np

    out = dict(_drawn_inputs(seed))
    spreads = {'L0_ffn_gate_b': (0.0, 0.1),
     'L0_ffn_b1': (0.0, 0.8),
     'L0_ffn_b2': (0.0, 0.752),
     'L1_gnn_eb1': (0.0, 0.269),
     'L1_gnn_eb2': (0.0, 0.1),
     'L1_gnn_nb1': (0.0, 0.647),
     'L1_gnn_nb2': (0.0, 0.1),
     'L1_gnn_ln_gamma': (1.0, 0.2),
     'L1_gnn_ln_beta': (0.0, 0.1),
     'L1_ffn_br': (0.0, 0.506)}
    factors = {'edge_attr_64': 3.566,
     'L1_ffn_gamma': 8.0,
     'L1_ffn_beta': 8.0,
     'L1_ffn_Wr': 3.325,
     'L1_ffn_W1': 2.928,
     'L1_ffn_b1': 22.892,
     'L1_ffn_W2': 2.838,
     'L1_ffn_b2': 8.0}
    for name, (base, spread) in spreads.items():
        noise = np.random.default_rng([zlib.crc32(name.encode()), seed]).standard_normal(out[name].shape)
        drawn = base * np.exp(spread * noise) if base else spread * noise
        out[name] = jnp.asarray(drawn.astype(out[name].dtype))
    for name, factor in factors.items():
        out[name] = (out[name] * factor).astype(out[name].dtype)
    return out
```

```python
from contextlib import ExitStack

import concourse.bass as bass
from concourse import mybir

f32, i32, u32 = mybir.dt.float32, mybir.dt.int32, mybir.dt.uint32
ALU, ACT, AX = mybir.AluOpType, mybir.ActivationFunctionType, mybir.AxisListType
ENG = mybir.EngineType
ds = bass.ds

P = 128
NODES, D = 3125, 256
NT = -(-NODES // P)
NPAD = NT * P
TAIL = NODES - (NT - 1) * P
GRP = 5
NG = NT // GRP
WIN = 64
NWIN = -(-NODES // WIN)
NWPAD = 2 * NT
EDGES = 53125
ET = -(-EDGES // P)
ETP, ETQ = 104, 4
EROW = (ET + 1) * P
UN = 8
CHUNK = ET + NWIN - 1
ITERS = CHUNK // UN
TABLE = CHUNK + UN
MAXCHUNKS = -(-ET * NWIN // CHUNK)
DM = 512
ED = 64
E = 8
CAP = -(-5 * NODES // (4 * E))
ESLOT = 512
F0 = 1024
TRASH0 = E * ESLOT
H1 = 512
T1 = (2 * NODES - E) // P + E
TRASH1 = T1 * P
BIGW = NWPAD * DM
EPS = 1e-5
assert ETP * ETQ == ET and CHUNK % UN == 0 and NT % GRP == 0 and ESLOT >= CAP


class Steps:

    def __init__(self, eng, sem, start=0):
        self.eng, self.sem, self.start, self.n = eng, sem, start, 0

    def __call__(self, instruction):
        instruction.then_inc(self.sem, 1)
        self.n += 1
        return instruction

    def wait(self):
        hold(self.eng, self.sem, self.start + self.n)


def hold(eng, sem, value):
    eng.wait_ge(sem, value)
    eng.nop(nofuse=True)


def build(nc, io, out):
    ctx = ExitStack()
    with ctx:
        sb = lambda name, shape, dt=f32: ctx.enter_context(nc.sbuf_tensor(name, shape, dt))
        sem = lambda name: ctx.enter_context(nc.semaphore(name))
        sems = lambda name, n: [sem(f"{name}{k}") for k in range(n)]
        of_phase = []

        def phase_sem(name):
            of_phase.append(nc.alloc_semaphore(name=name))
            return of_phase[-1]
        dram = lambda name, shape, dt=f32: nc.dram_tensor(name, shape, dt).ap()

        def load_regs(eng, ap, lo, hi):
            return nc.values_load_multi_w_load_instructions(
                ap, engines=[eng], min_val=lo, max_val=hi,
                skip_runtime_bounds_check_because="the table is built in range")[1]

        H0 = dram("h0_rows", (NPAD, D))
        BUF0 = dram("expert_in0", (TRASH0 + NPAD, D))
        Y0 = dram("expert_out0", (TRASH0, D))
        PROJ = dram("src_proj", (NPAD, DM))
        BUF1 = dram("expert_in1", (TRASH1 + 2 * NPAD, D))
        Y1 = dram("expert_out1", (TRASH1, D))

        ident = sb("ident", [P, P])
        before = sb("before", [P, P])
        upto = sb("upto", [P, P])
        ones = sb("ones", [P, P])
        zeros = sb("zeros", [P, 1024])
        iota = sb("iota", [P, NWIN * WIN])
        part = sb("part", [P, 1])
        node_id = sb("node_id", [P, NWIN])
        X = sb("X", [P, NT, D])
        src_col = sb("src_col", [P, ET + 1], i32)
        dst_col = sb("dst_col", [P, ET + 1])
        w_col = sb("w_col", [P, ET + 1])
        ends0, starts0, first0 = (sb(n, [ETP, ETQ]) for n in ("ends0", "starts0", "first0"))
        ends, starts, first, nfirst = (sb(n, [ETP, ETQ]) for n in ("ends", "starts", "first", "nfirst"))
        chunks_f, chunks_i = sb("chunks_f", [1, 1]), sb("chunks_i", [1, 1], i32)
        tile_of = sb("tile_of", [1, TABLE], i32)
        win_of = sb("win_of", [1, TABLE], i32)
        CNT = sb("CNT", [WIN, NWPAD])
        idx = sb("idx", [P, UN], i32)
        BIG = sb("BIG", [P, BIGW])
        SCR = sb("SCR", [P, 10240])
        stats = sb("stats", [P, GRP, 6])
        mv = sb("mv", [P, GRP, 2])
        std = sb("std", [P, GRP])
        rstd = sb("rstd", [P, GRP])
        eps = sb("eps", [P, 1])
        SCR2 = sb("SCR2", [P, 2560])
        NIDT = sb("NIDT", [P, NT])
        expert8 = sb("expert8", [P, E])
        LG, OH1, OH2, RT, CUM = (SCR2[:, k * NT * E:(k + 1) * NT * E].rearrange("p (t e) -> p t e", e=E) for k in range(5))
        r_a, r_b, r_c, keep1, keep2 = (sb(n, [P, NT]) for n in ("r_a", "r_b", "r_c", "keep1", "keep2"))
        to1, to2, from1, from2 = (sb(n, [P, NT], i32) for n in ("to1", "to2", "from1", "from2"))
        weights_in = sem("weights_in")

        BANKS = [ctx.enter_context(nc.psum_tensor(f"bank{k}", [P, 512], f32)) for k in range(8)]

        acc0 = BIG[:, 0:NWPAD * 257].rearrange("p (w n) -> p w n", n=257)
        HN = BIG[:, NWPAD * 257:NWPAD * 257 + NT * D].rearrange("p (t d) -> p t d", d=D)
        zero_fill = sem("zero_fill")

        def ln_stats(dve, st, tiles):
            for k in range(GRP):
                st(nc.vector.bn_stats(stats[:, k, :], tiles[:, k, :]))
            st.wait()
            for k in range(GRP):
                st(nc.vector.bn_aggr(mv[:, k, :], stats[:, k, :]))

        def ln_apply(dve, st, tiles, to):
            st(nc.vector.reciprocal(rstd[:], std[:]))
            st.wait()
            for k in range(GRP):
                st(nc.vector.tensor_scalar(to[:, k, :], tiles[:, k, :], mv[:, k, 0:1], rstd[:, k:k + 1],
                                           ALU.subtract, ALU.mult))

        LN_A, LN_B = 2 * GRP, 1 + GRP

        def end_phase():
            with nc.Block() as block:
                clear(block, of_phase)
            for s in of_phase:
                nc.release_semaphore(s)
            of_phase.clear()

        def clear(block, which):
            @block.gpsimd
            def _(pool):
                for s in which:
                    pool.sem_clear(s)

        x_in, e_in, a_ready, a_stats, a_std, a_hn, a_st, a_items, a_const, a_pool = (
            phase_sem(n) for n in ("x_in", "e_in", "a_tail", "a_stats", "a_std", "a_hn", "a_st", "a_items", "a_const", "a_pool"))
        h0_out = phase_sem("h0_out")
        dt_i = SCR[0:ETP, 0:ETQ * P].bitcast(i32).rearrange("p (q e) -> p q e", q=ETQ)
        dst_int = SCR[:, 1024:1024 + ET + 1].bitcast(i32)
        lo_i, hi_i = (SCR[0:ETP, 512 + 8 * k:512 + 8 * k + ETQ].bitcast(i32) for k in range(2))
        lo_f, n_f, incl, one4 = (SCR[0:ETP, 544 + 8 * k:544 + 8 * k + ETQ] for k in range(4))
        chunk_hit = SCR[0:1, 600:600 + MAXCHUNKS]
        with nc.Block() as block:
            @block.sync
            def _(sp):
                sp.wait_ge(a_ready, 1)
                for g in range(NG - 1):
                    sp.dma_start(X[:, g * GRP:(g + 1) * GRP, :],
                                 io["x"][g * GRP * P:(g + 1) * GRP * P, :].rearrange("(t p) d -> p t d", p=P)).then_inc(x_in, 16)
                g = NG - 1
                sp.dma_start(X[:, g * GRP:NT - 1, :],
                             io["x"][g * GRP * P:(NT - 1) * P, :].rearrange("(t p) d -> p t d", p=P)).then_inc(x_in, 16)
                sp.dma_start(X[0:TAIL, NT - 1, :], io["x"][(NT - 1) * P:NODES, :]).then_inc(x_in, 16)
                with sp.Fori(0, NG) as g:
                    sp.wait_ge(a_hn, g + 1)
                    sp.dma_start(H0.rearrange("(t p) d -> p t d", p=P)[:, ds(g * GRP, GRP), :],
                                 HN[:, ds(g * GRP, GRP), :]).then_inc(h0_out, 16)
                sp.wait_ge(h0_out, 16 * NG)

            @block.scalar
            def _(act):
                act.dma_start(dt_i, io["dst_tiles"].rearrange("p (q e) -> p q e", q=ETQ)).then_inc(e_in, 16)
                act.dma_start(dst_int[:], io["dst_col"]).then_inc(e_in, 16)
                act.dma_start(src_col[:], io["src_col"]).then_inc(e_in, 16)
                act.dma_start(w_col[:], io["w_col"]).then_inc(e_in, 16)
                nc.scalar.preload_act_table(ACT.Sqrt)
                with act.Fori(0, NG) as g:
                    hold(act, a_stats, g + 1)
                    nc.scalar.activation(std[:], mv[:, :, 1], ACT.Sqrt, bias=eps[:, 0:1]).then_inc(a_std, 1)

            @block.gpsimd
            def _(pool):
                nc.gpsimd.iota(iota[:], [[1, NWIN * WIN]], base=0, channel_multiplier=0,
                               allow_small_or_imprecise_dtypes=True).then_inc(a_const, 1)
                nc.gpsimd.iota(part[:], [[1, 1]], base=0, channel_multiplier=1,
                               allow_small_or_imprecise_dtypes=True).then_inc(a_const, 1)
                nc.gpsimd.iota(node_id[:], [[WIN, NWIN]], base=0, channel_multiplier=1,
                               allow_small_or_imprecise_dtypes=True).then_inc(a_const, 1)
                nc.gpsimd.iota(NIDT[:], [[P, NT]], base=0, channel_multiplier=1,
                               allow_small_or_imprecise_dtypes=True)
                nc.gpsimd.iota(expert8[:], [[1, E]], base=-E, channel_multiplier=0,
                               allow_small_or_imprecise_dtypes=True)
                nc.gpsimd.memset(zeros[:], 0.0)
                nc.gpsimd.memset(BIG[:, 0:NWPAD * 257], 0.0)

            @block.vector
            def _(dve):
                nc.vector.memset(eps[:], EPS)
                nc.vector.memset(X[:, NT - 1, :], 0.0).then_inc(a_ready, 1)
                nc.vector.memset(ones[:], 1.0)
                dve.wait_ge(a_const, 3)
                nc.vector.tensor_scalar(ident[:], iota[:, 0:P], part[:, 0:1], None, ALU.is_equal)
                nc.vector.tensor_scalar(before[:], iota[:, 0:P], part[:, 0:1], None, ALU.is_gt)
                nc.vector.tensor_scalar(upto[:], iota[:, 0:P], part[:, 0:1], None, ALU.is_ge)
                st = Steps(dve, a_items)
                st(nc.vector.memset(one4, 1.0))
                dve.wait_ge(e_in, 64)
                st(nc.vector.tensor_reduce(lo_i, dt_i, AX.X, ALU.min))
                st(nc.vector.tensor_reduce(hi_i, dt_i, AX.X, ALU.max))
                st.wait()
                shift = WIN.bit_length() - 1
                st(nc.vector.tensor_scalar(lo_i, lo_i, shift, None, ALU.arith_shift_right))
                st(nc.vector.tensor_scalar(hi_i, hi_i, shift, None, ALU.arith_shift_right))
                st.wait()
                st(nc.vector.tensor_copy(lo_f, lo_i))
                st.wait()
                st(nc.vector.scalar_tensor_tensor(n_f, hi_i, 1.0, lo_f, ALU.add, ALU.subtract))
                st.wait()
                st(nc.vector.tensor_tensor_scan(incl, one4, n_f, 0.0, ALU.mult, ALU.add))
                st.wait()
                items_a = st.n
                st(nc.vector.tensor_copy(dst_col[:], dst_int[:]))
                dve.wait_ge(a_pool, 1)
                st(nc.vector.tensor_scalar(ends0[:], incl, BANKS[0][0:ETP, 0:1], None, ALU.add))
                st(nc.vector.tensor_scalar(chunk_hit, iota[0:1, 0:MAXCHUNKS], float(CHUNK), BANKS[1][0:1, 0:1], ALU.mult, ALU.is_lt))
                st.wait()
                st(nc.vector.tensor_tensor(starts0[:], ends0[:], n_f, ALU.subtract))
                st(nc.vector.tensor_reduce(chunks_f[:], chunk_hit, AX.X, ALU.add))
                st.wait()
                st(nc.vector.tensor_tensor(first0[:], lo_f, starts0[:], ALU.subtract))
                st(nc.vector.tensor_copy(chunks_i[:], chunks_f[:]))
                dve.wait_ge(x_in, 16 * (NG + 1))
                with dve.Fori(0, NG) as g:
                    tiles = X[:, ds(g * GRP, GRP), :]
                    st = Steps(dve, a_st, g * (LN_A + LN_B))
                    ln_stats(dve, st, tiles)
                    st.wait()
                    dve.sem_inc(a_stats, 1)
                    hold(dve, a_std, g + 1)
                    ln_apply(dve, st, tiles, HN[:, ds(g * GRP, GRP), :])
                    st.wait()
                    dve.sem_inc(a_hn, 1)

            @block.tensor
            def _(pe):
                pe.wait_ge(a_items, 8)
                nc.tensor.matmul(BANKS[0][0:ETP, 0:1], before[0:ETP, 0:ETP], incl[:, ETQ - 1:ETQ], start=True, stop=True)
                nc.tensor.matmul(BANKS[1][0:1, 0:1], ones[0:ETP, 0:1], incl[:, ETQ - 1:ETQ], start=True, stop=True).then_inc(a_pool, 1)

        n_chunks = nc.values_load(chunks_i[0:1, 0:1], min_val=1, max_val=MAXCHUNKS,
                                  skip_runtime_bounds_check_because="counted up to MAXCHUNKS")

        end_phase()

        t_m, t_pe, t_up, t_st = (sem(n) for n in ("t_masks", "t_sums", "t_done", "t_st"))
        table_sems = [t_m, t_pe, t_up, t_st]
        past_end = SCR[0:ETP, 0:ETQ * TABLE].rearrange("p (q j) -> p q j", q=ETQ)
        past_start = SCR[0:ETP, ETQ * TABLE:2 * ETQ * TABLE].rearrange("p (q j) -> p q j", q=ETQ)

        def start_items(block):
            @block.vector
            def _(dve):
                nc.vector.tensor_copy(ends[:], ends0[:])
                nc.vector.tensor_copy(starts[:], starts0[:])
                nc.vector.tensor_copy(first[:], first0[:])
                nc.vector.tensor_scalar(nfirst[:], first0[:], -1.0, None, ALU.mult)

        def build_table(block):
            @block.vector
            def _(dve):
                for q in range(ETQ):
                    nc.vector.tensor_scalar(past_end[:, q, :], iota[0:ETP, 0:TABLE], ends[:, q:q + 1], None, ALU.is_ge).then_inc(t_m, 1)
                    nc.vector.tensor_scalar(past_start[:, q, :], iota[0:ETP, 0:TABLE], starts[:, q:q + 1], None, ALU.is_ge).then_inc(t_m, 1)
                dve.wait_ge(t_pe, 1)
                st = Steps(dve, t_st)
                st(nc.vector.tensor_copy(tile_of[:], BANKS[0][0:1, 0:TABLE]))
                st(nc.vector.tensor_tensor(SCR[0:1, 0:TABLE], BANKS[1][0:1, 0:TABLE], iota[0:1, 0:TABLE], ALU.add))
                st.wait()
                nc.vector.tensor_scalar(win_of[:], SCR[0:1, 0:TABLE], float(NWIN - 1), None, ALU.min)
                for t, by in ((ends, -CHUNK), (starts, -CHUNK), (first, CHUNK), (nfirst, -CHUNK)):
                    nc.vector.tensor_scalar(t[:], t[:], float(by), None, ALU.add)

            @block.tensor
            def _(pe):
                for q in range(ETQ):
                    pe.wait_ge(t_m, 2 * (q + 1))
                    last = q == ETQ - 1
                    nc.tensor.matmul(BANKS[0][0:1, 0:TABLE], ones[0:ETP, 0:1], past_end[:, q, :], start=q == 0, stop=last)
                    nc.tensor.matmul(BANKS[1][0:1, 0:TABLE], first[:, q:q + 1], past_start[:, q, :], start=q == 0, stop=False)
                    m = nc.tensor.matmul(BANKS[1][0:1, 0:TABLE], nfirst[:, q:q + 1], past_end[:, q, :], start=False, stop=last)
                m.then_inc(t_pe, 1)

        rows_in = sems("rows_in", UN)
        rows_in1 = sems("rows1_in", UN)
        b_idx, b_scaled, b_S, b_pe, b_acc = (sem(n) for n in ("b_idx", "b_scaled", "b_onehot", "b_summed", "b_acc"))
        b_sems = [b_idx, b_scaled, b_S, b_pe, b_acc]
        rows0 = SCR[:, 0:UN * D].rearrange("p (k n) -> p k n", n=D)
        msg0 = SCR[:, UN * D:UN * D + 4 * 257].rearrange("p (k n) -> p k n", n=257)
        S0 = SCR[:, 3200:3200 + 4 * WIN].rearrange("p (k n) -> p k n", n=WIN)

        def gather_items(pool, table, ring, source, arrived, done):
            def copy_index(slot, t):
                nc.gpsimd.tensor_copy(idx[:, slot:slot + 1], src_col[:, ds(t, 1)]).then_inc(b_idx, 1)
            ahead = UN // 2
            for k, t in enumerate(load_regs(ENG.Pool, table[0:1, 0:ahead], 0, ET)):
                copy_index(k, t)
            with pool.Fori(0, ITERS) as i:
                ts = load_regs(ENG.Pool, table[0:1, ds(i * UN + ahead, UN)], 0, ET)
                for k in range(UN):
                    hold(pool, done, i * UN + (k + 1 + ahead))
                    copy_index((k + ahead) % UN, ts[k])
                    hold(pool, b_idx, i * UN + (k + 1))
                    nc.gpsimd.indirect_dma_start(
                        out=ring[:, k, :], out_offset=None, in_=source,
                        in_offset=bass.IndirectOffsetOnAxis(ap=idx[:, k:k + 1].bitcast(u32), axis=0)).then_inc(arrived[k], 16)

        def edge_sum0(block, chunk):
            @block.gpsimd
            def _(pool):
                gather_items(pool, tile_of, rows0, H0, rows_in, b_scaled)

            @block.scalar
            def _(act):
                nc.scalar.preload_act_table(ACT.Copy)
                act.sem_inc(b_scaled, UN)
                with act.Fori(0, ITERS) as i:
                    ts = load_regs(ENG.Activation, tile_of[0:1, ds(i * UN, UN)], 0, ET)
                    for k in range(UN):
                        act.wait_ge(rows_in[k], chunk * (ITERS * 16) + i * 16 + 16)
                        act.nop(nofuse=True)
                        hold(act, b_pe, i * UN + (k + 1))
                        nc.scalar.activation(msg0[:, k % 4, 0:D], rows0[:, k, :], ACT.Copy,
                                             scale=w_col[:, ds(ts[k], 1)]).then_inc(b_scaled, 1)

            @block.vector
            def _(dve):
                nc.vector.memset(msg0[:, :, D:D + 1], 1.0).then_inc(b_S, 1)
                dve.sem_inc(b_acc, 4)
                with dve.Fori(0, ITERS) as i:
                    ts = load_regs(ENG.DVE, tile_of[0:1, ds(i * UN, UN)], 0, ET)
                    ws = load_regs(ENG.DVE, win_of[0:1, ds(i * UN, UN)], 0, NWIN - 1)

                    def onehot(k):
                        hold(dve, b_pe, i * UN + (k + 1))
                        nc.vector.tensor_scalar(S0[:, k % 4, :], iota[:, ds(ws[k] * WIN, WIN)], dst_col[:, ds(ts[k], 1)],
                                                None, ALU.is_equal).then_inc(b_S, 1)
                    onehot(0)
                    onehot(1)
                    for k in range(UN):
                        if k + 2 < UN:
                            onehot(k + 2)
                        hold(dve, b_pe, i * UN + (k + 5))
                        hold(dve, b_acc, i * UN + (k + 4))
                        a = acc0[0:WIN, ds(ws[k], 1), :]
                        nc.vector.tensor_tensor(a, a, BANKS[k % 4][0:WIN, 0:257].rearrange("p (o n) -> p o n", o=1), ALU.add).then_inc(b_acc, 1)

            @block.tensor
            def _(pe):
                pe.sem_inc(b_pe, 4)
                with pe.Fori(0, ITERS) as i:
                    for k in range(UN):
                        pe.wait_ge(b_S, i * UN + (k + 2))
                        pe.wait_ge(b_scaled, i * UN + (k + 1 + UN))
                        pe.wait_ge(b_acc, i * UN + (k + 1))
                        nc.tensor.matmul(BANKS[k % 4][0:WIN, 0:257], S0[:, k % 4, :], msg0[:, k % 4, :],
                                         start=True, stop=True).then_inc(b_pe, 1)

        with nc.Block() as block:
            start_items(block)

            @block.sync
            def _(sp):
                for buf, rows in ((BUF0, TRASH0), (BUF1, TRASH1)):
                    flat = buf[0:rows, :].rearrange("(p r) d -> p (r d)", p=P)
                    width = flat.shape[1]
                    for a in range(0, width, 1024):
                        sp.dma_start(flat[:, a:a + 1024], zeros[:]).then_inc(zero_fill, 16)
        with nc.Fori(0, n_chunks) as chunk:
            with nc.Block() as block:
                build_table(block)
            with nc.Block() as block:
                edge_sum0(block, chunk)
            with nc.Block() as block:
                clear(block, table_sems + b_sems)

        def group(t3, g):
            return t3[:, ds(g * GRP, GRP), :]

        def t_bank(k):
            return BANKS[k // 2][:, (k % 2) * 256:(k % 2) * 256 + 256].rearrange("p (c n) -> p c n", c=2)

        def pe_transposes(stage):
            for k in range(GRP):
                for c in range(2):
                    m = nc.tensor.transpose(t_bank(k)[:, c, :], stage[:, k, c * P:(c + 1) * P], ident[:])
            return m

        def act_evacuate(to):
            nc.scalar.activation(to[:, 0:512], BANKS[0][:, :], ACT.Copy)
            nc.scalar.activation(to[:, 512:1024], BANKS[1][:, :], ACT.Copy)
            return nc.scalar.activation(to[:, 1024:1280], BANKS[2][:, 0:256], ACT.Copy)

        stage_acc = SCR[0:WIN, 0:2560].rearrange("p (w n) -> p w n", n=D)
        xt_flat = SCR[:, 2560:3840]
        xt = xt_flat.rearrange("p (k c n) -> p k c n", c=2, n=P)
        hstage = SCR[:, 3840:5120].rearrange("p (k n) -> p k n", n=D)
        W0s = SCR[:, 5120:5632].rearrange("p (c n) -> p c n", c=2)
        gate_ws = SCR[:, 5632:5648].rearrange("p (c n) -> p c n", c=2)
        gate_bs = SCR[:, 5648:5656]

        c_stage, c_T, c_ev, c_O, c_stats, c_std, c_h, c_L, c_lg, c_pool, c_st = (
            phase_sem("c_" + n) for n in ("stage", "transposed", "evacuated", "sums", "stats", "std", "norm", "logits", "logits_read", "copied", "st"))
        O_PAIRS = ((3, 0, 2), (4, 2, 2), (5, 4, 1))

        def node_update0(block):
            @block.sync
            def _(sp):
                sp.dma_start(W0s, io["L0_gnn_weight"].rearrange("(c p) n -> p c n", p=P)).then_inc(weights_in, 16)
                sp.dma_start(gate_ws, io["L0_ffn_gate_w"].rearrange("(c p) n -> p c n", p=P)).then_inc(weights_in, 16)
                sp.dma_start(gate_bs, io["L0_ffn_gate_b"].partition_broadcast(P)).then_inc(weights_in, 16)

            @block.scalar
            def _(act):
                nc.scalar.preload_act_table(ACT.Sqrt)
                nc.scalar.activation(CNT[:], acc0[0:WIN, :, D], ACT.Copy)
                act.sem_inc(c_ev, 1)
                with act.Fori(0, NG) as g:
                    hold(act, c_T, 2 * g + 1)
                    nc.scalar.activation(stage_acc[:, :, :], acc0[0:WIN, ds(g * 2 * GRP, 2 * GRP), 0:D], ACT.Copy).then_inc(c_stage, 1)
                    hold(act, c_L, g + 1)
                    hold(act, c_T, 2 * g + 3)
                    act_evacuate(xt_flat).then_inc(c_ev, 1)
                    hold(act, c_stats, g + 1)
                    nc.scalar.activation(std[:], mv[:, :, 1], ACT.Sqrt, bias=eps[:, 0:1]).then_inc(c_std, 1)
                    hold(act, c_T, 2 * g + 4)
                    act_evacuate(xt_flat).then_inc(c_ev, 1)

            @block.tensor
            def _(pe):
                pe.sem_inc(c_T, 2)
                pe.sem_inc(c_L, 1)
                pe.wait_ge(weights_in, 48)
                with pe.Fori(0, NG) as g:
                    pe.wait_ge(c_stage, g + 1)
                    hold(pe, c_ev, 2 * g + 1)
                    for k in range(GRP):
                        for c in range(2):
                            for a in range(2):
                                m = nc.tensor.transpose(t_bank(k)[:, c, a * WIN:(a + 1) * WIN],
                                                        stage_acc[:, 2 * k + a, c * P:(c + 1) * P], ident[0:WIN, 0:WIN])
                    m.then_inc(c_T, 1)
                    pe.wait_ge(c_ev, 2 * g + 2)
                    for bank, t0, n in O_PAIRS:
                        for k in range(t0, t0 + n):
                            for c in range(2):
                                m = nc.tensor.matmul(BANKS[bank][:, (k - t0) * D:(k - t0 + 1) * D], xt[:, k, c, :], W0s[:, c, :],
                                                     start=c == 0, stop=c == 1)
                        m.then_inc(c_O, 1)
                    pe.wait_ge(c_h, g + 1)
                    pe_transposes(hstage).then_inc(c_T, 1)
                    pe.wait_ge(c_ev, 2 * g + 3)
                    pe.wait_ge(c_lg, g + 1)
                    for k in range(GRP):
                        for c in range(2):
                            m = nc.tensor.matmul(BANKS[6][:, k * E:(k + 1) * E], xt[:, k, c, :], gate_ws[:, c, :], start=c == 0, stop=c == 1)
                    m.then_inc(c_L, 1)

            @block.vector
            def _(dve):
                dve.sem_inc(c_lg, 1)
                dve.wait_ge(weights_in, 48)
                with dve.Fori(0, NG) as g:
                    st = Steps(dve, c_st, g * (len(O_PAIRS) + LN_A + LN_B))
                    for q, (bank, t0, n) in enumerate(O_PAIRS):
                        hold(dve, c_O, len(O_PAIRS) * g + (q + 1))
                        xs = X[:, ds(g * GRP + t0, n), :]
                        st(nc.vector.scalar_tensor_tensor(xs, BANKS[bank][:, 0:n * D].rearrange("p (k n) -> p k n", n=D), 0.0, xs,
                                                          ALU.max, ALU.add))
                    st.wait()
                    ln_stats(dve, st, group(X, g))
                    st.wait()
                    dve.sem_inc(c_stats, 1)
                    hold(dve, c_std, g + 1)
                    hold(dve, c_T, 2 * g + 2)
                    hold(dve, c_pool, g + 1)
                    ln_apply(dve, st, group(X, g), hstage)
                    st.wait()
                    dve.sem_inc(c_h, 1)
                    hold(dve, c_L, g + 2)
                    nc.vector.tensor_tensor(group(LG, g), BANKS[6][:, 0:GRP * E].rearrange("p (k e) -> p k e", e=E),
                                            gate_bs.unsqueeze(1).to_broadcast([P, GRP, E]), ALU.add).then_inc(c_lg, 1)

            @block.gpsimd
            def _(pool):
                pool.sem_inc(c_pool, 1)
                with pool.Fori(0, NG) as g:
                    hold(pool, c_h, g + 1)
                    nc.gpsimd.tensor_copy(group(HN, g), hstage).then_inc(c_pool, 1)

        with nc.Block() as block:
            node_update0(block)

        def bce(t2):
            return t2[:].unsqueeze(2).to_broadcast([P, NT, E])

        def bct(row):
            return row.unsqueeze(1).to_broadcast([P, NT, E])

        def first_best(st, logits, best, onehot, scratch):
            st(nc.vector.tensor_reduce(best[:], logits[:], AX.X, ALU.max))
            st.wait()
            st(nc.vector.tensor_tensor(onehot[:], logits[:], bce(best), ALU.is_equal))
            st.wait()
            st(nc.vector.tensor_tensor(onehot[:], onehot[:], bct(expert8[:]), ALU.mult))
            st.wait()
            st(nc.vector.tensor_reduce(scratch[:], onehot[:], AX.X, ALU.min))
            st.wait()
            st(nc.vector.tensor_tensor(onehot[:], bct(expert8[:]), bce(scratch), ALU.is_equal))
            st.wait()

        def ranks(dve, st, counted, ready, summed, wait_value):
            st.wait()
            dve.sem_inc(ready, 1)
            dve.wait_ge(summed, wait_value)
            for e in range(E):
                st(nc.vector.tensor_tensor_scan(CUM[:, :, e], ones[:, 0:NT], BANKS[1][:, 0:NT * E].rearrange("p (t e) -> p t e", e=E)[:, :, e],
                                                0.0, ALU.mult, ALU.add))
            st(nc.vector.tensor_copy(RT[:], BANKS[1][:, 0:NT * E].rearrange("p (t e) -> p t e", e=E)))
            st.wait()
            st(nc.vector.tensor_tensor(RT[:], CUM[:], RT[:], ALU.subtract))
            st.wait()
            st(nc.vector.tensor_tensor(RT[:], RT[:], BANKS[0][:, 0:NT * E].rearrange("p (t e) -> p t e", e=E), ALU.add))
            st.wait()

        def pe_ranks(pe, counted, ready, summed, value):
            pe.wait_ge(ready, value)
            flat = counted[:].rearrange("p t e -> p (t e)")
            nc.tensor.matmul(BANKS[0][:, 0:NT * E], upto[:], flat, start=True, stop=True)
            nc.tensor.matmul(BANKS[1][:, 0:NT * E], ones[:], flat, start=True, stop=True).then_inc(summed, 1)

        r_st, r_ready, r_sum, r_exp = (phase_sem("r_" + n) for n in ("st", "ready", "summed", "exp"))
        r_done = sem("r_scattered")

        def route0(block):
            @block.vector
            def _(dve):
                st = Steps(dve, r_st)
                first_best(st, LG, r_a, OH1, r_b)
                st(nc.vector.tensor_tensor(LG[:], LG[:], bce(r_a), ALU.subtract))
                st.wait()
                dve.sem_inc(r_exp, 1)
                ranks(dve, st, OH1, r_ready, r_sum, 1)
                st(nc.vector.tensor_tensor(RT[:], RT[:], OH1[:], ALU.mult))
                st.wait()
                st(nc.vector.tensor_reduce(r_c[:], RT[:], AX.X, ALU.add))
                st.wait()
                st(nc.vector.tensor_scalar(keep1[:], r_c[:], float(CAP), None, ALU.is_le))
                st(nc.vector.tensor_scalar(r_b[:], r_b[:], float(ESLOT), float(E * ESLOT - 1), ALU.mult, ALU.add))
                st(nc.vector.tensor_scalar(r_a[:], r_c[:], float(CAP), None, ALU.min))
                st.wait()
                st(nc.vector.tensor_tensor(r_a[:], r_a[:], r_b[:], ALU.add))
                st.wait()
                st(nc.vector.tensor_scalar(r_b[:], NIDT[:], float(TRASH0), None, ALU.add))
                st.wait()
                st(nc.vector.tensor_copy(from1[:], r_a[:]))
                st.wait()
                st(nc.vector.tensor_tensor(r_a[:], r_a[:], r_b[:], ALU.subtract))
                st.wait()
                st(nc.vector.tensor_tensor(r_a[:], r_a[:], keep1[:], ALU.mult))
                st.wait()
                st(nc.vector.tensor_tensor(r_a[:], r_a[:], r_b[:], ALU.add))
                st.wait()
                st(nc.vector.tensor_copy(to1[:], r_a[:]))
                st.wait()
                dve.sem_inc(r_ready, 1)
                dve.wait_ge(r_exp, 2)
                st(nc.vector.tensor_reduce(r_c[:], LG[:], AX.X, ALU.add))
                st.wait()
                st(nc.vector.reciprocal(r_c[:], r_c[:]))
                st.wait()
                st(nc.vector.tensor_tensor(keep1[:], keep1[:], r_c[:], ALU.mult))

            @block.scalar
            def _(act):
                act.wait_ge(r_exp, 1)
                nc.scalar.activation(LG[:], LG[:], ACT.Exp).then_inc(r_exp, 1)

            @block.tensor
            def _(pe):
                pe_ranks(pe, OH1, r_ready, r_sum, 1)

            @block.gpsimd
            def _(pool):
                pool.wait_ge(zero_fill, 16 * (TRASH0 + TRASH1) * D // (P * 1024))
                pool.wait_ge(r_ready, 2)
                for t in range(NT):
                    nc.gpsimd.indirect_dma_start(
                        out=BUF0, out_offset=bass.IndirectOffsetOnAxis(ap=to1[:, t:t + 1].bitcast(u32), axis=0),
                        in_=HN[:, t, :], in_offset=None).then_inc(r_done, 16)
                pool.wait_ge(r_done, 16 * NT)

        with nc.Block() as block:
            route0(block)

        end_phase()

        d_w, d_x = ([phase_sem(f"{n}{k}") for k in range(2)] for n in ("d_weights", "d_rows"))
        d_T, d_xT, d_h, d_hT, d_y, d_ys = (phase_sem("d_" + n) for n in ("transposed", "xT", "hidden", "relu", "y", "y_staged"))
        d_store, d_free = sem("d_store"), phase_sem("d_stage_free")
        w1s = [BIG[:, a * 4096:a * 4096 + 2048].rearrange("p (c f) -> p c f", c=2) for a in range(2)]
        w2s = [BIG[:, a * 4096 + 2048:a * 4096 + 4096].rearrange("p (f n) -> p f n", n=D) for a in range(2)]
        hT = [BIG[:, 8192 + a * 4096:8192 + (a + 1) * 4096].rearrange("p (f s) -> p f s", s=ESLOT) for a in range(2)]
        xin = [SCR[:, a * 1024:(a + 1) * 1024].rearrange("p (s n) -> p s n", n=D) for a in range(2)]
        xT = [SCR[:, 2048 + a * 1024:2048 + (a + 1) * 1024].rearrange("p (c s) -> p c s", c=2) for a in range(2)]
        ys = [SCR[:, 4096 + a * 1024:4096 + (a + 1) * 1024].rearrange("p (s n) -> p s n", n=D) for a in range(2)]
        b2s = SCR[:, 6144:6144 + E * D].rearrange("p (e n) -> p e n", e=E)
        b1s = SCR[:, 8192:8192 + 64]
        d_bias = phase_sem("d_bias")
        NF = F0 // P
        NS = ESLOT // P

        def experts0(block):
            @block.sync
            def _(sp):
                sp.dma_start(b1s, io["b1_col"]).then_inc(d_bias, 16)
                sp.dma_start(b2s, io["L0_ffn_b2"].rearrange("e n -> (e n)").partition_broadcast(P).rearrange("p (e n) -> p e n", e=E)).then_inc(d_bias, 16)
                with sp.Fori(0, E // 2) as i:
                    for a in range(2):
                        hold(sp, d_y, NS * (2 * i + a) + NS + 1)
                        sp.dma_start(xin[a], BUF0[ds((2 * i + a) * ESLOT, ESLOT), :].rearrange("(s p) n -> p s n", p=P)).then_inc(d_x[a], 16)
                        sp.dma_start(w1s[a], io["L0_ffn_w1"][ds(2 * i + a, 1), :, :].rearrange("e (c p) f -> p (e c) f", p=P)).then_inc(d_w[a], 16)
                        sp.dma_start(w2s[a], io["L0_ffn_w2"][ds(2 * i + a, 1), :, :].rearrange("e (f p) n -> p (e f) n", p=P)).then_inc(d_w[a], 16)

            @block.tensor
            def _(pe):
                pe.sem_inc(d_y, 2 * NS + 1)
                with pe.Fori(0, E // 2) as i:
                    for a in range(2):
                        n = 2 * i + a
                        pe.wait_ge(d_x[a], i * 16 + 16)
                        pe.wait_ge(d_xT, n + 1)
                        for s in range(NS):
                            for c in range(2):
                                m = nc.tensor.transpose(BANKS[c][:, s * P:(s + 1) * P], xin[a][:, s, c * P:(c + 1) * P], ident[:])
                        m.then_inc(d_T, 1)
                    for a in range(2):
                        n = 2 * i + a
                        pe.wait_ge(d_xT, n + 2)
                        pe.wait_ge(d_w[a], i * 32 + 32)
                        for f in range(NF):
                            pe.wait_ge(d_hT, n * NF + (f + 1))
                            for c in range(2):
                                m = nc.tensor.matmul(BANKS[2 + f % 4][:, 0:ESLOT], w1s[a][:, c, f * P:(f + 1) * P], xT[a][:, c, :],
                                                     start=c == 0, stop=c == 1)
                            m.then_inc(d_h, 1)
                        pe.wait_ge(d_hT, (n + 1) * NF + 4)
                        for s in range(NS):
                            pe.wait_ge(d_ys, n * NS + (s + 1))
                            for f in range(NF):
                                m = nc.tensor.matmul(BANKS[6 + s % 2][:, 0:D], hT[a][:, f, s * P:(s + 1) * P], w2s[a][:, f, :],
                                                     start=f == 0, stop=f == NF - 1)
                            m.then_inc(d_y, 1)

            @block.scalar
            def _(act):
                act.sem_inc(d_xT, 1)
                act.sem_inc(d_hT, 4)
                nc.scalar.preload_act_table(ACT.Relu)
                act.wait_ge(d_bias, 32)
                with act.Fori(0, E // 2) as i:
                    for a in range(2):
                        n = 2 * i + a
                        hold(act, d_T, n + 1)
                        nc.scalar.activation(xT[a][:, 0, :], BANKS[0][:, :], ACT.Copy)
                        nc.scalar.activation(xT[a][:, 1, :], BANKS[1][:, :], ACT.Copy).then_inc(d_xT, 1)
                    for a in range(2):
                        n = 2 * i + a
                        for f in range(NF):
                            hold(act, d_h, n * NF + (f + 1))
                            nc.scalar.activation(hT[a][:, f, :], BANKS[2 + f % 4][:, 0:ESLOT], ACT.Relu,
                                                 bias=b1s[:, ds(n * NF + f, 1)]).then_inc(d_hT, 1)

            @block.vector
            def _(dve):
                dve.sem_inc(d_ys, 2)
                dve.wait_ge(d_bias, 32)
                with dve.Fori(0, E // 2) as i:
                    for a in range(2):
                        n = 2 * i + a
                        hold(dve, d_free, n + 1)
                        for s in range(NS):
                            hold(dve, d_y, n * NS + (s + 2 + 2 * NS))
                            nc.vector.tensor_tensor(ys[a][:, s:s + 1, :], BANKS[6 + s % 2][:, 0:D].unsqueeze(1), b2s[:, ds(n, 1), :],
                                                    ALU.add).then_inc(d_ys, 1)

            @block.gpsimd
            def _(pool):
                pool.sem_inc(d_free, 2)
                with pool.Fori(0, E // 2) as i:
                    for a in range(2):
                        n = 2 * i + a
                        hold(pool, d_ys, (n + 1) * NS + 2)
                        nc.gpsimd.dma_start(Y0[ds(n * ESLOT, ESLOT), :].rearrange("(s p) n -> p s n", p=P), ys[a]).then_inc(d_store, 16)
                        hold(pool, d_store, n * 16 + 16)
                        pool.sem_inc(d_free, 1)

        with nc.Block() as block:
            experts0(block)

        GY = SCR[:, 0:1280].rearrange("p (k n) -> p k n", n=D)
        eW1s = SCR[:, 5120:5120 + 4 * DM].rearrange("p (c n) -> p c n", n=DM)
        eb1s = SCR[:, 7168:7168 + DM]
        pstage = SCR[:, 7680:7680 + 5 * DM].rearrange("p (k n) -> p k n", n=DM)
        finite = SCR2[:, 0:1280].bitcast(i32).rearrange("p (k n) -> p k n", n=D)
        beyond = SCR2[:, 1280:2560].rearrange("p (k n) -> p k n", n=D)
        below = SCR[:, 1280:2560].rearrange("p (k n) -> p k n", n=D)
        Q = BIG[0:WIN, :].rearrange("p (w n) -> p w n", n=DM)
        acc1 = BIG[WIN:P, :].rearrange("p (w n) -> p w n", n=DM)
        e_gy = sems("e_rows", GRP)
        e_idx, e_used, e_sign, e_y, e_T, e_xt, e_stats, e_std, e_h, e_pq, e_p, e_q, e_ps, e_store, e_st, e_w, e_pr = (
            phase_sem("e_" + n) for n in ("index", "rows_used", "replacement", "scaled", "transposed", "xt", "stats", "std", "norm",
                                    "products", "src_read", "dst_read", "store_done", "store", "st", "weights", "pair_read"))

        def project(block):
            @block.sync
            def _(sp):
                sp.dma_start(eW1s, io["L1_gnn_eW1"][0:4 * P, :].rearrange("(c p) n -> p c n", p=P)).then_inc(e_w, 16)
                sp.dma_start(eb1s, io["L1_gnn_eb1"].partition_broadcast(P)).then_inc(e_w, 16)
                sp.sem_inc(e_ps, 1)
                with sp.Fori(0, NG) as g:
                    hold(sp, e_p, GRP * g + GRP + 1)
                    sp.dma_start(PROJ.rearrange("(t p) n -> p t n", p=P)[:, ds(g * GRP, GRP), :], pstage).then_inc(e_store, 16)
                    hold(sp, e_store, g * 16 + 16)
                    sp.sem_inc(e_ps, 1)

            @block.gpsimd
            def _(pool):
                pool.sem_inc(e_used, 1)
                nc.gpsimd.memset(BIG[WIN:P, :], 0.0).then_inc(e_clear, 1)
                pool.wait_ge(e_clear, 1)
                with pool.Fori(0, NG) as g:
                    hold(pool, e_used, g + 1)
                    nc.gpsimd.tensor_copy(idx[:, 0:GRP], from1[:, ds(g * GRP, GRP)]).then_inc(e_idx, 1)
                    hold(pool, e_idx, g + 1)
                    for k in range(GRP):
                        nc.gpsimd.indirect_dma_start(
                            out=GY[:, k, :], out_offset=None, in_=Y0,
                            in_offset=bass.IndirectOffsetOnAxis(ap=idx[:, k:k + 1].bitcast(u32), axis=0)).then_inc(e_gy[k], 16)
                    hold(pool, e_y, g + 1)
                    nc.gpsimd.tensor_scalar(beyond, GY, 0.0, 1e4, ALU.is_gt, ALU.mult).then_inc(e_pr, 1)
                    nc.gpsimd.tensor_scalar(below, GY, 0.0, -1e4, ALU.is_lt, ALU.mult).then_inc(e_pr, 1)
                    hold(pool, e_pr, g * 2 + 2)
                    nc.gpsimd.tensor_tensor(beyond, beyond, below, ALU.add).then_inc(e_sign, 1)

            @block.scalar
            def _(act):
                act.sem_inc(e_xt, 1)
                nc.scalar.preload_act_table(ACT.Sqrt)
                with act.Fori(0, NG) as g:
                    hold(act, e_stats, g + 1)
                    nc.scalar.activation(std[:], mv[:, :, 1], ACT.Sqrt, bias=eps[:, 0:1]).then_inc(e_std, 1)
                    hold(act, e_T, g + 1)
                    hold(act, e_pq, g * 2 * GRP + 1)
                    act_evacuate(xt_flat).then_inc(e_xt, 1)
                    for k in range(GRP):
                        for a in range(2):
                            if a == 0:
                                hold(act, e_pq, g * 2 * GRP + (2 * k + 3))
                            nc.scalar.activation(Q[:, ds((g * GRP + k) * 2 + a, 1), :],
                                                 BANKS[3 + (2 * k + 1) % 5][a * WIN:(a + 1) * WIN, :].unsqueeze(1),
                                                 ACT.Copy).then_inc(e_q, 1)

            @block.tensor
            def _(pe):
                pe.sem_inc(e_pq, 1)
                pe.sem_inc(e_p, 0 + 1)
                pe.wait_ge(e_w, 32)
                with pe.Fori(0, NG) as g:
                    pe.wait_ge(e_h, g + 1)
                    pe.wait_ge(e_xt, g + 1)
                    pe_transposes(hstage).then_inc(e_T, 1)
                    pe.wait_ge(e_xt, g + 2)
                    for k in range(GRP):
                        for side in range(2):
                            n = 2 * k + side
                            if n >= 5:
                                m = n - 5
                                if m % 2:
                                    pe.wait_ge(e_q, g * 2 * GRP + (m + 1))
                                else:
                                    pe.wait_ge(e_p, g * GRP + (m // 2 + 2))
                            else:
                                pass
                            for c in range(2):
                                mm = nc.tensor.matmul(BANKS[3 + n % 5][:, :], xt[:, k, c, :], eW1s[:, 2 * side + c, :],
                                                      start=c == 0, stop=c == 1)
                            mm.then_inc(e_pq, 1)
                    pe.wait_ge(e_q, (g + 1) * 2 * GRP)
                    pe.wait_ge(e_p, (g + 1) * GRP + 1)

            @block.vector
            def _(dve):
                dve.wait_ge(e_w, 32)
                with dve.Fori(0, NG) as g:
                    st = Steps(dve, e_st, g * (3 + LN_A + LN_B))
                    for k in range(GRP):
                        hold(dve, e_gy[k], g * 16 + 16)
                    st(nc.vector.tensor_tensor(GY, GY, keep1[:, ds(g * GRP, GRP)].unsqueeze(2).to_broadcast([P, GRP, D]), ALU.mult))
                    st.wait()
                    dve.sem_inc(e_y, 1)
                    st(nc.vector.tensor_scalar(finite, GY, 0.0, 0.0, ALU.mult, ALU.is_equal))
                    st.wait()
                    hold(dve, e_sign, g + 1)
                    nc.vector.copy_predicated(beyond, finite, GY).then_inc(e_pr2, 1)
                    hold(dve, e_pr2, g + 1)
                    st(nc.vector.tensor_tensor(group(X, g), group(X, g), beyond, ALU.add))
                    st.wait()
                    dve.sem_inc(e_used, 1)
                    ln_stats(dve, st, group(X, g))
                    st.wait()
                    dve.sem_inc(e_stats, 1)
                    hold(dve, e_std, g + 1)
                    ln_apply(dve, st, group(X, g), hstage)
                    st.wait()
                    dve.sem_inc(e_h, 1)
                    hold(dve, e_ps, g + 1)
                    for k in range(GRP):
                        hold(dve, e_pq, g * 2 * GRP + (2 * k + 2))
                        nc.vector.tensor_tensor(pstage[:, k, :], BANKS[3 + (2 * k) % 5][:, :], eb1s, ALU.add).then_inc(e_p, 1)

        e_pr2, e_clear = phase_sem("e_selected"), phase_sem("e_cleared")
        with nc.Block() as block:
            project(block)

        end_phase()

        f_rows = SCR[:, 0:UN * DM].rearrange("p (k n) -> p k n", n=DM)
        f_rhs = SCR[:, 4096:4096 + 4 * DM].rearrange("p (k n) -> p k n", n=DM)
        f_msg = SCR[:, 6144:6144 + 4 * DM].rearrange("p (k n) -> p k n", n=DM)
        f_cat = SCR[:, 8192:8192 + 4 * P].rearrange("p (k n) -> p k n", n=P)
        f_dst = SCR[:, 8704:8704 + 4 * P].bitcast(i32).rearrange("p (k n) -> p k n", n=P)
        f_S = SCR[:, 9216:9216 + 4 * WIN].rearrange("p (k n) -> p k n", n=WIN)
        f_in = [phase_sem(f"f_edges{k}") for k in range(UN)]
        f_cats, f_qs, f_U, f_add, f_relu, f_onehot, f_seg, f_acc, f_w = (
            phase_sem("f_" + n) for n in ("cat", "rhs", "inputs", "added", "relu", "onehot", "summed", "acc", "weights"))
        f_sems = [b_idx, *f_in, f_cats, f_qs, f_U, f_add, f_relu, f_onehot, f_seg, f_acc]
        LEAD = 3

        def edge_sum1(block, chunk):
            @block.gpsimd
            def _(pool):
                gather_items(pool, tile_of, f_rows, PROJ, rows_in1, f_add)

            @block.sync
            def _(sp):
                def load(slot, n, t):
                    sp.dma_start(f_cat[WIN:P, slot, :], io["attr_t"][:, ds(t * P, P)]).then_inc(f_in[n], 16)
                    sp.dma_start(f_dst[0:WIN, slot, :], io["dst_row"][ds(t * P, P)].partition_broadcast(WIN)).then_inc(f_in[n], 16)
                with sp.Fori(0, ITERS) as i:
                    ts = load_regs(ENG.SP, tile_of[0:1, ds(i * UN, UN)], 0, ET)
                    for k in range(UN):
                        hold(sp, f_U, i * UN + (k + 1))
                        load(k % 4, k, ts[k])
                ts = load_regs(ENG.SP, tile_of[0:1, CHUNK:CHUNK + LEAD], 0, ET)
                for k in range(LEAD):
                    sp.wait_ge(f_U, CHUNK + k + 1)
                    load(k % 4, k, ts[k])
                for k in range(LEAD):
                    sp.wait_ge(f_in[k], 32 * (ITERS + 1))

            @block.scalar
            def _(act):
                def copy_q(slot, w):
                    nc.scalar.activation(f_rhs[0:WIN, slot:slot + 1, :], Q[:, ds(w, 1), :], ACT.Copy).then_inc(f_qs, 1)
                nc.scalar.preload_act_table(ACT.Relu)
                for k, w in enumerate(load_regs(ENG.Activation, win_of[0:1, 0:LEAD], 0, NWIN - 1)):
                    copy_q(k, w)
                with act.Fori(0, ITERS) as i:
                    ws = load_regs(ENG.Activation, win_of[0:1, ds(i * UN + LEAD, UN)], 0, NWIN - 1)
                    for k in range(UN):
                        hold(act, f_U, i * UN + (k + LEAD + 1))
                        copy_q((k + LEAD) % 4, ws[k])
                        hold(act, f_add, i * UN + (k + 1 + UN))
                        nc.scalar.activation(f_msg[:, k % 4, :], f_msg[:, k % 4, :], ACT.Relu).then_inc(f_relu, 1)

            @block.vector
            def _(dve):
                def cat(slot, w):
                    nc.vector.tensor_scalar(f_cat[0:WIN, slot, :], f_dst[0:WIN, slot, :], node_id[0:WIN, ds(w, 1)], None,
                                            ALU.is_equal).then_inc(f_cats, 1)
                dve.sem_inc(f_add, UN)
                dve.sem_inc(f_acc, 4)
                for k, w in enumerate(load_regs(ENG.DVE, win_of[0:1, 0:LEAD], 0, NWIN - 1)):
                    dve.wait_ge(f_in[k], 32)
                    cat(k, w)
                with dve.Fori(0, ITERS) as i:
                    ts = load_regs(ENG.DVE, tile_of[0:1, ds(i * UN, UN)], 0, ET)
                    ws = load_regs(ENG.DVE, win_of[0:1, ds(i * UN, UN + LEAD)], 0, NWIN - 1)

                    def accumulate(k):
                        hold(dve, f_seg, i * UN + (k + 5))
                        hold(dve, f_acc, i * UN + (k + 4))
                        a = acc1[:, ds(ws[k], 1), :]
                        nc.vector.tensor_tensor(a, a, BANKS[4 + k % 4][WIN:P, :].unsqueeze(1), ALU.add).then_inc(f_acc, 1)
                    for k in range(UN):
                        hold(dve, f_seg, i * UN + (k + 1))
                        nc.vector.tensor_scalar(f_S[:, k % 4, :], iota[:, ds(ws[k] * WIN, WIN)], dst_col[:, ds(ts[k], 1)],
                                                None, ALU.is_equal).then_inc(f_onehot, 1)
                        n = (k + LEAD) % UN
                        if k + LEAD < UN:
                            hold(dve, f_in[n], i * 32 + 32)
                        else:
                            hold(dve, f_in[n], i * 32 + 64)
                        cat((k + LEAD) % 4, ws[k + LEAD])
                        hold(dve, f_U, i * UN + (k + 5))
                        dve.wait_ge(rows_in1[k], chunk * (ITERS * 16) + i * 16 + 16)
                        nc.vector.tensor_tensor(f_msg[:, k % 4, :], f_rows[:, k, :], BANKS[k % 4][:, :], ALU.add).then_inc(f_add, 1)
                        if k >= 2:
                            accumulate(k - 2)
                    accumulate(UN - 2)
                    accumulate(UN - 1)

            @block.tensor
            def _(pe):
                pe.sem_inc(f_U, 4)
                pe.sem_inc(f_seg, 4)
                with pe.Fori(0, ITERS) as i:
                    def inputs(k):
                        if k + LEAD < UN:
                            pass
                        pe.wait_ge(f_in[k], i * 32 + 32)
                        pe.wait_ge(f_cats, i * UN + (k + 1))
                        pe.wait_ge(f_qs, i * UN + (k + 1))
                        pe.wait_ge(f_add, i * UN + (k - 3 + UN))
                        nc.tensor.matmul(BANKS[k % 4][:, :], f_cat[:, k % 4, :], f_rhs[:, k % 4, :], start=True, stop=True).then_inc(f_U, 1)

                    def segment(k):
                        pe.wait_ge(f_onehot, i * UN + (k + 1))
                        pe.wait_ge(f_relu, i * UN + (k + 1))
                        pe.wait_ge(f_acc, i * UN + (k + 1))
                        nc.tensor.matmul(BANKS[4 + k % 4][WIN:P, :], f_S[:, k % 4, :], f_msg[:, k % 4, :], start=True, stop=True).then_inc(f_seg, 1)
                    for k in range(UN):
                        inputs(k)
                        if k >= 2:
                            segment(k - 2)
                    segment(UN - 2)
                    segment(UN - 1)

        with nc.Block() as block:
            start_items(block)

            @block.sync
            def _(sp):
                for k in range(4):
                    sp.dma_start(f_rhs[WIN:P, k, :], io["L1_gnn_eW1"][2 * D:2 * D + ED, :]).then_inc(f_w, 16)
                sp.wait_ge(f_w, 64)
        with nc.Fori(0, n_chunks) as chunk:
            with nc.Block() as block:
                build_table(block)
            with nc.Block() as block:
                edge_sum1(block, chunk)
            with nc.Block() as block:
                clear(block, table_sems + f_sems)

        GN = GRP * P
        HALF = GN // 2
        stage1 = BIG[0:WIN, 0:2 * GRP * DM].rearrange("p (w n) -> p w n", n=DM)
        diag = BIG[0:WIN, 5120:5120 + GN]
        AT = SCR[:, 0:4 * GN].rearrange("p (c n) -> p c n", n=GN)
        HID = AT
        GT = SCR[:, 2560:2560 + 2 * GN].rearrange("p (c n) -> p c n", n=GN)
        HT = SCR[:, 3840:3840 + 2 * GN].rearrange("p (c n) -> p c n", n=GN)
        HS = SCR[:, 5120:6400].rearrange("p (k n) -> p k n", n=D)
        eW2s = SCR[:, 6400:7424].rearrange("p (c n) -> p c n", n=D)
        nW2s = SCR[:, 7424:8448].rearrange("p (c n) -> p c n", n=D)
        eb2s, nb2s, gam, bet = (SCR[:, 8448 + k * D:8448 + (k + 1) * D] for k in range(4))
        nb1s = SCR[:, 9472:9476]
        nW1s = SCR2[:, 0:2048].rearrange("p (c n) -> p c n", n=DM)
        g_w = phase_sem("g_weights")
        (g_stage, g_T, g_hT, g_at, g_agg, g_gt, g_hid, g_relu, g_out, g_h, g_diag, g_stats, g_std, g_z, g_st) = (
            phase_sem("g_" + n) for n in ("stage", "sumsT", "rowsT", "evacuated", "agg", "agg_read", "hidden", "relu", "out", "rows",
                                    "diag", "stats", "std", "out_read", "st"))

        def rows_of(vec):
            return vec.unsqueeze(1).to_broadcast([P, GRP, D])

        def node_update1(block):
            @block.sync
            def _(sp):
                for to, name in ((eW2s, "L1_gnn_eW2"), (nW1s, "L1_gnn_nW1"), (nW2s, "L1_gnn_nW2")):
                    sp.dma_start(to, io[name].rearrange("(c p) n -> p c n", p=P)).then_inc(g_w, 16)
                for to, name in ((eb2s, "L1_gnn_eb2"), (nb2s, "L1_gnn_nb2"), (gam, "L1_gnn_ln_gamma"), (bet, "L1_gnn_ln_beta")):
                    sp.dma_start(to, io[name].partition_broadcast(P)).then_inc(g_w, 16)
                sp.dma_start(nb1s, io["nb1_col"]).then_inc(g_w, 16)

            @block.scalar
            def _(act):
                nc.scalar.preload_act_table(ACT.Sqrt)
                act.wait_ge(g_w, 128)
                with act.Fori(0, NG) as g:
                    hold(act, g_T, g + 1)
                    nc.scalar.activation(stage1, acc1[:, ds(g * 2 * GRP, 2 * GRP), :], ACT.Copy).then_inc(g_stage, 1)
                    hold(act, g_stats, 2 * g + 1)
                    nc.scalar.activation(std[:], mv[:, :, 1], ACT.Sqrt, bias=eps[:, 0:1]).then_inc(g_std, 1)
                    hold(act, g_T, g + 2)
                    hold(act, g_out, 3 * g + 1)
                    for k in range(GRP):
                        nc.scalar.activation(AT[:, :, k * P:(k + 1) * P], BANKS[k][:, :].rearrange("p (c n) -> p c n", n=P),
                                             ACT.Copy).then_inc(g_at, 1)
                    hold(act, g_hT, g + 1)
                    for q, (_, t0, n) in enumerate(O_PAIRS):
                        nc.scalar.activation(HT[:, :, t0 * P:(t0 + n) * P].rearrange("p c (k n) -> p k c n", n=P),
                                             BANKS[5 + q][:, 0:n * 256].rearrange("p (k c n) -> p k c n", k=n, c=2),
                                             ACT.Copy).then_inc(g_at, 1)
                    for n in range(4):
                        hold(act, g_agg, 4 * g + (n + 1))
                        nc.scalar.activation(GT[:, n // 2, (n % 2) * HALF:(n % 2 + 1) * HALF], BANKS[n][:, 0:HALF], ACT.Copy).then_inc(g_gt, 1)
                    for n in range(8):
                        hold(act, g_hid, 8 * g + (n + 1))
                        nc.scalar.activation(HID[:, n // 2, (n % 2) * HALF:(n % 2 + 1) * HALF], BANKS[4 + n % 4][:, 0:HALF], ACT.Relu,
                                             bias=nb1s[:, n // 2:n // 2 + 1]).then_inc(g_relu, 1)
                    hold(act, g_stats, 2 * g + 2)
                    nc.scalar.activation(std[:], mv[:, :, 1], ACT.Sqrt, bias=eps[:, 0:1]).then_inc(g_std, 1)

            @block.tensor
            def _(pe):
                pe.sem_inc(g_T, 1)
                pe.sem_inc(g_out, 1)
                pe.wait_ge(g_w, 128)
                with pe.Fori(0, NG) as g:
                    hold(pe, g_stage, g + 1)
                    hold(pe, g_z, 3 * g + 1)
                    for k in range(GRP):
                        for c in range(4):
                            for a in range(2):
                                m = nc.tensor.transpose(BANKS[k][:, c * P + a * WIN:c * P + (a + 1) * WIN],
                                                        stage1[:, 2 * k + a, c * P:(c + 1) * P], ident[0:WIN, 0:WIN])
                    m.then_inc(g_T, 1)
                    pe.wait_ge(g_h, g + 1)
                    for k in range(GRP):
                        for c in range(2):
                            m = nc.tensor.transpose(BANKS[5 + k // 2][:, (k % 2) * 256 + c * P:(k % 2) * 256 + (c + 1) * P],
                                                    HS[:, k, c * P:(c + 1) * P], ident[:])
                    m.then_inc(g_hT, 1)
                    pe.wait_ge(g_at, 8 * g + 8)
                    pe.wait_ge(g_diag, g + 1)
                    for n in range(4):
                        to = BANKS[n][:, 0:HALF]
                        cols = slice((n % 2) * HALF, (n % 2 + 1) * HALF)
                        for c in range(4):
                            nc.tensor.matmul(to, eW2s[:, c, (n // 2) * P:(n // 2 + 1) * P], AT[:, c, cols], start=c == 0, stop=False)
                        nc.tensor.matmul(to, eb2s[0:WIN, (n // 2) * P:(n // 2 + 1) * P], diag[:, cols], start=False, stop=True).then_inc(g_agg, 1)
                    pe.wait_ge(g_gt, 4 * g + 4)
                    for n in range(8):
                        pe.wait_ge(g_relu, 8 * g + (n + 1))
                        to = BANKS[4 + n % 4][:, 0:HALF]
                        cols = slice((n % 2) * HALF, (n % 2 + 1) * HALF)
                        f = slice((n // 2) * P, (n // 2 + 1) * P)
                        for c in range(4):
                            m = nc.tensor.matmul(to, nW1s[:, c, f], (HT if c < 2 else GT)[:, c % 2, cols], start=c == 0, stop=c == 3)
                        m.then_inc(g_hid, 1)
                    pe.wait_ge(g_relu, 8 * g + 8 + 4)
                    for q, (_, t0, n) in enumerate(O_PAIRS):
                        for k in range(t0, t0 + n):
                            for f in range(4):
                                m = nc.tensor.matmul(BANKS[q][:, (k - t0) * D:(k - t0 + 1) * D], HID[:, f, k * P:(k + 1) * P], nW2s[:, f, :],
                                                     start=f == 0, stop=f == 3)
                        m.then_inc(g_out, 1)

            @block.vector
            def _(dve):
                dve.sem_inc(g_z, 1)
                dve.sem_inc(g_relu, 4)
                dve.wait_ge(g_w, 128)
                with dve.Fori(0, NG) as g:
                    st = Steps(dve, g_st, g * (2 * (LN_A + LN_B) + 8))
                    nc.vector.tensor_tensor(diag.rearrange("p (w n) -> p w n", n=WIN),
                                            ident[0:WIN, 0:WIN].unsqueeze(1).to_broadcast([WIN, 2 * GRP, WIN]),
                                            CNT[:, ds(g * 2 * GRP, 2 * GRP)].unsqueeze(2).to_broadcast([WIN, 2 * GRP, WIN]),
                                            ALU.mult).then_inc(g_diag, 1)
                    ln_stats(dve, st, group(X, g))
                    st.wait()
                    dve.sem_inc(g_stats, 1)
                    hold(dve, g_std, 2 * g + 1)
                    ln_apply(dve, st, group(X, g), HS)
                    st.wait()
                    dve.sem_inc(g_h, 1)
                    hold(dve, g_hT, g + 1)
                    st(nc.vector.tensor_tensor(HS, HS, rows_of(nb2s), ALU.add))
                    st.wait()
                    for q, (_, t0, n) in enumerate(O_PAIRS):
                        hold(dve, g_out, 3 * g + (q + 2))
                        st(nc.vector.tensor_tensor(HS[:, t0:t0 + n, :], HS[:, t0:t0 + n, :],
                                                   BANKS[q][:, 0:n * D].rearrange("p (k n) -> p k n", n=D), ALU.add))
                    st.wait()
                    dve.sem_inc(g_z, 3)
                    ln_stats(dve, st, HS)
                    st.wait()
                    dve.sem_inc(g_stats, 1)
                    hold(dve, g_std, 2 * g + 2)
                    ln_apply(dve, st, HS, HS)
                    st.wait()
                    st(nc.vector.tensor_tensor(HS, HS, rows_of(gam), ALU.mult))
                    st.wait()
                    st(nc.vector.tensor_tensor(HS, HS, rows_of(bet), ALU.add))
                    st.wait()
                    st(nc.vector.tensor_tensor(group(X, g), group(X, g), HS, ALU.add))
                    st.wait()
                    st(nc.vector.memset(std[:, 0:1], 0.0))
                    st.wait()

        with nc.Block() as block:
            node_update1(block)

        end_phase()

        XN = BIG[:, 0:NT * D].rearrange("p (t n) -> p t n", n=D)
        W1s = BIG[:, 6400:6400 + E * 2 * H1].rearrange("p (e c h) -> p e c h", e=E, c=2)
        W2s = BIG[:, 14592:14592 + E * 4 * D].rearrange("p (e f n) -> p e f n", e=E, f=4)
        b2r = BIG[:, 22784:22784 + E * D].rearrange("p (e n) -> p e n", e=E)
        b1r = SCR[:, 6144:6144 + E * H1].rearrange("p (e h) -> p e h", e=E)
        hs3 = SCR[:, 0:1280].rearrange("p (k n) -> p k n", n=D)
        gam1, bet1 = SCR[:, 5120:5376], SCR[:, 5376:5632]
        Wrs = SCR[:, 5632:5648].rearrange("p (c e) -> p c e", c=2)
        brs = SCR[:, 5648:5656]
        tile_expert = sb("tile_expert", [1, T1], i32)
        h_w, h_big, h_T, h_xt, h_stats, h_std, h_n, h_L, h_lg, h_copied, h_st = (
            phase_sem("h_" + n) for n in ("weights", "expert_weights", "transposed", "xt", "stats", "std", "rows", "logits", "logits_read", "copied", "st"))

        def router1(block):
            @block.sync
            def _(sp):
                sp.dma_start(gam1, io["L1_ffn_gamma"].partition_broadcast(P)).then_inc(h_w, 16)
                sp.dma_start(bet1, io["L1_ffn_beta"].partition_broadcast(P)).then_inc(h_w, 16)
                sp.dma_start(Wrs, io["L1_ffn_Wr"].rearrange("(c p) e -> p c e", p=P)).then_inc(h_w, 16)
                sp.dma_start(brs, io["L1_ffn_br"].partition_broadcast(P)).then_inc(h_w, 16)
                for e in range(E):
                    sp.dma_start(W1s[:, e, :, :], io["L1_ffn_W1"][e, :, :].rearrange("(c p) h -> p c h", p=P)).then_inc(h_big, 16)
                    sp.dma_start(W2s[:, e, :, :], io["L1_ffn_W2"][e, :, :].rearrange("(f p) n -> p f n", p=P)).then_inc(h_big, 16)
                sp.dma_start(b1r, io["L1_ffn_b1"].rearrange("e h -> (e h)").partition_broadcast(P).rearrange("p (e h) -> p e h", e=E)).then_inc(h_big, 16)
                sp.dma_start(b2r, io["L1_ffn_b2"].rearrange("e h -> (e h)").partition_broadcast(P).rearrange("p (e h) -> p e h", e=E)).then_inc(h_big, 16)

            @block.scalar
            def _(act):
                act.sem_inc(h_xt, 1)
                nc.scalar.preload_act_table(ACT.Sqrt)
                with act.Fori(0, NG) as g:
                    for a in range(2):
                        hold(act, h_stats, 2 * g + (a + 1))
                        nc.scalar.activation(std[:], mv[:, :, 1], ACT.Sqrt, bias=eps[:, 0:1]).then_inc(h_std, 1)
                    hold(act, h_T, g + 1)
                    hold(act, h_L, g + 1)
                    act_evacuate(xt_flat).then_inc(h_xt, 1)

            @block.tensor
            def _(pe):
                pe.sem_inc(h_L, 1)
                pe.wait_ge(h_w, 64)
                with pe.Fori(0, NG) as g:
                    pe.wait_ge(h_n, g + 1)
                    pe.wait_ge(h_xt, g + 1)
                    pe_transposes(hstage).then_inc(h_T, 1)
                    pe.wait_ge(h_xt, g + 2)
                    pe.wait_ge(h_lg, g + 1)
                    for k in range(GRP):
                        for c in range(2):
                            m = nc.tensor.matmul(BANKS[6][:, k * E:(k + 1) * E], xt[:, k, c, :], Wrs[:, c, :], start=c == 0, stop=c == 1)
                    m.then_inc(h_L, 1)

            @block.vector
            def _(dve):
                dve.sem_inc(h_lg, 1)
                dve.wait_ge(h_w, 64)
                with dve.Fori(0, NG) as g:
                    st = Steps(dve, h_st, g * (2 * (LN_A + LN_B) + 2))
                    ln_stats(dve, st, group(X, g))
                    st.wait()
                    dve.sem_inc(h_stats, 1)
                    hold(dve, h_std, 2 * g + 1)
                    ln_apply(dve, st, group(X, g), hs3)
                    st.wait()
                    ln_stats(dve, st, hs3)
                    st.wait()
                    dve.sem_inc(h_stats, 1)
                    hold(dve, h_std, 2 * g + 2)
                    ln_apply(dve, st, hs3, hs3)
                    st.wait()
                    st(nc.vector.tensor_tensor(hs3, hs3, rows_of(gam1), ALU.mult))
                    st.wait()
                    hold(dve, h_copied, g + 1)
                    st(nc.vector.tensor_tensor(hstage, hs3, rows_of(bet1), ALU.add))
                    st.wait()
                    dve.sem_inc(h_n, 1)
                    hold(dve, h_L, g + 2)
                    nc.vector.tensor_tensor(group(LG, g), BANKS[6][:, 0:GRP * E].rearrange("p (k e) -> p k e", e=E),
                                            brs.unsqueeze(1).to_broadcast([P, GRP, E]), ALU.add).then_inc(h_lg, 1)

            @block.gpsimd
            def _(pool):
                pool.sem_inc(h_copied, 1)
                with pool.Fori(0, NG) as g:
                    hold(pool, h_n, g + 1)
                    nc.gpsimd.tensor_copy(group(XN, g), hstage).then_inc(h_copied, 1)

        with nc.Block() as block:
            router1(block)

        q_st, q_ready, q_sum, q_exp = (phase_sem("q_" + n) for n in ("st", "ready", "summed", "exp"))
        q_done = sem("q_scattered")
        used_tiles = SCR[:, 0:E]
        tiles_i = SCR[:, 8:8 + E].bitcast(i32)
        tiles_f, tiles_end, first_slot = (SCR[:, 16 + 8 * k:24 + 8 * k] for k in range(3))
        past = SCR[0:1, 64:64 + T1 * E].rearrange("p (t e) -> p t e", e=E)
        te_f = SCR[0:1, 640:640 + T1]
        valid = r_c

        def route1(block):
            @block.vector
            def _(dve):
                st = Steps(dve, q_st)
                first_best(st, LG, r_a, OH1, r_b)
                st(nc.vector.scalar_tensor_tensor(LG[:], OH1[:], -3e38, LG[:], ALU.mult, ALU.add))
                st.wait()
                first_best(st, LG, r_c, OH2, r_b)
                st(nc.vector.tensor_tensor(keep2[:], r_c[:], r_a[:], ALU.subtract))
                st.wait()
                dve.sem_inc(q_exp, 1)
                st(nc.vector.tensor_scalar(valid[:], NIDT[:], float(NODES), None, ALU.is_lt))
                st.wait()
                st(nc.vector.tensor_tensor(OH1[:], OH1[:], bce(valid), ALU.mult))
                st(nc.vector.tensor_tensor(OH2[:], OH2[:], bce(valid), ALU.mult))
                st.wait()
                st(nc.vector.tensor_tensor(LG[:], OH1[:], OH2[:], ALU.add))
                ranks(dve, st, LG, q_ready, q_sum, 1)
                members = CUM[:, NT - 1, :]
                st(nc.vector.tensor_scalar(tiles_i, members, float(P - 1), None, ALU.add))
                st.wait()
                st(nc.vector.tensor_scalar(tiles_i, tiles_i, P.bit_length() - 1, None, ALU.arith_shift_right))
                st.wait()
                st(nc.vector.tensor_copy(tiles_f, tiles_i))
                st.wait()
                st(nc.vector.tensor_tensor_scan(tiles_end, ones[:, 0:E], tiles_f, 0.0, ALU.mult, ALU.add))
                st.wait()
                st(nc.vector.tensor_tensor(first_slot, tiles_end, tiles_f, ALU.subtract))
                st(nc.vector.tensor_tensor(past, iota[0:1, 0:T1].unsqueeze(2).to_broadcast([1, T1, E]),
                                           tiles_end[0:1, :].unsqueeze(1).to_broadcast([1, T1, E]), ALU.is_ge))
                st.wait()
                st(nc.vector.tensor_scalar(first_slot, first_slot, float(P), -1.0, ALU.mult, ALU.add))
                st(nc.vector.tensor_reduce(te_f, past, AX.X, ALU.add))
                st.wait()
                st(nc.vector.tensor_scalar(tile_expert[:], te_f, float(E - 1), None, ALU.min))
                st(nc.vector.tensor_tensor(RT[:], RT[:], bct(first_slot), ALU.add))
                st.wait()
                for a, (oh, to, frm) in enumerate(((OH1, to1, from1), (OH2, to2, from2))):
                    st(nc.vector.tensor_tensor(CUM[:], RT[:], oh[:], ALU.mult))
                    st.wait()
                    st(nc.vector.tensor_reduce(r_a[:], CUM[:], AX.X, ALU.add))
                    st.wait()
                    st(nc.vector.tensor_copy(frm[:], r_a[:]))
                    st(nc.vector.tensor_scalar(r_b[:], NIDT[:], float(TRASH1 + a * NPAD), None, ALU.add))
                    st.wait()
                    st(nc.vector.tensor_tensor(r_a[:], r_a[:], r_b[:], ALU.subtract))
                    st.wait()
                    st(nc.vector.tensor_tensor(r_a[:], r_a[:], valid[:], ALU.mult))
                    st.wait()
                    st(nc.vector.tensor_tensor(r_a[:], r_a[:], r_b[:], ALU.add))
                    st.wait()
                    st(nc.vector.tensor_copy(to[:], r_a[:]))
                    st.wait()
                dve.sem_inc(q_ready, 1)
                dve.wait_ge(q_exp, 2)
                st(nc.vector.tensor_scalar(keep1[:], keep2[:], 1.0, None, ALU.add))
                st.wait()
                st(nc.vector.reciprocal(keep1[:], keep1[:]))
                st.wait()
                st(nc.vector.tensor_tensor(keep2[:], keep2[:], keep1[:], ALU.mult))

            @block.scalar
            def _(act):
                act.wait_ge(q_exp, 1)
                nc.scalar.activation(keep2[:], keep2[:], ACT.Exp).then_inc(q_exp, 1)

            @block.tensor
            def _(pe):
                pe_ranks(pe, LG, q_ready, q_sum, 1)

            @block.gpsimd
            def _(pool):
                pool.wait_ge(q_ready, 2)
                for to in (to1, to2):
                    for t in range(NT):
                        nc.gpsimd.indirect_dma_start(
                            out=BUF1, out_offset=bass.IndirectOffsetOnAxis(ap=to[:, t:t + 1].bitcast(u32), axis=0),
                            in_=XN[:, t, :], in_offset=None).then_inc(q_done, 16)
                pool.wait_ge(q_done, 32 * NT)
                pool.wait_ge(h_big, 16 * (2 * E + 2))

        with nc.Block() as block:
            route1(block)

        end_phase()

        i_rows = [BIG[:, k * D:(k + 1) * D] for k in range(4)]
        i_xT = [BIG[:, 1024 + k * D:1024 + (k + 1) * D].rearrange("p (c n) -> p c n", c=2) for k in range(4)]
        i_h = [BIG[:, 2048 + k * H1:2048 + (k + 1) * H1] for k in range(4)]
        i_hT = [BIG[:, 4096 + k * H1:4096 + (k + 1) * H1].rearrange("p (f n) -> p f n", n=P) for k in range(2)]
        i_y = [BIG[:, 5120 + k * D:5120 + (k + 1) * D] for k in range(4)]
        i_in, i_out = [phase_sem(f"i_in{k}") for k in range(8)], sems("i_out", 4)
        i_T, i_x, i_m1, i_b1, i_gelu, i_Th, i_hTs, i_m2, i_ys, i_stored = (
            phase_sem("i_" + n) for n in ("rowsT", "xT", "hidden", "biased", "gelu", "hiddenT", "hT", "out", "y", "stored"))
        UT = 8

        def experts1(block):
            @block.sync
            def _(sp):
                with sp.Fori(0, T1 // UT) as i:
                    for k in range(UT):
                        n = i * UT + k
                        hold(sp, i_T, n + 1)
                        sp.dma_start(i_rows[k % 4], BUF1[ds(n * P, P), :]).then_inc(i_in[k], 16)

            @block.tensor
            def _(pe):
                pe.sem_inc(i_T, 4)
                pe.sem_inc(i_m2, 2)
                with pe.Fori(0, T1 // UT) as i:
                    es = load_regs(ENG.PE, tile_expert[0:1, ds(i * UT, UT)], 0, E - 1)

                    def first(k):
                        n = i * UT + k
                        pe.wait_ge(i_in[k], i * 16 + 16)
                        pe.wait_ge(i_x, n + 1)
                        for c in range(2):
                            m = nc.tensor.transpose(BANKS[0][:, c * P:(c + 1) * P], i_rows[k % 4][:, c * P:(c + 1) * P], ident[:])
                        m.then_inc(i_T, 1)
                        pe.wait_ge(i_x, n + 2)
                        pe.wait_ge(i_b1, n + 1)
                        for c in range(2):
                            m = nc.tensor.matmul(BANKS[1 + k % 2][:, 0:H1], i_xT[k % 4][:, c, :],
                                                 W1s[:, ds(es[k], 1), c, :].rearrange("p e h -> p (e h)"), start=c == 0, stop=c == 1)
                        m.then_inc(i_m1, 1)

                    def turn(k):
                        n = i * UT + k
                        pe.wait_ge(i_gelu, n + 1)
                        pe.wait_ge(i_hTs, n + 1)
                        for f in range(4):
                            m = nc.tensor.transpose(BANKS[3 + k % 2][:, f * P:(f + 1) * P], i_h[k % 4][:, f * P:(f + 1) * P], ident[:])
                        m.then_inc(i_Th, 1)

                    def second(k):
                        n = i * UT + k
                        pe.wait_ge(i_hTs, n + 3)
                        pe.wait_ge(i_ys, n + 1)
                        for f in range(4):
                            m = nc.tensor.matmul(BANKS[5 + k % 2][:, 0:D], i_hT[k % 2][:, f, :],
                                                 W2s[:, ds(es[k], 1), f, :].rearrange("p e n -> p (e n)"), start=f == 0, stop=f == 3)
                        m.then_inc(i_m2, 1)
                    first(0)
                    for k in range(UT):
                        if k + 1 < UT:
                            first(k + 1)
                        turn(k)
                        if k:
                            second(k - 1)
                    second(UT - 1)

            @block.scalar
            def _(act):
                act.sem_inc(i_x, 1)
                nc.scalar.preload_act_table(ACT.Gelu)
                with act.Fori(0, T1 // UT) as i:
                    def rows(k):
                        hold(act, i_T, i * UT + (k + 5))
                        nc.scalar.activation(i_xT[k % 4].rearrange("p c n -> p (c n)"), BANKS[0][:, 0:D], ACT.Copy).then_inc(i_x, 1)
                    rows(0)
                    for k in range(UT):
                        if k + 1 < UT:
                            rows(k + 1)
                        hold(act, i_b1, i * UT + (k + 3))
                        nc.scalar.activation(i_h[k % 4], i_h[k % 4], ACT.Gelu).then_inc(i_gelu, 1)

            @block.vector
            def _(dve):
                dve.sem_inc(i_b1, 2)
                dve.sem_inc(i_hTs, 2)
                dve.sem_inc(i_ys, 2)
                with dve.Fori(0, T1 // UT) as i:
                    es = load_regs(ENG.DVE, tile_expert[0:1, ds(i * UT, UT)], 0, E - 1)

                    def bias(k):
                        n = i * UT + k
                        hold(dve, i_m1, n + 1)
                        if k % 4 == 0:
                            pass
                        nc.vector.tensor_tensor(i_h[k % 4].unsqueeze(1), BANKS[1 + k % 2][:, 0:H1].unsqueeze(1), b1r[:, ds(es[k], 1), :],
                                                ALU.add).then_inc(i_b1, 1)

                    def turn(k):
                        n = i * UT + k
                        hold(dve, i_Th, n + 1)
                        hold(dve, i_m2, n + 1)
                        nc.vector.tensor_copy(i_hT[k % 2].rearrange("p f n -> p (f n)"), BANKS[3 + k % 2][:, :]).then_inc(i_hTs, 1)

                    def finish(k):
                        n = i * UT + k
                        hold(dve, i_m2, n + 3)
                        hold(dve, i_stored, n + 1)
                        nc.vector.tensor_tensor(i_y[k % 4].unsqueeze(1), BANKS[5 + k % 2][:, 0:D].unsqueeze(1), b2r[:, ds(es[k], 1), :],
                                                ALU.add).then_inc(i_ys, 1)
                    bias(0)
                    for k in range(UT):
                        if k + 1 < UT:
                            bias(k + 1)
                        turn(k)
                        if k:
                            finish(k - 1)
                    finish(UT - 1)

            @block.gpsimd
            def _(pool):
                pool.sem_inc(i_stored, 4)
                with pool.Fori(0, T1 // UT) as i:
                    for k in range(UT):
                        n = i * UT + k
                        hold(pool, i_ys, n + 3)
                        nc.gpsimd.dma_start(Y1[ds(n * P, P), :], i_y[k % 4]).then_inc(i_out[k % 4], 16)
                        hold(pool, i_out[k % 4], i * 32 + (16 if k < 4 else 32))
                        pool.sem_inc(i_stored, 1)

        with nc.Block() as block:
            experts1(block)

        j_rows = [[SCR[:, (2 * s + a) * 1280:(2 * s + a + 1) * 1280].rearrange("p (k n) -> p k n", n=D) for a in range(2)] for s in range(1)]
        j_idx = sb("j_idx", [P, 2, GRP], i32)
        j_in = sems("j_in", 2 * GRP)
        j_cp, j_used, j_x, j_st, j_out = (phase_sem("j_" + n) for n in ("index", "used", "x", "st", "out"))

        def combine(block):
            @block.gpsimd
            def _(pool):
                pool.sem_inc(j_used, 1)
                with pool.Fori(0, NG) as g:
                    hold(pool, j_used, g + 1)
                    nc.gpsimd.tensor_copy(j_idx[:, 0, :], from1[:, ds(g * GRP, GRP)]).then_inc(j_cp, 1)
                    nc.gpsimd.tensor_copy(j_idx[:, 1, :], from2[:, ds(g * GRP, GRP)]).then_inc(j_cp, 1)
                    hold(pool, j_cp, 2 * g + 2)
                    for a in range(2):
                        for k in range(GRP):
                            nc.gpsimd.indirect_dma_start(
                                out=j_rows[0][a][:, k, :], out_offset=None, in_=Y1,
                                in_offset=bass.IndirectOffsetOnAxis(ap=j_idx[:, a, k:k + 1].bitcast(u32), axis=0)).then_inc(j_in[a * GRP + k], 16)

            @block.vector
            def _(dve):
                with dve.Fori(0, NG) as g:
                    st = Steps(dve, j_st, g * 4)
                    for a, keep in enumerate((keep1, keep2)):
                        for k in range(GRP):
                            hold(dve, j_in[a * GRP + k], g * 16 + 16)
                        st(nc.vector.tensor_tensor(j_rows[0][a], j_rows[0][a], keep[:, ds(g * GRP, GRP)].unsqueeze(2).to_broadcast([P, GRP, D]), ALU.mult))
                        st.wait()
                        st(nc.vector.tensor_tensor(group(X, g), group(X, g), j_rows[0][a], ALU.add))
                        st.wait()
                    dve.sem_inc(j_used, 1)
                    dve.sem_inc(j_x, 1)

            @block.sync
            def _(sp):
                with sp.Fori(0, NG - 1) as g:
                    hold(sp, j_x, g + 1)
                    sp.dma_start(out[ds(g * GN, GN), :].rearrange("(k p) n -> p k n", p=P), group(X, g)).then_inc(j_out, 16)
                sp.wait_ge(j_x, NG)
                sp.dma_start(out[(NG - 1) * GN:(NT - 1) * P, :].rearrange("(k p) n -> p k n", p=P), X[:, (NG - 1) * GRP:NT - 1, :]).then_inc(j_out, 16)
                sp.dma_start(out[(NT - 1) * P:NODES, :], X[0:TAIL, NT - 1, :]).then_inc(j_out, 16)
                sp.wait_ge(j_out, 16 * (NG + 1))

        with nc.Block() as block:
            combine(block)


WEIGHTS = ["L0_gnn_weight", "L0_ffn_gate_w", "L0_ffn_gate_b", "L0_ffn_w1", "L0_ffn_b1", "L0_ffn_w2", "L0_ffn_b2",
           "L1_gnn_eW1", "L1_gnn_eb1", "L1_gnn_eW2", "L1_gnn_eb2", "L1_gnn_nW1", "L1_gnn_nb1", "L1_gnn_nW2",
           "L1_gnn_nb2", "L1_gnn_ln_gamma", "L1_gnn_ln_beta", "L1_ffn_gamma", "L1_ffn_beta", "L1_ffn_Wr", "L1_ffn_br",
           "L1_ffn_W1", "L1_ffn_b1", "L1_ffn_W2", "L1_ffn_b2"]


def kernel(**inputs):
    import numpy as np
    import concourse.bacc as bacc
    from concourse.bass_utils import run_bass_kernel_spmd

    pad = EROW - EDGES
    src = np.concatenate([np.asarray(inputs["src"]), np.zeros(pad, np.int32)])
    dst = np.concatenate([np.asarray(inputs["dst"]), np.full(pad, NODES, np.int32)])
    w = np.concatenate([np.asarray(inputs["edge_weight"]), np.zeros(pad, np.float32)])
    attr = np.concatenate([np.asarray(inputs["edge_attr_64"]), np.zeros((pad, ED), np.float32)])
    arrays = {
        "x": np.asarray(inputs["x"]),
        "src_col": src.reshape(ET + 1, P).T,
        "dst_col": dst.reshape(ET + 1, P).T,
        "w_col": w.reshape(ET + 1, P).T,
        "dst_tiles": dst[:ET * P].reshape(ETP, ETQ * P),
        "dst_row": dst,
        "attr_t": attr.T,
        "nb1_col": np.asarray(inputs["L1_gnn_nb1"]).reshape(DM // P, P).T,
        "b1_col": np.asarray(inputs["L0_ffn_b1"]).reshape(E * F0 // P, P).T,
    }
    for name in WEIGHTS:
        arrays[name] = np.asarray(inputs[name])
    arrays = {n: np.ascontiguousarray(a) for n, a in arrays.items()}
    nc = bacc.Bacc("TRN2", target_bir_lowering=False, num_devices=1)
    io = {n: nc.dram_tensor(f"in_{n}", a.shape, mybir.dt.from_np(a.dtype), kind="ExternalInput").ap()
          for n, a in arrays.items()}
    out = nc.dram_tensor("out_x", (NODES, D), f32, kind="ExternalOutput").ap()
    build(nc, io, out)
    r = run_bass_kernel_spmd(nc, [{f"in_{n}": a for n, a in arrays.items()}], core_ids=[0])
    return r.results[0]["out_x"]
```

```python
from contextlib import ExitStack

import concourse.bass as bass
from concourse import mybir

f32, i32, u32 = mybir.dt.float32, mybir.dt.int32, mybir.dt.uint32
ALU, ACT, AX = mybir.AluOpType, mybir.ActivationFunctionType, mybir.AxisListType
ENG = mybir.EngineType
ds = bass.ds

P = 128
NODES, D = 3125, 256
NT = -(-NODES // P)
NPAD = NT * P
TAIL = NODES - (NT - 1) * P
GRP = 5
NG = NT // GRP
WIN0, NWIN0 = P, NT
WIN = 64
NWIN = -(-NODES // WIN)
NWPAD = 2 * NT
EDGES = 53125
ET = -(-EDGES // P)
ETP, ETQ = 104, 4
EROW = (ET + 1) * P
CHUNK0 = ET + NWIN0 - 1
UN0 = 20
CHUNK1 = ET + NWIN - 1
UN1 = 16
LEAD, LAG = 3, 2
TABLE = CHUNK1 + UN1
MAXCHUNKS = -(-ET * NWIN // CHUNK1)
DM = 512
ED = 64
E = 8
CAP = -(-5 * NODES // (4 * E))
ESLOT = 512
F0 = 1024
TRASH0 = E * ESLOT
H1 = 512
T1 = (2 * NODES - E) // P + E
TRASH1 = T1 * P
BIGW = NWPAD * DM
EPS = 1e-5
assert ETP * ETQ == ET and CHUNK0 % UN0 == 0 and CHUNK1 % UN1 == 0 and TABLE >= CHUNK0 + UN0 and NT % GRP == 0 and ESLOT >= CAP


class Steps:

    def __init__(self, eng, sem, start=0):
        self.eng, self.sem, self.start, self.n = eng, sem, start, 0

    def __call__(self, instruction):
        instruction.then_inc(self.sem, 1)
        self.n += 1
        return instruction

    def wait(self):
        hold(self.eng, self.sem, self.start + self.n)


def hold(eng, sem, value):
    eng.wait_ge(sem, value)
    eng.nop(nofuse=True)


def build(nc, io, out):
    ctx = ExitStack()
    with ctx:
        sb = lambda name, shape, dt=f32: ctx.enter_context(nc.sbuf_tensor(name, shape, dt))
        sem = lambda name: ctx.enter_context(nc.semaphore(name))
        sems = lambda name, n: [sem(f"{name}{k}") for k in range(n)]
        of_phase = []

        def phase_sem(name):
            of_phase.append(nc.alloc_semaphore(name=name))
            return of_phase[-1]
        dram = lambda name, shape, dt=f32: nc.dram_tensor(name, shape, dt).ap()

        def load_regs(eng, ap, lo, hi):
            return nc.values_load_multi_w_load_instructions(
                ap, engines=[eng], min_val=lo, max_val=hi,
                skip_runtime_bounds_check_because="the table is built in range")[1]

        H0 = dram("h0_rows", (NPAD, D))
        BUF0 = dram("expert_in0", (TRASH0 + NPAD, D))
        Y0 = dram("expert_out0", (TRASH0, D))
        PROJ = dram("src_proj", (NPAD, DM))
        BUF1 = dram("expert_in1", (TRASH1 + 2 * NPAD, D))
        Y1 = dram("expert_out1", (TRASH1, D))

        ident = sb("ident", [P, P])
        before = sb("before", [P, P])
        upto = sb("upto", [P, P])
        ones = sb("ones", [P, P])
        zeros = sb("zeros", [P, 1024])
        iota = sb("iota", [P, TABLE])
        part = sb("part", [P, 1])
        X = sb("X", [P, NT, D])
        lo_dst, hi_dst = (sb(n, [ETP, ETQ], i32) for n in ("lo_dst", "hi_dst"))
        lo_win, hi_win = (sb(n, [ETP, ETQ], i32) for n in ("lo_win", "hi_win"))
        lo_f, n_f, incl, one4 = (sb(n, [ETP, ETQ]) for n in ("lo_f", "n_f", "incl", "one4"))
        ends, starts, first, nfirst = (sb(n, [ETP, ETQ]) for n in ("ends", "starts", "first", "nfirst"))
        chunk_hit = sb("chunk_hit", [1, MAXCHUNKS])
        chunks_f, chunks_i = sb("chunks_f", [1, 1]), sb("chunks_i", [1, 1], i32)
        tile_of = sb("tile_of", [1, TABLE], i32)
        win_of = sb("win_of", [1, LAG + TABLE], i32)
        src_items = sb("src_items", [P, TABLE], i32)
        dst_items = sb("dst_items", [P, TABLE])
        aux_items = sb("aux_items", [P, TABLE])
        CNT = sb("CNT", [P, NT])
        idx = sb("idx", [P, UN0], i32)
        BIG = sb("BIG", [P, BIGW])
        SCR = sb("SCR", [P, 10240])
        stats = sb("stats", [P, GRP, 6])
        mv = sb("mv", [P, GRP, 2])
        std = sb("std", [P, GRP])
        rstd = sb("rstd", [P, GRP])
        eps = sb("eps", [P, 1])
        scaled_ones = sb("scaled_ones", [1, 3, P])
        ones_of = lambda v: scaled_ones[0:1, (-WIN0, WIN, -WIN).index(v), :]
        SCR2 = sb("SCR2", [P, 2560])
        NIDT = sb("NIDT", [P, NT])
        expert8 = sb("expert8", [P, E])
        LG, OH1, OH2, RT, CUM = (SCR2[:, k * NT * E:(k + 1) * NT * E].rearrange("p (t e) -> p t e", e=E) for k in range(5))
        r_a, r_b, r_c, keep1, keep2 = (sb(n, [P, NT]) for n in ("r_a", "r_b", "r_c", "keep1", "keep2"))
        to1, to2, from1, from2 = (sb(n, [P, NT], i32) for n in ("to1", "to2", "from1", "from2"))
        weights_in = sem("weights_in")

        BANKS = [ctx.enter_context(nc.psum_tensor(f"bank{k}", [P, 512], f32)) for k in range(8)]

        acc0 = BIG[:, 0:NT * 257].rearrange("p (w n) -> p w n", n=257)
        HN = BIG[:, NT * 257:NT * 257 + NT * D].rearrange("p (t d) -> p t d", d=D)
        zero_fill = sem("zero_fill")

        def ln_stats(dve, st, tiles):
            for k in range(GRP):
                st(nc.vector.bn_stats(stats[:, k, :], tiles[:, k, :]))
            st.wait()
            for k in range(GRP):
                st(nc.vector.bn_aggr(mv[:, k, :], stats[:, k, :]))

        def ln_apply(dve, st, tiles, to):
            st(nc.vector.reciprocal(rstd[:], std[:]))
            st.wait()
            for k in range(GRP):
                st(nc.vector.tensor_scalar(to[:, k, :], tiles[:, k, :], mv[:, k, 0:1], rstd[:, k:k + 1],
                                           ALU.subtract, ALU.mult))

        LN_A, LN_B = 2 * GRP, 1 + GRP

        def end_phase():
            with nc.Block() as block:
                clear(block, of_phase)
            for s in of_phase:
                nc.release_semaphore(s)
            of_phase.clear()

        def clear(block, which):
            @block.gpsimd
            def _(pool):
                for s in which:
                    pool.sem_clear(s)

        x_in, e_in, a_ready, a_stats, a_std, a_hn, a_st, a_const = (
            phase_sem(n) for n in ("x_in", "e_in", "a_tail", "a_stats", "a_std", "a_hn", "a_st", "a_const"))
        h0_out = phase_sem("h0_out")
        dt_i = SCR[0:ETP, 0:ETQ * P].bitcast(i32).rearrange("p (q e) -> p q e", q=ETQ)
        with nc.Block() as block:
            @block.sync
            def _(sp):
                sp.wait_ge(a_ready, 1)
                for g in range(NG - 1):
                    sp.dma_start(X[:, g * GRP:(g + 1) * GRP, :],
                                 io["x"][g * GRP * P:(g + 1) * GRP * P, :].rearrange("(t p) d -> p t d", p=P)).then_inc(x_in, 16)
                g = NG - 1
                sp.dma_start(X[:, g * GRP:NT - 1, :],
                             io["x"][g * GRP * P:(NT - 1) * P, :].rearrange("(t p) d -> p t d", p=P)).then_inc(x_in, 16)
                sp.dma_start(X[0:TAIL, NT - 1, :], io["x"][(NT - 1) * P:NODES, :]).then_inc(x_in, 16)
                with sp.Fori(0, NG) as g:
                    sp.wait_ge(a_hn, g + 1)
                    sp.dma_start(H0.rearrange("(t p) d -> p t d", p=P)[:, ds(g * GRP, GRP), :],
                                 HN[:, ds(g * GRP, GRP), :]).then_inc(h0_out, 16)
                sp.wait_ge(h0_out, 16 * NG)

            @block.scalar
            def _(act):
                act.dma_start(dt_i, io["dst_tiles"].rearrange("p (q e) -> p q e", q=ETQ)).then_inc(e_in, 16)
                nc.scalar.preload_act_table(ACT.Sqrt)
                with act.Fori(0, NG) as g:
                    hold(act, a_stats, g + 1)
                    nc.scalar.activation(std[:], mv[:, :, 1], ACT.Sqrt, bias=eps[:, 0:1]).then_inc(a_std, 1)

            @block.gpsimd
            def _(pool):
                nc.gpsimd.iota(iota[:], [[1, TABLE]], base=0, channel_multiplier=0,
                               allow_small_or_imprecise_dtypes=True).then_inc(a_const, 1)
                nc.gpsimd.iota(part[:], [[1, 1]], base=0, channel_multiplier=1,
                               allow_small_or_imprecise_dtypes=True).then_inc(a_const, 1)
                nc.gpsimd.iota(NIDT[:], [[P, NT]], base=0, channel_multiplier=1,
                               allow_small_or_imprecise_dtypes=True)
                nc.gpsimd.iota(expert8[:], [[1, E]], base=-E, channel_multiplier=0,
                               allow_small_or_imprecise_dtypes=True)
                nc.gpsimd.memset(zeros[:], 0.0)
                nc.gpsimd.memset(BIG[:, 0:NT * 257], 0.0)

            @block.vector
            def _(dve):
                nc.vector.memset(eps[:], EPS)
                nc.vector.memset(X[:, NT - 1, :], 0.0).then_inc(a_ready, 1)
                nc.vector.memset(ones[:], 1.0)
                dve.wait_ge(a_const, 2)
                nc.vector.tensor_scalar(ident[:], iota[:, 0:P], part[:, 0:1], None, ALU.is_equal)
                nc.vector.tensor_scalar(before[:], iota[:, 0:P], part[:, 0:1], None, ALU.is_gt)
                nc.vector.tensor_scalar(upto[:], iota[:, 0:P], part[:, 0:1], None, ALU.is_ge)
                nc.vector.memset(one4[:], 1.0)
                nc.vector.memset(ones_of(-WIN0), -float(WIN0))
                nc.vector.memset(ones_of(WIN), float(WIN))
                nc.vector.memset(ones_of(-WIN), -float(WIN))
                nc.vector.memset(win_of[:, 0:LAG], float(NWPAD - 1))
                dve.wait_ge(e_in, 16)
                nc.vector.tensor_reduce(lo_dst[:], dt_i, AX.X, ALU.min)
                nc.vector.tensor_reduce(hi_dst[:], dt_i, AX.X, ALU.max)
                dve.wait_ge(x_in, 16 * (NG + 1))
                with dve.Fori(0, NG) as g:
                    tiles = X[:, ds(g * GRP, GRP), :]
                    st = Steps(dve, a_st, g * (LN_A + LN_B))
                    ln_stats(dve, st, tiles)
                    st.wait()
                    dve.sem_inc(a_stats, 1)
                    hold(dve, a_std, g + 1)
                    ln_apply(dve, st, tiles, HN[:, ds(g * GRP, GRP), :])
                    st.wait()
                    dve.sem_inc(a_hn, 1)

        end_phase()

        n_pe, n_st = sem("n_sums"), sem("n_st")
        t_ld, t_conv, t_m, t_pe, t_win, t_rel, t_st = (
            sem("t_" + n) for n in ("tiles_in", "converted", "masks", "sums", "windows", "dst_and_nodes", "st"))
        table_sems = [n_pe, n_st, t_ld, t_conv, t_m, t_pe, t_win, t_rel, t_st]
        cols = lambda k: SCR[0:ETP, k * ETQ * TABLE:(k + 1) * ETQ * TABLE].rearrange("p (q j) -> p q j", q=ETQ)
        past_end, past_start, in_tile = cols(0), cols(1), cols(2)
        tiles_at = lambda k: SCR[0:ETP, 3 * ETQ * TABLE + k * ETQ * P:3 * ETQ * TABLE + (k + 1) * ETQ * P]
        dst_t, src_t, w_t = (tiles_at(k).rearrange("p (q e) -> p q e", q=ETQ) for k in range(3))
        dst_ti, src_ti = (tiles_at(k).bitcast(i32) for k in (3, 4))
        win_f = SCR[0:1, 9216:9216 + TABLE]

        def item_ranges(block, win, chunk):
            @block.vector
            def _(dve):
                st = Steps(dve, n_st)
                shift = win.bit_length() - 1
                st(nc.vector.tensor_scalar(lo_win[:], lo_dst[:], shift, None, ALU.arith_shift_right))
                st(nc.vector.tensor_scalar(hi_win[:], hi_dst[:], shift, None, ALU.arith_shift_right))
                st.wait()
                st(nc.vector.tensor_copy(lo_f[:], lo_win[:]))
                st.wait()
                st(nc.vector.scalar_tensor_tensor(n_f[:], hi_win[:], 1.0, lo_f[:], ALU.add, ALU.subtract))
                st.wait()
                st(nc.vector.tensor_tensor_scan(incl[:], one4[:], n_f[:], 0.0, ALU.mult, ALU.add))
                st.wait()
                dve.sem_inc(n_pe, 1)
                dve.wait_ge(n_pe, 2)
                st(nc.vector.tensor_scalar(ends[:], incl[:], BANKS[0][0:ETP, 0:1], None, ALU.add))
                st(nc.vector.tensor_scalar(chunk_hit[:], iota[0:1, 0:MAXCHUNKS], float(chunk), BANKS[1][0:1, 0:1], ALU.mult, ALU.is_lt))
                st.wait()
                st(nc.vector.tensor_tensor(starts[:], ends[:], n_f[:], ALU.subtract))
                st(nc.vector.tensor_reduce(chunks_f[:], chunk_hit[:], AX.X, ALU.add))
                st.wait()
                st(nc.vector.tensor_tensor(first[:], lo_f[:], starts[:], ALU.subtract))
                st(nc.vector.tensor_tensor(nfirst[:], starts[:], lo_f[:], ALU.subtract))
                st(nc.vector.tensor_copy(chunks_i[:], chunks_f[:]))

            @block.tensor
            def _(pe):
                pe.wait_ge(n_pe, 1)
                nc.tensor.matmul(BANKS[0][0:ETP, 0:1], before[0:ETP, 0:ETP], incl[:, ETQ - 1:ETQ], start=True, stop=True)
                nc.tensor.matmul(BANKS[1][0:1, 0:1], ones[0:ETP, 0:1], incl[:, ETQ - 1:ETQ], start=True, stop=True).then_inc(n_pe, 1)

        def load_chunks():
            return nc.values_load(chunks_i[0:1, 0:1], min_val=1, max_val=MAXCHUNKS,
                                  skip_runtime_bounds_check_because="counted up to MAXCHUNKS")

        def build_table(block, win, nwin, chunk, weights):
            @block.sync
            def _(sp):
                sp.dma_start(dst_ti, io["dst_tiles"]).then_inc(t_ld, 16)
                sp.dma_start(src_ti, io["src_tiles"]).then_inc(t_ld, 16)
                if weights:
                    sp.dma_start(tiles_at(2), io["w_tiles"]).then_inc(t_ld, 16)

            @block.scalar
            def _(act):
                nc.scalar.preload_act_table(ACT.Copy)
                act.wait_ge(t_ld, 48 if weights else 32)
                nc.scalar.activation(tiles_at(0), dst_ti, ACT.Copy).then_inc(t_conv, 1)
                nc.scalar.activation(tiles_at(1), src_ti, ACT.Copy).then_inc(t_conv, 1)
                act.wait_ge(t_pe, 1)
                nc.scalar.activation(src_items[:], BANKS[2][:, 0:TABLE], ACT.Copy)
                if weights:
                    act.wait_ge(t_pe, 2)
                    nc.scalar.activation(aux_items[:], BANKS[4][:, 0:TABLE], ACT.Copy)

            @block.vector
            def _(dve):
                for q in range(ETQ):
                    nc.vector.tensor_scalar(past_end[:, q, :], iota[0:ETP, 0:TABLE], ends[:, q:q + 1], None, ALU.is_ge).then_inc(t_m, 1)
                    nc.vector.tensor_scalar(past_start[:, q, :], iota[0:ETP, 0:TABLE], starts[:, q:q + 1], None, ALU.is_ge).then_inc(t_m, 1)
                dve.wait_ge(t_m, 2 * ETQ)
                nc.vector.tensor_tensor(in_tile, past_start, past_end, ALU.subtract).then_inc(t_m, 1)
                dve.wait_ge(t_win, 1)
                st = Steps(dve, t_st)
                st(nc.vector.tensor_tensor(win_f, BANKS[1][0:1, 0:TABLE], iota[0:1, 0:TABLE], ALU.add))
                nc.vector.tensor_copy(tile_of[:], BANKS[0][0:1, 0:TABLE])
                st.wait()
                st(nc.vector.tensor_scalar(win_f, win_f, float(nwin - 1), None, ALU.min))
                st.wait()
                dve.sem_inc(t_win, 1)
                nc.vector.tensor_copy(win_of[:, LAG:], win_f)
                for t, by in ((ends, -chunk), (starts, -chunk), (first, chunk), (nfirst, -chunk)):
                    nc.vector.tensor_scalar(t[:], t[:], float(by), None, ALU.add)
                dve.wait_ge(t_rel, 1)
                nc.vector.tensor_copy(dst_items[:], BANKS[3][:, 0:TABLE])
                if not weights:
                    nc.vector.tensor_scalar(aux_items[0:win, :], BANKS[5][0:win, 0:TABLE], part[0:win, 0:1], None, ALU.add)

            @block.tensor
            def _(pe):
                for q in range(ETQ):
                    pe.wait_ge(t_m, 2 * (q + 1))
                    last = q == ETQ - 1
                    nc.tensor.matmul(BANKS[0][0:1, 0:TABLE], ones[0:ETP, 0:1], past_end[:, q, :], start=q == 0, stop=last)
                    nc.tensor.matmul(BANKS[1][0:1, 0:TABLE], first[:, q:q + 1], past_start[:, q, :], start=q == 0, stop=False)
                    m = nc.tensor.matmul(BANKS[1][0:1, 0:TABLE], nfirst[:, q:q + 1], past_end[:, q, :], start=False, stop=last)
                m.then_inc(t_win, 1)
                pe.wait_ge(t_conv, 2)
                pe.wait_ge(t_m, 2 * ETQ + 1)
                for bank, tiles in ((2, src_t), (4, w_t)) if weights else ((2, src_t),):
                    for q in range(ETQ):
                        m = nc.tensor.matmul(BANKS[bank][:, 0:TABLE], tiles[:, q, :], in_tile[:, q, :], start=q == 0, stop=q == ETQ - 1)
                    m.then_inc(t_pe, 1)
                for q in range(ETQ):
                    nc.tensor.matmul(BANKS[3][:, 0:TABLE], dst_t[:, q, :], in_tile[:, q, :], start=q == 0, stop=False)
                pe.wait_ge(t_win, 2)
                m = nc.tensor.matmul(BANKS[3][:, 0:TABLE], ones_of(-win), win_f, start=False, stop=True)
                if not weights:
                    m = nc.tensor.matmul(BANKS[5][0:win, 0:TABLE], ones_of(win)[:, 0:win], win_f, start=True, stop=True)
                m.then_inc(t_rel, 1)

        R0 = UN0 // 2
        rows_in = sems("rows_in", R0)
        R1 = UN1 // 2
        rows_in1 = sems("rows1_in", R1)
        b_idx, b_scaled, b_S, b_pe, b_acc = (sem(n) for n in ("b_idx", "b_scaled", "b_onehot", "b_summed", "b_acc"))
        b_sems = [b_idx, b_scaled, b_S, b_pe, b_acc]
        rows0 = SCR[:, 0:R0 * D].rearrange("p (k n) -> p k n", n=D)
        msg0 = SCR[:, 2560:2560 + 4 * 257].rearrange("p (k n) -> p k n", n=257)
        S0 = SCR[:, 3600:3600 + 4 * WIN0].rearrange("p (k n) -> p k n", n=WIN0)

        def gather_items(pool, unroll, iters, ring, source, arrived, done):
            slots = unroll // 2
            with pool.Fori(0, iters) as i:
                for k in range(unroll):
                    hold(pool, done, i * unroll + (k + 1))
                    if k % slots == 0:
                        nc.gpsimd.tensor_copy(idx[:, k:k + slots], src_items[:, ds(i * unroll + k, slots)]).then_inc(b_idx, 1)
                        hold(pool, b_idx, i * 2 + (k // slots + 1))
                    nc.gpsimd.indirect_dma_start(
                        out=ring[:, k % slots, :], out_offset=None, in_=source,
                        in_offset=bass.IndirectOffsetOnAxis(ap=idx[:, k:k + 1].bitcast(u32), axis=0)).then_inc(arrived[k % slots], 16)

        def edge_sum0(block, chunk):
            ITERS = CHUNK0 // UN0

            @block.gpsimd
            def _(pool):
                gather_items(pool, UN0, ITERS, rows0, H0, rows_in, b_scaled)

            @block.scalar
            def _(act):
                act.sem_inc(b_scaled, R0)
                with act.Fori(0, ITERS) as i:
                    for k in range(UN0):
                        act.wait_ge(rows_in[k % R0], chunk * (ITERS * 32) + i * 32 + 16 * (k // R0 + 1))
                        act.nop(nofuse=True)
                        hold(act, b_pe, i * UN0 + (k + 1))
                        nc.scalar.activation(msg0[:, k % 4, 0:D], rows0[:, k % R0, :], ACT.Copy,
                                             scale=aux_items[:, ds(i * UN0 + k, 1)]).then_inc(b_scaled, 1)

            @block.vector
            def _(dve):
                nc.vector.memset(msg0[:, :, D:D + 1], 1.0).then_inc(b_S, 1)
                dve.sem_inc(b_acc, 4)
                with dve.Fori(0, ITERS) as i:
                    ws = load_regs(ENG.DVE, win_of[0:1, ds(i * UN0 + LAG, UN0)], 0, NWIN0 - 1)

                    def onehot(k):
                        hold(dve, b_pe, i * UN0 + (k + 1))
                        nc.vector.tensor_scalar(S0[:, k % 4, :], iota[:, 0:WIN0], dst_items[:, ds(i * UN0 + k, 1)],
                                                None, ALU.is_equal).then_inc(b_S, 1)
                    onehot(0)
                    onehot(1)
                    for k in range(UN0):
                        if k + 2 < UN0:
                            onehot(k + 2)
                        hold(dve, b_pe, i * UN0 + (k + 5))
                        hold(dve, b_acc, i * UN0 + (k + 4))
                        a = acc0[:, ds(ws[k], 1), :]
                        nc.vector.tensor_tensor(a, a, BANKS[k % 4][:, 0:257].rearrange("p (o n) -> p o n", o=1), ALU.add).then_inc(b_acc, 1)

            @block.tensor
            def _(pe):
                pe.sem_inc(b_pe, 4)
                with pe.Fori(0, ITERS) as i:
                    for k in range(UN0):
                        pe.wait_ge(b_S, i * UN0 + (k + 2))
                        pe.wait_ge(b_scaled, i * UN0 + (k + 1 + R0))
                        pe.wait_ge(b_acc, i * UN0 + (k + 1))
                        nc.tensor.matmul(BANKS[k % 4][:, 0:257], S0[:, k % 4, :], msg0[:, k % 4, :],
                                         start=True, stop=True).then_inc(b_pe, 1)

        with nc.Block() as block:
            item_ranges(block, WIN0, CHUNK0)
        n_chunks0 = load_chunks()
        with nc.Fori(0, n_chunks0) as chunk:
            with nc.Block() as block:
                build_table(block, WIN0, NWIN0, CHUNK0, weights=True)
            with nc.Block() as block:
                edge_sum0(block, chunk)
            with nc.Block() as block:
                clear(block, table_sems + b_sems)

        def group(t3, g):
            return t3[:, ds(g * GRP, GRP), :]

        def walk_tiles(eng, *stages):
            most = max(lead for _, lead in stages)

            def turn(s):
                for step, lead in stages:
                    if 0 <= s + lead < NT:
                        step(s + lead, (s + lead) % 4, (s + lead) // 4)
            rounds = (NT - most) // 4
            for s in range(-most, 0):
                turn(s)
            with eng.Fori(0, rounds) as i:
                for k in range(4):
                    for step, lead in stages:
                        step(i * 4 + (k + lead), (k + lead) % 4, i + (k + lead) // 4)
            for s in range(4 * rounds, NT):
                turn(s)

        def tile_stats(st, tile, slot):
            st(nc.vector.bn_stats(stats[:, slot, :], tile))
            st.wait()
            st(nc.vector.bn_aggr(mv[:, slot, :], stats[:, slot, :]))
            st.wait()

        def tile_norm(st, tile, slot, to):
            st(nc.vector.reciprocal(rstd[:, slot:slot + 1], std[:, slot:slot + 1]))
            st.wait()
            st(nc.vector.tensor_scalar(to, tile, mv[:, slot, 0:1], rstd[:, slot:slot + 1], ALU.subtract, ALU.mult))
            st.wait()

        def tile_std(slot):
            return nc.scalar.activation(std[:, slot:slot + 1], mv[:, slot, 1:2], ACT.Sqrt, bias=eps[:, 0:1])

        def pe_transpose(bank, rows):
            nc.tensor.transpose(BANKS[bank][:, 0:P], rows[:, 0:P], ident[:])
            return nc.tensor.transpose(BANKS[bank][:, P:D], rows[:, P:D], ident[:])

        def ring4(at):
            return SCR[:, at:at + 4 * D].rearrange("p (s n) -> p s n", n=D)

        def halves(slot_tile):
            return slot_tile.rearrange("p (c n) -> p c n", c=2)

        stage_acc, xt1, h_rows, xt2 = ring4(0), ring4(1024), ring4(2048), ring4(3072)
        W0s = SCR[:, 5120:5632].rearrange("p (c n) -> p c n", c=2)
        gate_ws = SCR[:, 5632:5648].rearrange("p (c n) -> p c n", c=2)
        gate_bs = SCR[:, 5648:5656]

        c_stage, c_T1, c_x1, c_O, c_stats, c_std, c_h, c_T2, c_x2, c_L, c_lg, c_hn, c_x, c_bn, c_rstd = (
            phase_sem("c_" + n) for n in ("stage", "sumsT", "sumsT_read", "out", "stats", "std", "norm", "normT", "normT_read",
                                          "logits", "logits_read", "copied", "updated", "bn_stats", "rstd"))
        O_PAIRS = ((3, 0, 2), (4, 2, 2), (5, 4, 1))

        def node_update0(block):
            @block.sync
            def _(sp):
                sp.dma_start(W0s, io["L0_gnn_weight"].rearrange("(c p) n -> p c n", p=P)).then_inc(weights_in, 16)
                sp.dma_start(gate_ws, io["L0_ffn_gate_w"].rearrange("(c p) n -> p c n", p=P)).then_inc(weights_in, 16)
                sp.dma_start(gate_bs, io["L0_ffn_gate_b"].partition_broadcast(P)).then_inc(weights_in, 16)
                for buf, rows in ((BUF0, TRASH0), (BUF1, TRASH1)):
                    flat = buf[0:rows, :].rearrange("(p r) d -> p (r d)", p=P)
                    width = flat.shape[1]
                    for a in range(0, width, 1024):
                        sp.dma_start(flat[:, a:a + 1024], zeros[:]).then_inc(zero_fill, 16)

            @block.gpsimd
            def _(pool):
                def stage(n, slot, use):
                    hold(pool, c_T1, n + 1)
                    nc.gpsimd.tensor_copy(stage_acc[:, slot:slot + 1, :], acc0[:, ds(n, 1), 0:D]).then_inc(c_stage, 1)

                def copy_norm(n, slot, use):
                    hold(pool, c_h, n + 1)
                    nc.gpsimd.tensor_copy(HN[:, ds(n, 1), :], h_rows[:, slot:slot + 1, :]).then_inc(c_hn, 1)
                pool.sem_inc(c_hn, 4)
                nc.gpsimd.tensor_copy(CNT[:], acc0[:, :, D])
                walk_tiles(pool, (stage, 5), (copy_norm, 1))

            @block.tensor
            def _(pe):
                pe.sem_inc(c_T1, 4)
                pe.sem_inc(c_O, 4)
                pe.sem_inc(c_T2, 4)
                pe.sem_inc(c_L, 4)
                pe.wait_ge(weights_in, 48)

                def turn_sums(n, slot, use):
                    pe.wait_ge(c_stage, n + 1)
                    pe.wait_ge(c_x1, n + 1)
                    pe_transpose(slot % 2, stage_acc[:, slot, :]).then_inc(c_T1, 1)

                def product(n, slot, use):
                    pe.wait_ge(c_x1, n + 3)
                    pe.wait_ge(c_x, n + 1)
                    for c in range(2):
                        m = nc.tensor.matmul(BANKS[2 + slot % 2][:, 0:D], halves(xt1[:, slot, :])[:, c, :], W0s[:, c, :], start=c == 0, stop=c == 1)
                    m.then_inc(c_O, 1)

                def turn_norm(n, slot, use):
                    pe.wait_ge(c_h, n + 1)
                    pe.wait_ge(c_x2, n + 1)
                    pe_transpose(4 + slot % 2, h_rows[:, slot, :]).then_inc(c_T2, 1)

                def logits(n, slot, use):
                    pe.wait_ge(c_x2, n + 3)
                    pe.wait_ge(c_lg, n + 1)
                    for c in range(2):
                        m = nc.tensor.matmul(BANKS[6 + slot % 2][:, 0:E], halves(xt2[:, slot, :])[:, c, :], gate_ws[:, c, :], start=c == 0, stop=c == 1)
                    m.then_inc(c_L, 1)
                walk_tiles(pe, (turn_sums, 5), (product, 4), (turn_norm, 1), (logits, 0))

            @block.scalar
            def _(act):
                act.sem_inc(c_x1, 2)
                act.sem_inc(c_x2, 2)
                nc.scalar.preload_act_table(ACT.Sqrt)

                def read_sums(n, slot, use):
                    hold(act, c_T1, n + 5)
                    hold(act, c_O, n + 1)
                    nc.scalar.activation(xt1[:, slot, :], BANKS[slot % 2][:, 0:D], ACT.Copy).then_inc(c_x1, 1)

                def deviation(n, slot, use):
                    hold(act, c_stats, n + 1)
                    tile_std(slot).then_inc(c_std, 1)

                def read_norm(n, slot, use):
                    hold(act, c_T2, n + 5)
                    hold(act, c_L, n + 1)
                    nc.scalar.activation(xt2[:, slot, :], BANKS[4 + slot % 2][:, 0:D], ACT.Copy).then_inc(c_x2, 1)
                walk_tiles(act, (read_sums, 5), (deviation, 3), (read_norm, 1))

            @block.vector
            def _(dve):
                dve.sem_inc(c_lg, 2)
                dve.sem_inc(c_x, 2)
                dve.wait_ge(weights_in, 48)

                def update(n, slot, use):
                    hold(dve, c_O, n + 5)
                    x = X[:, ds(n, 1), :]
                    nc.vector.scalar_tensor_tensor(x, BANKS[2 + slot % 2][:, 0:D].unsqueeze(1), 0.0, x, ALU.max, ALU.add).then_inc(c_x, 1)

                def invert(n, slot, use):
                    hold(dve, c_std, n + 1)
                    nc.vector.reciprocal(rstd[:, slot:slot + 1], std[:, slot:slot + 1]).then_inc(c_rstd, 1)

                def gather_stats(n, slot, use):
                    hold(dve, c_x, n + 3)
                    nc.vector.bn_stats(stats[:, slot, :], X[:, ds(n, 1), :].rearrange("p o n -> p (o n)")).then_inc(c_bn, 1)

                def norm(n, slot, use):
                    hold(dve, c_rstd, n + 1)
                    hold(dve, c_T2, n + 1)
                    hold(dve, c_hn, n + 1)
                    nc.vector.tensor_scalar(h_rows[:, slot:slot + 1, :], X[:, ds(n, 1), :], mv[:, slot, 0:1], rstd[:, slot:slot + 1],
                                            ALU.subtract, ALU.mult).then_inc(c_h, 1)

                def aggregate(n, slot, use):
                    hold(dve, c_bn, n + 1)
                    nc.vector.bn_aggr(mv[:, slot, :], stats[:, slot, :]).then_inc(c_stats, 1)

                def read_logits(n, slot, use):
                    hold(dve, c_L, n + 5)
                    nc.vector.tensor_tensor(LG[:, ds(n, 1), :], BANKS[6 + slot % 2][:, 0:E].unsqueeze(1),
                                            gate_bs.unsqueeze(1), ALU.add).then_inc(c_lg, 1)
                walk_tiles(dve, (update, 3), (invert, 2), (gather_stats, 3), (norm, 2), (aggregate, 3), (read_logits, 0))

        with nc.Block() as block:
            node_update0(block)

        def t_bank(k):
            return BANKS[k // 2][:, (k % 2) * 256:(k % 2) * 256 + 256].rearrange("p (c n) -> p c n", c=2)

        def pe_transposes(stage):
            for k in range(GRP):
                for c in range(2):
                    m = nc.tensor.transpose(t_bank(k)[:, c, :], stage[:, k, c * P:(c + 1) * P], ident[:])
            return m

        def act_evacuate(to):
            nc.scalar.activation(to[:, 0:512], BANKS[0][:, :], ACT.Copy)
            nc.scalar.activation(to[:, 512:1024], BANKS[1][:, :], ACT.Copy)
            return nc.scalar.activation(to[:, 1024:1280], BANKS[2][:, 0:256], ACT.Copy)

        xt_flat = SCR[:, 2560:3840]
        xt = xt_flat.rearrange("p (k c n) -> p k c n", c=2, n=P)
        hstage = SCR[:, 3840:5120].rearrange("p (k n) -> p k n", n=D)

        def bce(t2):
            return t2[:].unsqueeze(2).to_broadcast([P, NT, E])

        def bct(row):
            return row.unsqueeze(1).to_broadcast([P, NT, E])

        def first_best(st, logits, best, onehot, scratch):
            st(nc.vector.tensor_reduce(best[:], logits[:], AX.X, ALU.max))
            st.wait()
            st(nc.vector.tensor_tensor(onehot[:], logits[:], bce(best), ALU.is_equal))
            st.wait()
            st(nc.vector.tensor_tensor(onehot[:], onehot[:], bct(expert8[:]), ALU.mult))
            st.wait()
            st(nc.vector.tensor_reduce(scratch[:], onehot[:], AX.X, ALU.min))
            st.wait()
            st(nc.vector.tensor_tensor(onehot[:], bct(expert8[:]), bce(scratch), ALU.is_equal))
            st.wait()

        def ranks(dve, st, counted, ready, summed, wait_value):
            st.wait()
            dve.sem_inc(ready, 1)
            dve.wait_ge(summed, wait_value)
            for e in range(E):
                st(nc.vector.tensor_tensor_scan(CUM[:, :, e], ones[:, 0:NT], BANKS[1][:, 0:NT * E].rearrange("p (t e) -> p t e", e=E)[:, :, e],
                                                0.0, ALU.mult, ALU.add))
            st(nc.vector.tensor_copy(RT[:], BANKS[1][:, 0:NT * E].rearrange("p (t e) -> p t e", e=E)))
            st.wait()
            st(nc.vector.tensor_tensor(RT[:], CUM[:], RT[:], ALU.subtract))
            st.wait()
            st(nc.vector.tensor_tensor(RT[:], RT[:], BANKS[0][:, 0:NT * E].rearrange("p (t e) -> p t e", e=E), ALU.add))
            st.wait()

        def pe_ranks(pe, counted, ready, summed, value):
            pe.wait_ge(ready, value)
            flat = counted[:].rearrange("p t e -> p (t e)")
            nc.tensor.matmul(BANKS[0][:, 0:NT * E], upto[:], flat, start=True, stop=True)
            nc.tensor.matmul(BANKS[1][:, 0:NT * E], ones[:], flat, start=True, stop=True).then_inc(summed, 1)

        r_st, r_ready, r_sum, r_exp = (phase_sem("r_" + n) for n in ("st", "ready", "summed", "exp"))
        r_done = sem("r_scattered")

        def route0(block):
            @block.vector
            def _(dve):
                st = Steps(dve, r_st)
                first_best(st, LG, r_a, OH1, r_b)
                st(nc.vector.tensor_tensor(LG[:], LG[:], bce(r_a), ALU.subtract))
                st.wait()
                dve.sem_inc(r_exp, 1)
                ranks(dve, st, OH1, r_ready, r_sum, 1)
                st(nc.vector.tensor_tensor(RT[:], RT[:], OH1[:], ALU.mult))
                st.wait()
                st(nc.vector.tensor_reduce(r_c[:], RT[:], AX.X, ALU.add))
                st.wait()
                st(nc.vector.tensor_scalar(keep1[:], r_c[:], float(CAP), None, ALU.is_le))
                st(nc.vector.tensor_scalar(r_b[:], r_b[:], float(ESLOT), float(E * ESLOT - 1), ALU.mult, ALU.add))
                st(nc.vector.tensor_scalar(r_a[:], r_c[:], float(CAP), None, ALU.min))
                st.wait()
                st(nc.vector.tensor_tensor(r_a[:], r_a[:], r_b[:], ALU.add))
                st.wait()
                st(nc.vector.tensor_scalar(r_b[:], NIDT[:], float(TRASH0), None, ALU.add))
                st.wait()
                st(nc.vector.tensor_copy(from1[:], r_a[:]))
                st.wait()
                st(nc.vector.tensor_tensor(r_a[:], r_a[:], r_b[:], ALU.subtract))
                st.wait()
                st(nc.vector.tensor_tensor(r_a[:], r_a[:], keep1[:], ALU.mult))
                st.wait()
                st(nc.vector.tensor_tensor(r_a[:], r_a[:], r_b[:], ALU.add))
                st.wait()
                st(nc.vector.tensor_copy(to1[:], r_a[:]))
                st.wait()
                dve.sem_inc(r_ready, 1)
                dve.wait_ge(r_exp, 2)
                st(nc.vector.tensor_reduce(r_c[:], LG[:], AX.X, ALU.add))
                st.wait()
                st(nc.vector.reciprocal(r_c[:], r_c[:]))
                st.wait()
                st(nc.vector.tensor_tensor(keep1[:], keep1[:], r_c[:], ALU.mult))

            @block.scalar
            def _(act):
                act.wait_ge(r_exp, 1)
                nc.scalar.activation(LG[:], LG[:], ACT.Exp).then_inc(r_exp, 1)

            @block.tensor
            def _(pe):
                pe_ranks(pe, OH1, r_ready, r_sum, 1)

            @block.gpsimd
            def _(pool):
                pool.wait_ge(zero_fill, 16 * (TRASH0 + TRASH1) * D // (P * 1024))
                pool.wait_ge(r_ready, 2)
                for t in range(NT):
                    nc.gpsimd.indirect_dma_start(
                        out=BUF0, out_offset=bass.IndirectOffsetOnAxis(ap=to1[:, t:t + 1].bitcast(u32), axis=0),
                        in_=HN[:, t, :], in_offset=None).then_inc(r_done, 16)
                pool.wait_ge(r_done, 16 * NT)

        with nc.Block() as block:
            route0(block)

        end_phase()

        d_w, d_x = ([phase_sem(f"{n}{k}") for k in range(2)] for n in ("d_weights", "d_rows"))
        d_T, d_xT, d_h, d_hT, d_y, d_ys = (phase_sem("d_" + n) for n in ("transposed", "xT", "hidden", "relu", "y", "y_staged"))
        d_store, d_free = sem("d_store"), phase_sem("d_stage_free")
        w1s = [BIG[:, a * 4096:a * 4096 + 2048].rearrange("p (c f) -> p c f", c=2) for a in range(2)]
        w2s = [BIG[:, a * 4096 + 2048:a * 4096 + 4096].rearrange("p (f n) -> p f n", n=D) for a in range(2)]
        hT = [BIG[:, 8192 + a * 4096:8192 + (a + 1) * 4096].rearrange("p (f s) -> p f s", s=ESLOT) for a in range(2)]
        xin = [SCR[:, a * 1024:(a + 1) * 1024].rearrange("p (s n) -> p s n", n=D) for a in range(2)]
        xT = [SCR[:, 2048 + a * 1024:2048 + (a + 1) * 1024].rearrange("p (c s) -> p c s", c=2) for a in range(2)]
        ys = [SCR[:, 4096 + a * 1024:4096 + (a + 1) * 1024].rearrange("p (s n) -> p s n", n=D) for a in range(2)]
        b2s = SCR[:, 6144:6144 + E * D].rearrange("p (e n) -> p e n", e=E)
        b1s = SCR[:, 8192:8192 + 64]
        d_bias = phase_sem("d_bias")
        NF = F0 // P
        NS = ESLOT // P

        def experts0(block):
            @block.sync
            def _(sp):
                sp.dma_start(b1s, io["b1_col"]).then_inc(d_bias, 16)
                sp.dma_start(b2s, io["L0_ffn_b2"].rearrange("e n -> (e n)").partition_broadcast(P).rearrange("p (e n) -> p e n", e=E)).then_inc(d_bias, 16)
                with sp.Fori(0, E // 2) as i:
                    for a in range(2):
                        hold(sp, d_y, NS * (2 * i + a) + NS + 1)
                        sp.dma_start(xin[a], BUF0[ds((2 * i + a) * ESLOT, ESLOT), :].rearrange("(s p) n -> p s n", p=P)).then_inc(d_x[a], 16)
                        sp.dma_start(w1s[a], io["L0_ffn_w1"][ds(2 * i + a, 1), :, :].rearrange("e (c p) f -> p (e c) f", p=P)).then_inc(d_w[a], 16)
                        sp.dma_start(w2s[a], io["L0_ffn_w2"][ds(2 * i + a, 1), :, :].rearrange("e (f p) n -> p (e f) n", p=P)).then_inc(d_w[a], 16)

            @block.tensor
            def _(pe):
                pe.sem_inc(d_y, 2 * NS + 1)
                with pe.Fori(0, E // 2) as i:
                    for a in range(2):
                        n = 2 * i + a
                        pe.wait_ge(d_x[a], i * 16 + 16)
                        pe.wait_ge(d_xT, n + 1)
                        for s in range(NS):
                            for c in range(2):
                                m = nc.tensor.transpose(BANKS[c][:, s * P:(s + 1) * P], xin[a][:, s, c * P:(c + 1) * P], ident[:])
                        m.then_inc(d_T, 1)
                    for a in range(2):
                        n = 2 * i + a
                        pe.wait_ge(d_xT, n + 2)
                        pe.wait_ge(d_w[a], i * 32 + 32)
                        for f in range(NF):
                            pe.wait_ge(d_hT, n * NF + (f + 1))
                            for c in range(2):
                                m = nc.tensor.matmul(BANKS[2 + f % 4][:, 0:ESLOT], w1s[a][:, c, f * P:(f + 1) * P], xT[a][:, c, :],
                                                     start=c == 0, stop=c == 1)
                            m.then_inc(d_h, 1)
                        pe.wait_ge(d_hT, (n + 1) * NF + 4)
                        for s in range(NS):
                            pe.wait_ge(d_ys, n * NS + (s + 1))
                            for f in range(NF):
                                m = nc.tensor.matmul(BANKS[6 + s % 2][:, 0:D], hT[a][:, f, s * P:(s + 1) * P], w2s[a][:, f, :],
                                                     start=f == 0, stop=f == NF - 1)
                            m.then_inc(d_y, 1)

            @block.scalar
            def _(act):
                act.sem_inc(d_xT, 1)
                act.sem_inc(d_hT, 4)
                nc.scalar.preload_act_table(ACT.Relu)
                act.wait_ge(d_bias, 32)
                with act.Fori(0, E // 2) as i:
                    for a in range(2):
                        n = 2 * i + a
                        hold(act, d_T, n + 1)
                        nc.scalar.activation(xT[a][:, 0, :], BANKS[0][:, :], ACT.Copy)
                        nc.scalar.activation(xT[a][:, 1, :], BANKS[1][:, :], ACT.Copy).then_inc(d_xT, 1)
                    for a in range(2):
                        n = 2 * i + a
                        for f in range(NF):
                            hold(act, d_h, n * NF + (f + 1))
                            nc.scalar.activation(hT[a][:, f, :], BANKS[2 + f % 4][:, 0:ESLOT], ACT.Relu,
                                                 bias=b1s[:, ds(n * NF + f, 1)]).then_inc(d_hT, 1)

            @block.vector
            def _(dve):
                dve.sem_inc(d_ys, 2)
                dve.wait_ge(d_bias, 32)
                with dve.Fori(0, E // 2) as i:
                    for a in range(2):
                        n = 2 * i + a
                        hold(dve, d_free, n + 1)
                        for s in range(NS):
                            hold(dve, d_y, n * NS + (s + 2 + 2 * NS))
                            nc.vector.tensor_tensor(ys[a][:, s:s + 1, :], BANKS[6 + s % 2][:, 0:D].unsqueeze(1), b2s[:, ds(n, 1), :],
                                                    ALU.add).then_inc(d_ys, 1)

            @block.gpsimd
            def _(pool):
                pool.sem_inc(d_free, 2)
                with pool.Fori(0, E // 2) as i:
                    for a in range(2):
                        n = 2 * i + a
                        hold(pool, d_ys, (n + 1) * NS + 2)
                        nc.gpsimd.dma_start(Y0[ds(n * ESLOT, ESLOT), :].rearrange("(s p) n -> p s n", p=P), ys[a]).then_inc(d_store, 16)
                        hold(pool, d_store, n * 16 + 16)
                        pool.sem_inc(d_free, 1)

        with nc.Block() as block:
            experts0(block)

        GY, finite_r, beyond_r, fill_r = ring4(0), ring4(1024), ring4(2048), ring4(3072)
        eW1s = SCR[:, 4096:4096 + 4 * DM].rearrange("p (c n) -> p c n", n=DM)
        eb1s = SCR[:, 6144:6144 + DM]
        pstage = SCR[:, 6656:6656 + 4 * DM].rearrange("p (s n) -> p s n", n=DM)
        h_rows1, xt3 = ring4(8704), SCR2[:, 0:1024].rearrange("p (s n) -> p s n", n=D)
        Q = BIG[0:WIN, :].rearrange("p (w n) -> p w n", n=DM)
        acc1 = BIG[WIN:P, :].rearrange("p (w n) -> p w n", n=DM)
        e_gy = sems("e_rows", 4)
        e_store = [phase_sem(f"e_store{k}") for k in range(4)]
        (e_idx, e_y, e_over, e_stats, e_std, e_rstd, e_h, e_T, e_xt, e_pq, e_p, e_q, e_landed, e_x, e_w) = (
            phase_sem("e_" + n) for n in ("index", "scaled", "beyond", "stats", "std", "rstd", "norm", "transposed", "xt",
                                          "products", "src_read", "dst_read", "landed", "x_steps", "weights"))
        XS = 6

        def project(block):
            @block.sync
            def _(sp):
                sp.dma_start(eW1s, io["L1_gnn_eW1"][0:4 * P, :].rearrange("(c p) n -> p c n", p=P)).then_inc(e_w, 16)
                sp.dma_start(eb1s, io["L1_gnn_eb1"].partition_broadcast(P)).then_inc(e_w, 16)

                def store(n, slot, use):
                    hold(sp, e_p, n + 3)
                    sp.dma_start(PROJ[ds(n * P, P), :], pstage[:, slot, :]).then_inc(e_store[slot], 16)

                def landed(n, slot, use):
                    hold(sp, e_store[slot], 16 * (use + 1))
                    sp.sem_inc(e_landed, 1)
                walk_tiles(sp, (store, 1), (landed, 0))

            @block.gpsimd
            def _(pool):
                def beyond(n, slot, use):
                    hold(pool, e_y, n + 1)
                    nc.gpsimd.tensor_scalar(beyond_r[:, slot, :], GY[:, slot, :], 0.0, 1e4, ALU.is_gt, ALU.mult).then_inc(e_over, 1)

                def gather(n, slot, use):
                    hold(pool, e_x, XS * n + 4)
                    nc.gpsimd.tensor_copy(idx[:, slot:slot + 1], from1[:, ds(n, 1)]).then_inc(e_idx, 1)
                    hold(pool, e_idx, n + 1)
                    nc.gpsimd.indirect_dma_start(
                        out=GY[:, slot, :], out_offset=None, in_=Y0,
                        in_offset=bass.IndirectOffsetOnAxis(ap=idx[:, slot:slot + 1].bitcast(u32), axis=0)).then_inc(e_gy[slot], 16)
                walk_tiles(pool, (gather, 6), (beyond, 4))
                pool.wait_ge(e_over, NT)
                nc.gpsimd.memset(BIG[WIN:P, :], 0.0)

            @block.scalar
            def _(act):
                act.sem_inc(e_xt, 2)
                act.sem_inc(e_q, 4)
                nc.scalar.preload_act_table(ACT.Sqrt)

                def scale(n, slot, use):
                    hold(act, e_gy[slot], 16 * (use + 1))
                    nc.scalar.activation(GY[:, slot, :], GY[:, slot, :], ACT.Copy, scale=keep1[:, ds(n, 1)]).then_inc(e_y, 1)

                def deviation(n, slot, use):
                    hold(act, e_stats, n + 1)
                    tile_std(slot).then_inc(e_std, 1)

                def read_norm(n, slot, use):
                    hold(act, e_T, n + 5)
                    hold(act, e_pq, 2 * n + 2)
                    nc.scalar.activation(xt3[:, slot, :], BANKS[slot % 2][:, 0:D], ACT.Copy).then_inc(e_xt, 1)

                def read_q(n, slot, use):
                    hold(act, e_pq, 2 * n + 10)
                    for a in range(2):
                        nc.scalar.activation(Q[:, ds(n * 2 + a, 1), :], BANKS[5 + 2 * (slot % 2)][a * WIN:(a + 1) * WIN, :].unsqueeze(1),
                                             ACT.Copy).then_inc(e_q, 1)
                walk_tiles(act, (read_norm, 1), (scale, 4), (deviation, 3), (read_q, 0))

            @block.tensor
            def _(pe):
                pe.sem_inc(e_T, 4)
                pe.sem_inc(e_pq, 8)
                pe.wait_ge(e_w, 32)

                def turn_norm(n, slot, use):
                    pe.wait_ge(e_h, n + 1)
                    pe.wait_ge(e_xt, n + 1)
                    pe_transpose(slot % 2, h_rows1[:, slot, :]).then_inc(e_T, 1)

                def products(n, slot, use):
                    pe.wait_ge(e_xt, n + 3)
                    pe.wait_ge(e_p, n + 1)
                    pe.wait_ge(e_q, 2 * n + 2)
                    for side in range(2):
                        for c in range(2):
                            m = nc.tensor.matmul(BANKS[4 + 2 * (slot % 2) + side][:, :], halves(xt3[:, slot, :])[:, c, :], eW1s[:, 2 * side + c, :],
                                                 start=c == 0, stop=c == 1)
                        m.then_inc(e_pq, 1)
                walk_tiles(pe, (turn_norm, 1), (products, 0))

            @block.vector
            def _(dve):
                dve.sem_inc(e_x, 4 * XS)
                dve.sem_inc(e_p, 2)
                dve.sem_inc(e_landed, 4)
                dve.wait_ge(e_w, 32)
                step = lambda n, k: XS * (n + 4) + k

                def masks(n, slot, use):
                    hold(dve, e_y, n + 1)
                    nc.vector.tensor_scalar(finite_r[:, slot, :].bitcast(i32), GY[:, slot, :], 0.0, 0.0, ALU.mult, ALU.is_equal).then_inc(e_x, 1)
                    nc.vector.tensor_scalar(fill_r[:, slot, :], GY[:, slot, :], 0.0, -1e4, ALU.is_lt, ALU.mult).then_inc(e_x, 1)

                def invert(n, slot, use):
                    hold(dve, e_std, n + 1)
                    nc.vector.reciprocal(rstd[:, slot:slot + 1], std[:, slot:slot + 1]).then_inc(e_rstd, 1)

                def fill(n, slot, use):
                    hold(dve, e_over, n + 1)
                    hold(dve, e_x, step(n, 2))
                    nc.vector.tensor_tensor(fill_r[:, slot, :], fill_r[:, slot, :], beyond_r[:, slot, :], ALU.add).then_inc(e_x, 1)

                def norm(n, slot, use):
                    hold(dve, e_rstd, n + 1)
                    hold(dve, e_T, n + 1)
                    nc.vector.tensor_scalar(h_rows1[:, slot:slot + 1, :], X[:, ds(n, 1), :], mv[:, slot, 0:1], rstd[:, slot:slot + 1],
                                            ALU.subtract, ALU.mult).then_inc(e_h, 1)

                def select(n, slot, use):
                    hold(dve, e_x, step(n, 3))
                    nc.vector.copy_predicated(fill_r[:, slot, :], finite_r[:, slot, :].bitcast(i32), GY[:, slot, :]).then_inc(e_x, 1)

                def add_bias(n, slot, use):
                    hold(dve, e_landed, n + 1)
                    hold(dve, e_pq, 2 * n + 9)
                    nc.vector.tensor_tensor(pstage[:, slot, :], BANKS[4 + 2 * (slot % 2)][:, :], eb1s, ALU.add).then_inc(e_p, 1)

                def update(n, slot, use):
                    hold(dve, e_x, step(n, 4))
                    nc.vector.tensor_tensor(X[:, ds(n, 1), :], X[:, ds(n, 1), :], fill_r[:, slot:slot + 1, :], ALU.add).then_inc(e_x, 1)
                    hold(dve, e_x, step(n, 5))
                    nc.vector.bn_stats(stats[:, slot, :], X[:, ds(n, 1), :].rearrange("p o n -> p (o n)")).then_inc(e_x, 1)
                    hold(dve, e_x, step(n, 6))
                    nc.vector.bn_aggr(mv[:, slot, :], stats[:, slot, :]).then_inc(e_stats, 1)
                walk_tiles(dve, (masks, 3), (invert, 2), (fill, 3), (norm, 2), (select, 3), (add_bias, 0), (update, 3))

        with nc.Block() as block:
            project(block)

        end_phase()

        f_rows = SCR[:, 0:R1 * DM].rearrange("p (k n) -> p k n", n=DM)
        f_rhs = SCR[:, 4096:4096 + 4 * DM].rearrange("p (k n) -> p k n", n=DM)
        f_msg = SCR[:, 6144:6144 + 4 * DM].rearrange("p (k n) -> p k n", n=DM)
        f_cat = SCR[:, 8192:8192 + 4 * P].rearrange("p (k n) -> p k n", n=P)
        f_dst = SCR[:, 8704:8704 + 4 * P].bitcast(i32).rearrange("p (k n) -> p k n", n=P)
        f_S = SCR[:, 9216:9216 + 4 * WIN].rearrange("p (k n) -> p k n", n=WIN)
        f_in = [phase_sem(f"f_edges{k}") for k in range(R1)]
        f_cats, f_qs, f_U, f_add, f_relu, f_onehot, f_seg, f_acc, f_w = (
            phase_sem("f_" + n) for n in ("cat", "rhs", "inputs", "added", "relu", "onehot", "summed", "acc", "weights"))
        f_sems = [b_idx, *f_in, f_cats, f_qs, f_U, f_add, f_relu, f_onehot, f_seg, f_acc, f_w]

        def edge_sum1(block, chunk):
            ITERS = CHUNK1 // UN1

            @block.gpsimd
            def _(pool):
                gather_items(pool, UN1, ITERS, f_rows, PROJ, rows_in1, f_add)

            @block.sync
            def _(sp):
                def load(slot, n, t):
                    sp.dma_start(f_cat[WIN:P, slot, :], io["attr_t"][:, ds(t * P, P)]).then_inc(f_in[n], 16)
                    sp.dma_start(f_dst[0:WIN, slot, :], io["dst_row"][ds(t * P, P)].partition_broadcast(WIN)).then_inc(f_in[n], 16)
                for k in range(4):
                    sp.dma_start(f_rhs[WIN:P, k, :], io["L1_gnn_eW1"][2 * D:2 * D + ED, :]).then_inc(f_w, 16)
                with sp.Fori(0, ITERS) as i:
                    ts = load_regs(ENG.SP, tile_of[0:1, ds(i * UN1, UN1)], 0, ET)
                    for k in range(UN1):
                        hold(sp, f_U, i * UN1 + (k + 1))
                        load(k % 4, k % R1, ts[k])
                ts = load_regs(ENG.SP, tile_of[0:1, CHUNK1:CHUNK1 + LEAD], 0, ET)
                for k in range(LEAD):
                    sp.wait_ge(f_U, CHUNK1 + k + 1)
                    load(k % 4, k, ts[k])
                for k in range(LEAD):
                    sp.wait_ge(f_in[k], 32 * (2 * ITERS + 1))

            @block.scalar
            def _(act):
                def copy_q(slot, w):
                    nc.scalar.activation(f_rhs[0:WIN, slot:slot + 1, :], Q[:, ds(w, 1), :], ACT.Copy).then_inc(f_qs, 1)
                nc.scalar.preload_act_table(ACT.Relu)
                for k, w in enumerate(load_regs(ENG.Activation, win_of[0:1, LAG:LAG + LEAD], 0, NWIN - 1)):
                    copy_q(k, w)
                with act.Fori(0, ITERS) as i:
                    ws = load_regs(ENG.Activation, win_of[0:1, ds(i * UN1 + LAG + LEAD, UN1)], 0, NWIN - 1)
                    for k in range(UN1):
                        hold(act, f_U, i * UN1 + (k + LEAD + 1))
                        copy_q((k + LEAD) % 4, ws[k])
                        hold(act, f_add, i * UN1 + (k + 1 + R1))
                        nc.scalar.activation(f_msg[:, k % 4, :], f_msg[:, k % 4, :], ACT.Relu).then_inc(f_relu, 1)

            @block.vector
            def _(dve):
                def cat(slot, item):
                    nc.vector.tensor_scalar(f_cat[0:WIN, slot, :], f_dst[0:WIN, slot, :], aux_items[0:WIN, item], None,
                                            ALU.is_equal).then_inc(f_cats, 1)

                def accumulate(slot, w, summed):
                    hold(dve, f_seg, summed)
                    hold(dve, f_acc, summed + 1)
                    a = acc1[:, ds(w, 1), :]
                    nc.vector.tensor_tensor(a, a, BANKS[4 + slot][WIN:P, :].unsqueeze(1), ALU.add).then_inc(f_acc, 1)
                dve.sem_inc(f_add, R1)
                dve.sem_inc(f_acc, 4)
                for slot in (2, 3):
                    nc.vector.memset(f_S[:, slot, :], 0.0).then_inc(f_onehot, 1)
                    nc.vector.memset(f_msg[:, slot, :], 0.0).then_inc(f_relu, 1)
                for k in range(LEAD):
                    dve.wait_ge(f_in[k], 32)
                    cat(k, slice(k, k + 1))
                with dve.Fori(0, ITERS) as i:
                    ws = load_regs(ENG.DVE, win_of[0:1, ds(i * UN1, UN1)], 0, NWPAD - 1)
                    for k in range(UN1):
                        n = i * UN1 + k
                        hold(dve, f_seg, n + 1)
                        nc.vector.tensor_scalar(f_S[:, k % 4, :], iota[:, 0:WIN], dst_items[:, ds(n, 1)],
                                                None, ALU.is_equal).then_inc(f_onehot, 1)
                        ahead = k + LEAD
                        hold(dve, f_in[ahead % R1], i * 64 + 32 * (ahead // R1 + 1))
                        cat(ahead % 4, ds(i * UN1 + ahead, 1))
                        hold(dve, f_U, n + 5)
                        dve.wait_ge(rows_in1[k % R1], chunk * (ITERS * 32) + i * 32 + 16 * (k // R1 + 1))
                        nc.vector.tensor_tensor(f_msg[:, k % 4, :], f_rows[:, k % R1, :], BANKS[k % 4][:, :], ALU.add).then_inc(f_add, 1)
                        accumulate((k - LAG) % 4, ws[k], n + 3)
                for k, w in enumerate(load_regs(ENG.DVE, win_of[0:1, CHUNK1:CHUNK1 + LAG], 0, NWPAD - 1)):
                    accumulate((k - LAG) % 4, w, CHUNK1 + k + 3)

            @block.tensor
            def _(pe):
                pe.sem_inc(f_U, 4)
                pe.sem_inc(f_seg, 2)

                def segment(slot, n):
                    pe.wait_ge(f_onehot, n + 1)
                    pe.wait_ge(f_relu, n + 1)
                    pe.wait_ge(f_acc, n + 1)
                    nc.tensor.matmul(BANKS[4 + slot][WIN:P, :], f_S[:, slot, :], f_msg[:, slot, :], start=True, stop=True).then_inc(f_seg, 1)
                pe.wait_ge(f_w, 64)
                with pe.Fori(0, ITERS) as i:
                    for k in range(UN1):
                        n = i * UN1 + k
                        pe.wait_ge(f_in[k % R1], i * 64 + 32 * (k // R1 + 1))
                        pe.wait_ge(f_cats, n + 1)
                        pe.wait_ge(f_qs, n + 1)
                        pe.wait_ge(f_add, n + (R1 - 3))
                        nc.tensor.matmul(BANKS[k % 4][:, :], f_cat[:, k % 4, :], f_rhs[:, k % 4, :], start=True, stop=True).then_inc(f_U, 1)
                        segment((k - LAG) % 4, n)
                for k in range(LAG):
                    segment((k - LAG) % 4, CHUNK1 + k)

        with nc.Block() as block:
            item_ranges(block, WIN, CHUNK1)
        n_chunks1 = load_chunks()
        with nc.Fori(0, n_chunks1) as chunk:
            with nc.Block() as block:
                build_table(block, WIN, NWIN, CHUNK1, weights=False)
            with nc.Block() as block:
                edge_sum1(block, chunk)
            with nc.Block() as block:
                clear(block, table_sems + f_sems)

        GN = GRP * P
        HALF = GN // 2
        stage1 = BIG[0:WIN, 0:2 * GRP * DM].rearrange("p (w n) -> p w n", n=DM)
        diag = SCR[:, 9536:9536 + GN]
        AT = SCR[:, 0:4 * GN].rearrange("p (c n) -> p c n", n=GN)
        HID = AT
        GT = SCR[:, 2560:2560 + 2 * GN].rearrange("p (c n) -> p c n", n=GN)
        HT = SCR[:, 3840:3840 + 2 * GN].rearrange("p (c n) -> p c n", n=GN)
        HS = SCR[:, 5120:6400].rearrange("p (k n) -> p k n", n=D)
        eW2s = SCR[:, 6400:7424].rearrange("p (c n) -> p c n", n=D)
        nW2s = SCR[:, 7424:8448].rearrange("p (c n) -> p c n", n=D)
        eb2s, nb2s, gam, bet = (SCR[:, 8448 + k * D:8448 + (k + 1) * D] for k in range(4))
        nb1s = SCR[:, 9472:9476]
        nW1s = SCR2[:, 0:2048].rearrange("p (c n) -> p c n", n=DM)
        g_w = phase_sem("g_weights")
        (g_stage, g_T, g_hT, g_at, g_agg, g_gt, g_hid, g_relu, g_out, g_h, g_diag, g_stats, g_std, g_z, g_st) = (
            phase_sem("g_" + n) for n in ("stage", "sumsT", "rowsT", "evacuated", "agg", "agg_read", "hidden", "relu", "out", "rows",
                                    "diag", "stats", "std", "out_read", "st"))

        def rows_of(vec):
            return vec.unsqueeze(1).to_broadcast([P, GRP, D])

        def node_update1(block):
            @block.sync
            def _(sp):
                for to, name in ((eW2s, "L1_gnn_eW2"), (nW1s, "L1_gnn_nW1"), (nW2s, "L1_gnn_nW2")):
                    sp.dma_start(to, io[name].rearrange("(c p) n -> p c n", p=P)).then_inc(g_w, 16)
                for to, name in ((eb2s, "L1_gnn_eb2"), (nb2s, "L1_gnn_nb2"), (gam, "L1_gnn_ln_gamma"), (bet, "L1_gnn_ln_beta")):
                    sp.dma_start(to, io[name].partition_broadcast(P)).then_inc(g_w, 16)
                sp.dma_start(nb1s, io["nb1_col"]).then_inc(g_w, 16)

            @block.scalar
            def _(act):
                nc.scalar.preload_act_table(ACT.Sqrt)
                act.wait_ge(g_w, 128)
                with act.Fori(0, NG) as g:
                    hold(act, g_T, g + 1)
                    nc.scalar.activation(stage1, acc1[:, ds(g * 2 * GRP, 2 * GRP), :], ACT.Copy).then_inc(g_stage, 1)
                    hold(act, g_stats, 2 * g + 1)
                    nc.scalar.activation(std[:], mv[:, :, 1], ACT.Sqrt, bias=eps[:, 0:1]).then_inc(g_std, 1)
                    hold(act, g_T, g + 2)
                    hold(act, g_out, 3 * g + 1)
                    for k in range(GRP):
                        nc.scalar.activation(AT[:, :, k * P:(k + 1) * P], BANKS[k][:, :].rearrange("p (c n) -> p c n", n=P),
                                             ACT.Copy).then_inc(g_at, 1)
                    hold(act, g_hT, g + 1)
                    for q, (_, t0, n) in enumerate(O_PAIRS):
                        nc.scalar.activation(HT[:, :, t0 * P:(t0 + n) * P].rearrange("p c (k n) -> p k c n", n=P),
                                             BANKS[5 + q][:, 0:n * 256].rearrange("p (k c n) -> p k c n", k=n, c=2),
                                             ACT.Copy).then_inc(g_at, 1)
                    for n in range(4):
                        hold(act, g_agg, 4 * g + (n + 1))
                        nc.scalar.activation(GT[:, n // 2, (n % 2) * HALF:(n % 2 + 1) * HALF], BANKS[n][:, 0:HALF], ACT.Copy).then_inc(g_gt, 1)
                    for n in range(8):
                        hold(act, g_hid, 8 * g + (n + 1))
                        nc.scalar.activation(HID[:, n // 2, (n % 2) * HALF:(n % 2 + 1) * HALF], BANKS[4 + n % 4][:, 0:HALF], ACT.Relu,
                                             bias=nb1s[:, n // 2:n // 2 + 1]).then_inc(g_relu, 1)
                    hold(act, g_stats, 2 * g + 2)
                    nc.scalar.activation(std[:], mv[:, :, 1], ACT.Sqrt, bias=eps[:, 0:1]).then_inc(g_std, 1)

            @block.tensor
            def _(pe):
                pe.sem_inc(g_T, 1)
                pe.sem_inc(g_out, 1)
                pe.wait_ge(g_w, 128)
                with pe.Fori(0, NG) as g:
                    hold(pe, g_stage, g + 1)
                    hold(pe, g_z, 3 * g + 1)
                    for k in range(GRP):
                        for c in range(4):
                            for a in range(2):
                                m = nc.tensor.transpose(BANKS[k][:, c * P + a * WIN:c * P + (a + 1) * WIN],
                                                        stage1[:, 2 * k + a, c * P:(c + 1) * P], ident[0:WIN, 0:WIN])
                    m.then_inc(g_T, 1)
                    pe.wait_ge(g_h, g + 1)
                    for k in range(GRP):
                        for c in range(2):
                            m = nc.tensor.transpose(BANKS[5 + k // 2][:, (k % 2) * 256 + c * P:(k % 2) * 256 + (c + 1) * P],
                                                    HS[:, k, c * P:(c + 1) * P], ident[:])
                    m.then_inc(g_hT, 1)
                    pe.wait_ge(g_at, 8 * g + 8)
                    pe.wait_ge(g_diag, g + 1)
                    for n in range(4):
                        to = BANKS[n][:, 0:HALF]
                        cols = slice((n % 2) * HALF, (n % 2 + 1) * HALF)
                        for c in range(4):
                            nc.tensor.matmul(to, eW2s[:, c, (n // 2) * P:(n // 2 + 1) * P], AT[:, c, cols], start=c == 0, stop=False)
                        nc.tensor.matmul(to, eb2s[:, (n // 2) * P:(n // 2 + 1) * P], diag[:, cols], start=False, stop=True).then_inc(g_agg, 1)
                    pe.wait_ge(g_gt, 4 * g + 4)
                    for n in range(8):
                        pe.wait_ge(g_relu, 8 * g + (n + 1))
                        to = BANKS[4 + n % 4][:, 0:HALF]
                        cols = slice((n % 2) * HALF, (n % 2 + 1) * HALF)
                        f = slice((n // 2) * P, (n // 2 + 1) * P)
                        for c in range(4):
                            m = nc.tensor.matmul(to, nW1s[:, c, f], (HT if c < 2 else GT)[:, c % 2, cols], start=c == 0, stop=c == 3)
                        m.then_inc(g_hid, 1)
                    pe.wait_ge(g_relu, 8 * g + 8 + 4)
                    for q, (_, t0, n) in enumerate(O_PAIRS):
                        for k in range(t0, t0 + n):
                            for f in range(4):
                                m = nc.tensor.matmul(BANKS[q][:, (k - t0) * D:(k - t0 + 1) * D], HID[:, f, k * P:(k + 1) * P], nW2s[:, f, :],
                                                     start=f == 0, stop=f == 3)
                        m.then_inc(g_out, 1)

            @block.vector
            def _(dve):
                dve.sem_inc(g_z, 1)
                dve.sem_inc(g_relu, 4)
                dve.wait_ge(g_w, 128)
                with dve.Fori(0, NG) as g:
                    st = Steps(dve, g_st, g * (2 * (LN_A + LN_B) + 8))
                    nc.vector.tensor_tensor(diag.rearrange("p (k n) -> p k n", n=P),
                                            ident[:].unsqueeze(1).to_broadcast([P, GRP, P]),
                                            CNT[:, ds(g * GRP, GRP)].unsqueeze(2).to_broadcast([P, GRP, P]),
                                            ALU.mult).then_inc(g_diag, 1)
                    ln_stats(dve, st, group(X, g))
                    st.wait()
                    dve.sem_inc(g_stats, 1)
                    hold(dve, g_std, 2 * g + 1)
                    ln_apply(dve, st, group(X, g), HS)
                    st.wait()
                    dve.sem_inc(g_h, 1)
                    hold(dve, g_hT, g + 1)
                    st(nc.vector.tensor_tensor(HS, HS, rows_of(nb2s), ALU.add))
                    st.wait()
                    for q, (_, t0, n) in enumerate(O_PAIRS):
                        hold(dve, g_out, 3 * g + (q + 2))
                        st(nc.vector.tensor_tensor(HS[:, t0:t0 + n, :], HS[:, t0:t0 + n, :],
                                                   BANKS[q][:, 0:n * D].rearrange("p (k n) -> p k n", n=D), ALU.add))
                    st.wait()
                    dve.sem_inc(g_z, 3)
                    ln_stats(dve, st, HS)
                    st.wait()
                    dve.sem_inc(g_stats, 1)
                    hold(dve, g_std, 2 * g + 2)
                    ln_apply(dve, st, HS, HS)
                    st.wait()
                    st(nc.vector.tensor_tensor(HS, HS, rows_of(gam), ALU.mult))
                    st.wait()
                    st(nc.vector.tensor_tensor(HS, HS, rows_of(bet), ALU.add))
                    st.wait()
                    st(nc.vector.tensor_tensor(group(X, g), group(X, g), HS, ALU.add))
                    st.wait()
                    st(nc.vector.memset(std[:, 0:1], 0.0))
                    st.wait()

        with nc.Block() as block:
            node_update1(block)

        end_phase()

        XN = BIG[:, 0:NT * D].rearrange("p (t n) -> p t n", n=D)
        W1s = BIG[:, 6400:6400 + E * 2 * H1].rearrange("p (e c h) -> p e c h", e=E, c=2)
        W2s = BIG[:, 14592:14592 + E * 4 * D].rearrange("p (e f n) -> p e f n", e=E, f=4)
        b2r = BIG[:, 22784:22784 + E * D].rearrange("p (e n) -> p e n", e=E)
        b1r = SCR[:, 6144:6144 + E * H1].rearrange("p (e h) -> p e h", e=E)
        pre_r, z_rows, xt4 = ring4(0), ring4(1024), ring4(2048)
        gam1, bet1 = SCR[:, 5120:5376], SCR[:, 5376:5632]
        Wrs = SCR[:, 5632:5648].rearrange("p (c e) -> p c e", c=2)
        brs = SCR[:, 5648:5656]
        stats2 = SCR[:, 5664:5688].rearrange("p (s n) -> p s n", n=6)
        mv2 = SCR[:, 5696:5704].rearrange("p (s n) -> p s n", n=2)
        std2, rstd2 = SCR[:, 5712:5716], SCR[:, 5720:5724]
        tile_expert = sb("tile_expert", [1, T1], i32)
        (h_w, h_big, h_T, h_xt, h_stats, h_std, h_stats2, h_std2, h_x, h_pre, h_y, h_z, h_L, h_lg, h_copied) = (
            phase_sem("h_" + n) for n in ("weights", "expert_weights", "transposed", "xt", "stats", "std", "stats2", "std2", "first_steps",
                                          "normed", "second_steps", "rows", "logits", "logits_read", "copied"))
        h_g, h_rstd, h_rstd2, h_pre2 = (phase_sem("h_" + n) for n in ("gamma", "rstd", "rstd2", "normed2"))

        def router1(block):
            @block.sync
            def _(sp):
                sp.dma_start(gam1, io["L1_ffn_gamma"].partition_broadcast(P)).then_inc(h_w, 16)
                sp.dma_start(bet1, io["L1_ffn_beta"].partition_broadcast(P)).then_inc(h_w, 16)
                sp.dma_start(Wrs, io["L1_ffn_Wr"].rearrange("(c p) e -> p c e", p=P)).then_inc(h_w, 16)
                sp.dma_start(brs, io["L1_ffn_br"].partition_broadcast(P)).then_inc(h_w, 16)
                for e in range(E):
                    sp.dma_start(W1s[:, e, :, :], io["L1_ffn_W1"][e, :, :].rearrange("(c p) h -> p c h", p=P)).then_inc(h_big, 16)
                    sp.dma_start(W2s[:, e, :, :], io["L1_ffn_W2"][e, :, :].rearrange("(f p) n -> p f n", p=P)).then_inc(h_big, 16)
                sp.dma_start(b1r, io["L1_ffn_b1"].rearrange("e h -> (e h)").partition_broadcast(P).rearrange("p (e h) -> p e h", e=E)).then_inc(h_big, 16)
                sp.dma_start(b2r, io["L1_ffn_b2"].rearrange("e h -> (e h)").partition_broadcast(P).rearrange("p (e h) -> p e h", e=E)).then_inc(h_big, 16)

            @block.scalar
            def _(act):
                act.sem_inc(h_xt, 2)
                act.sem_inc(h_copied, 4)
                nc.scalar.preload_act_table(ACT.Sqrt)

                def deviation(n, slot, use):
                    hold(act, h_stats, n + 1)
                    tile_std(slot).then_inc(h_std, 1)

                def deviation2(n, slot, use):
                    hold(act, h_stats2, n + 1)
                    nc.scalar.activation(std2[:, slot:slot + 1], mv2[:, slot, 1:2], ACT.Sqrt, bias=eps[:, 0:1]).then_inc(h_std2, 1)

                def copy_rows(n, slot, use):
                    hold(act, h_z, n + 1)
                    nc.scalar.activation(XN[:, ds(n, 1), :], z_rows[:, slot:slot + 1, :], ACT.Copy).then_inc(h_copied, 1)

                def read_rows(n, slot, use):
                    hold(act, h_T, n + 5)
                    hold(act, h_L, n + 1)
                    nc.scalar.activation(xt4[:, slot, :], BANKS[slot % 2][:, 0:D], ACT.Copy).then_inc(h_xt, 1)
                walk_tiles(act, (read_rows, 1), (copy_rows, 1), (deviation, 5), (deviation2, 3))

            @block.tensor
            def _(pe):
                pe.sem_inc(h_T, 4)
                pe.sem_inc(h_L, 4)
                pe.wait_ge(h_w, 64)

                def turn_rows(n, slot, use):
                    pe.wait_ge(h_z, n + 1)
                    pe.wait_ge(h_xt, n + 1)
                    pe_transpose(slot % 2, z_rows[:, slot, :]).then_inc(h_T, 1)

                def logits(n, slot, use):
                    pe.wait_ge(h_xt, n + 3)
                    pe.wait_ge(h_lg, n + 1)
                    for c in range(2):
                        m = nc.tensor.matmul(BANKS[2 + slot % 2][:, 0:E], halves(xt4[:, slot, :])[:, c, :], Wrs[:, c, :], start=c == 0, stop=c == 1)
                    m.then_inc(h_L, 1)
                walk_tiles(pe, (turn_rows, 1), (logits, 0))

            @block.vector
            def _(dve):
                dve.sem_inc(h_lg, 2)
                dve.wait_ge(h_w, 64)

                def stats_first(n, slot, use):
                    nc.vector.bn_stats(stats[:, slot, :], X[:, ds(n, 1), :].rearrange("p o n -> p (o n)")).then_inc(h_x, 1)

                def aggregate_first(n, slot, use):
                    hold(dve, h_x, n + 1)
                    nc.vector.bn_aggr(mv[:, slot, :], stats[:, slot, :]).then_inc(h_stats, 1)

                def invert_first(n, slot, use):
                    hold(dve, h_std, n + 1)
                    nc.vector.reciprocal(rstd[:, slot:slot + 1], std[:, slot:slot + 1]).then_inc(h_rstd, 1)

                def norm_first(n, slot, use):
                    hold(dve, h_rstd, n + 1)
                    hold(dve, h_g, n + 1)
                    nc.vector.tensor_scalar(pre_r[:, slot:slot + 1, :], X[:, ds(n, 1), :], mv[:, slot, 0:1], rstd[:, slot:slot + 1],
                                            ALU.subtract, ALU.mult).then_inc(h_pre, 1)

                def stats_second(n, slot, use):
                    hold(dve, h_pre, n + 1)
                    nc.vector.bn_stats(stats2[:, slot, :], pre_r[:, slot, :]).then_inc(h_y, 1)

                def aggregate_second(n, slot, use):
                    hold(dve, h_y, n + 1)
                    nc.vector.bn_aggr(mv2[:, slot, :], stats2[:, slot, :]).then_inc(h_stats2, 1)

                def invert_second(n, slot, use):
                    hold(dve, h_std2, n + 1)
                    nc.vector.reciprocal(rstd2[:, slot:slot + 1], std2[:, slot:slot + 1]).then_inc(h_rstd2, 1)

                def norm_second(n, slot, use):
                    hold(dve, h_rstd2, n + 1)
                    nc.vector.tensor_scalar(pre_r[:, slot, :], pre_r[:, slot, :], mv2[:, slot, 0:1], rstd2[:, slot:slot + 1],
                                            ALU.subtract, ALU.mult).then_inc(h_pre2, 1)

                def read_logits(n, slot, use):
                    hold(dve, h_L, n + 5)
                    nc.vector.tensor_tensor(LG[:, ds(n, 1), :], BANKS[2 + slot % 2][:, 0:E].unsqueeze(1), brs.unsqueeze(1),
                                            ALU.add).then_inc(h_lg, 1)
                walk_tiles(dve, (stats_first, 5), (invert_second, 2), (invert_first, 4), (aggregate_first, 5), (norm_second, 2),
                           (norm_first, 4), (stats_second, 3), (aggregate_second, 3), (read_logits, 0))

            @block.gpsimd
            def _(pool):
                pool.sem_inc(h_g, 4)

                def affine(n, slot, use):
                    hold(pool, h_pre2, n + 1)
                    hold(pool, h_T, n + 1)
                    hold(pool, h_copied, n + 1)
                    nc.gpsimd.tensor_tensor(z_rows[:, slot, :], pre_r[:, slot, :], gam1, ALU.mult).then_inc(h_g, 1)
                    hold(pool, h_g, n + 5)
                    nc.gpsimd.tensor_tensor(z_rows[:, slot, :], z_rows[:, slot, :], bet1, ALU.add).then_inc(h_z, 1)
                walk_tiles(pool, (affine, 2))

        with nc.Block() as block:
            router1(block)

        q_st, q_ready, q_sum, q_exp = (phase_sem("q_" + n) for n in ("st", "ready", "summed", "exp"))
        q_done = sem("q_scattered")
        used_tiles = SCR[:, 0:E]
        tiles_i = SCR[:, 8:8 + E].bitcast(i32)
        tiles_f, tiles_end, first_slot = (SCR[:, 16 + 8 * k:24 + 8 * k] for k in range(3))
        past = SCR[0:1, 64:64 + T1 * E].rearrange("p (t e) -> p t e", e=E)
        te_f = SCR[0:1, 640:640 + T1]
        valid = r_c

        def route1(block):
            @block.vector
            def _(dve):
                st = Steps(dve, q_st)
                first_best(st, LG, r_a, OH1, r_b)
                st(nc.vector.scalar_tensor_tensor(LG[:], OH1[:], -3e38, LG[:], ALU.mult, ALU.add))
                st.wait()
                first_best(st, LG, r_c, OH2, r_b)
                st(nc.vector.tensor_tensor(keep2[:], r_c[:], r_a[:], ALU.subtract))
                st.wait()
                dve.sem_inc(q_exp, 1)
                st(nc.vector.tensor_scalar(valid[:], NIDT[:], float(NODES), None, ALU.is_lt))
                st.wait()
                st(nc.vector.tensor_tensor(OH1[:], OH1[:], bce(valid), ALU.mult))
                st(nc.vector.tensor_tensor(OH2[:], OH2[:], bce(valid), ALU.mult))
                st.wait()
                st(nc.vector.tensor_tensor(LG[:], OH1[:], OH2[:], ALU.add))
                ranks(dve, st, LG, q_ready, q_sum, 1)
                members = CUM[:, NT - 1, :]
                st(nc.vector.tensor_scalar(tiles_i, members, float(P - 1), None, ALU.add))
                st.wait()
                st(nc.vector.tensor_scalar(tiles_i, tiles_i, P.bit_length() - 1, None, ALU.arith_shift_right))
                st.wait()
                st(nc.vector.tensor_copy(tiles_f, tiles_i))
                st.wait()
                st(nc.vector.tensor_tensor_scan(tiles_end, ones[:, 0:E], tiles_f, 0.0, ALU.mult, ALU.add))
                st.wait()
                st(nc.vector.tensor_tensor(first_slot, tiles_end, tiles_f, ALU.subtract))
                st(nc.vector.tensor_tensor(past, iota[0:1, 0:T1].unsqueeze(2).to_broadcast([1, T1, E]),
                                           tiles_end[0:1, :].unsqueeze(1).to_broadcast([1, T1, E]), ALU.is_ge))
                st.wait()
                st(nc.vector.tensor_scalar(first_slot, first_slot, float(P), -1.0, ALU.mult, ALU.add))
                st(nc.vector.tensor_reduce(te_f, past, AX.X, ALU.add))
                st.wait()
                st(nc.vector.tensor_scalar(tile_expert[:], te_f, float(E - 1), None, ALU.min))
                st(nc.vector.tensor_tensor(RT[:], RT[:], bct(first_slot), ALU.add))
                st.wait()
                for a, (oh, to, frm) in enumerate(((OH1, to1, from1), (OH2, to2, from2))):
                    st(nc.vector.tensor_tensor(CUM[:], RT[:], oh[:], ALU.mult))
                    st.wait()
                    st(nc.vector.tensor_reduce(r_a[:], CUM[:], AX.X, ALU.add))
                    st.wait()
                    st(nc.vector.tensor_copy(frm[:], r_a[:]))
                    st(nc.vector.tensor_scalar(r_b[:], NIDT[:], float(TRASH1 + a * NPAD), None, ALU.add))
                    st.wait()
                    st(nc.vector.tensor_tensor(r_a[:], r_a[:], r_b[:], ALU.subtract))
                    st.wait()
                    st(nc.vector.tensor_tensor(r_a[:], r_a[:], valid[:], ALU.mult))
                    st.wait()
                    st(nc.vector.tensor_tensor(r_a[:], r_a[:], r_b[:], ALU.add))
                    st.wait()
                    st(nc.vector.tensor_copy(to[:], r_a[:]))
                    st.wait()
                dve.sem_inc(q_ready, 1)
                dve.wait_ge(q_exp, 2)
                st(nc.vector.tensor_scalar(keep1[:], keep2[:], 1.0, None, ALU.add))
                st.wait()
                st(nc.vector.reciprocal(keep1[:], keep1[:]))
                st.wait()
                st(nc.vector.tensor_tensor(keep2[:], keep2[:], keep1[:], ALU.mult))

            @block.scalar
            def _(act):
                act.wait_ge(q_exp, 1)
                nc.scalar.activation(keep2[:], keep2[:], ACT.Exp).then_inc(q_exp, 1)

            @block.tensor
            def _(pe):
                pe_ranks(pe, LG, q_ready, q_sum, 1)

            @block.gpsimd
            def _(pool):
                pool.wait_ge(q_ready, 2)
                for to in (to1, to2):
                    for t in range(NT):
                        nc.gpsimd.indirect_dma_start(
                            out=BUF1, out_offset=bass.IndirectOffsetOnAxis(ap=to[:, t:t + 1].bitcast(u32), axis=0),
                            in_=XN[:, t, :], in_offset=None).then_inc(q_done, 16)
                pool.wait_ge(q_done, 32 * NT)
                pool.wait_ge(h_big, 16 * (2 * E + 2))

        with nc.Block() as block:
            route1(block)

        end_phase()

        i_rows = [BIG[:, k * D:(k + 1) * D] for k in range(4)]
        i_xT = [BIG[:, 1024 + k * D:1024 + (k + 1) * D].rearrange("p (c n) -> p c n", c=2) for k in range(4)]
        i_h = [BIG[:, 2048 + k * H1:2048 + (k + 1) * H1] for k in range(4)]
        i_hT = [BIG[:, 4096 + k * H1:4096 + (k + 1) * H1].rearrange("p (f n) -> p f n", n=P) for k in range(2)]
        i_y = [BIG[:, 5120 + k * D:5120 + (k + 1) * D] for k in range(4)]
        i_in, i_out = [phase_sem(f"i_in{k}") for k in range(8)], sems("i_out", 4)
        i_T, i_x, i_m1, i_b1, i_gelu, i_Th, i_hTs, i_m2, i_ys, i_stored = (
            phase_sem("i_" + n) for n in ("rowsT", "xT", "hidden", "biased", "gelu", "hiddenT", "hT", "out", "y", "stored"))
        UT = 8

        def experts1(block):
            @block.sync
            def _(sp):
                with sp.Fori(0, T1 // UT) as i:
                    for k in range(UT):
                        n = i * UT + k
                        hold(sp, i_T, n + 1)
                        sp.dma_start(i_rows[k % 4], BUF1[ds(n * P, P), :]).then_inc(i_in[k], 16)

            @block.tensor
            def _(pe):
                pe.sem_inc(i_T, 4)
                pe.sem_inc(i_m2, 2)
                with pe.Fori(0, T1 // UT) as i:
                    es = load_regs(ENG.PE, tile_expert[0:1, ds(i * UT, UT)], 0, E - 1)

                    def first(k):
                        n = i * UT + k
                        pe.wait_ge(i_in[k], i * 16 + 16)
                        pe.wait_ge(i_x, n + 1)
                        for c in range(2):
                            m = nc.tensor.transpose(BANKS[0][:, c * P:(c + 1) * P], i_rows[k % 4][:, c * P:(c + 1) * P], ident[:])
                        m.then_inc(i_T, 1)
                        pe.wait_ge(i_x, n + 2)
                        pe.wait_ge(i_b1, n + 1)
                        for c in range(2):
                            m = nc.tensor.matmul(BANKS[1 + k % 2][:, 0:H1], i_xT[k % 4][:, c, :],
                                                 W1s[:, ds(es[k], 1), c, :].rearrange("p e h -> p (e h)"), start=c == 0, stop=c == 1)
                        m.then_inc(i_m1, 1)

                    def turn(k):
                        n = i * UT + k
                        pe.wait_ge(i_gelu, n + 1)
                        pe.wait_ge(i_hTs, n + 1)
                        for f in range(4):
                            m = nc.tensor.transpose(BANKS[3 + k % 2][:, f * P:(f + 1) * P], i_h[k % 4][:, f * P:(f + 1) * P], ident[:])
                        m.then_inc(i_Th, 1)

                    def second(k):
                        n = i * UT + k
                        pe.wait_ge(i_hTs, n + 3)
                        pe.wait_ge(i_ys, n + 1)
                        for f in range(4):
                            m = nc.tensor.matmul(BANKS[5 + k % 2][:, 0:D], i_hT[k % 2][:, f, :],
                                                 W2s[:, ds(es[k], 1), f, :].rearrange("p e n -> p (e n)"), start=f == 0, stop=f == 3)
                        m.then_inc(i_m2, 1)
                    first(0)
                    for k in range(UT):
                        if k + 1 < UT:
                            first(k + 1)
                        turn(k)
                        if k:
                            second(k - 1)
                    second(UT - 1)

            @block.scalar
            def _(act):
                act.sem_inc(i_x, 1)
                nc.scalar.preload_act_table(ACT.Gelu)
                with act.Fori(0, T1 // UT) as i:
                    def rows(k):
                        hold(act, i_T, i * UT + (k + 5))
                        nc.scalar.activation(i_xT[k % 4].rearrange("p c n -> p (c n)"), BANKS[0][:, 0:D], ACT.Copy).then_inc(i_x, 1)
                    rows(0)
                    for k in range(UT):
                        if k + 1 < UT:
                            rows(k + 1)
                        hold(act, i_b1, i * UT + (k + 3))
                        nc.scalar.activation(i_h[k % 4], i_h[k % 4], ACT.Gelu).then_inc(i_gelu, 1)

            @block.vector
            def _(dve):
                dve.sem_inc(i_b1, 2)
                dve.sem_inc(i_hTs, 2)
                dve.sem_inc(i_ys, 2)
                with dve.Fori(0, T1 // UT) as i:
                    es = load_regs(ENG.DVE, tile_expert[0:1, ds(i * UT, UT)], 0, E - 1)

                    def bias(k):
                        n = i * UT + k
                        hold(dve, i_m1, n + 1)
                        if k % 4 == 0:
                            pass
                        nc.vector.tensor_tensor(i_h[k % 4].unsqueeze(1), BANKS[1 + k % 2][:, 0:H1].unsqueeze(1), b1r[:, ds(es[k], 1), :],
                                                ALU.add).then_inc(i_b1, 1)

                    def turn(k):
                        n = i * UT + k
                        hold(dve, i_Th, n + 1)
                        hold(dve, i_m2, n + 1)
                        nc.vector.tensor_copy(i_hT[k % 2].rearrange("p f n -> p (f n)"), BANKS[3 + k % 2][:, :]).then_inc(i_hTs, 1)

                    def finish(k):
                        n = i * UT + k
                        hold(dve, i_m2, n + 3)
                        hold(dve, i_stored, n + 1)
                        nc.vector.tensor_tensor(i_y[k % 4].unsqueeze(1), BANKS[5 + k % 2][:, 0:D].unsqueeze(1), b2r[:, ds(es[k], 1), :],
                                                ALU.add).then_inc(i_ys, 1)
                    bias(0)
                    for k in range(UT):
                        if k + 1 < UT:
                            bias(k + 1)
                        turn(k)
                        if k:
                            finish(k - 1)
                    finish(UT - 1)

            @block.gpsimd
            def _(pool):
                pool.sem_inc(i_stored, 4)
                with pool.Fori(0, T1 // UT) as i:
                    for k in range(UT):
                        n = i * UT + k
                        hold(pool, i_ys, n + 3)
                        nc.gpsimd.dma_start(Y1[ds(n * P, P), :], i_y[k % 4]).then_inc(i_out[k % 4], 16)
                        hold(pool, i_out[k % 4], i * 32 + (16 if k < 4 else 32))
                        pool.sem_inc(i_stored, 1)

        with nc.Block() as block:
            experts1(block)

        j_rows = [ring4(a * 4 * D) for a in range(2)]
        j_idx = sb("j_idx", [P, 2, 4], i32)
        j_in = [sems(f"j_in{a}_", 4) for a in range(2)]
        j_cp, j_half, j_x, j_out = (sem("j_" + n) for n in ("index", "first_added", "added", "out"))

        def combine(block):
            @block.gpsimd
            def _(pool):
                pool.sem_inc(j_x, 4)

                def gather(n, slot, use):
                    hold(pool, j_x, n + 1)
                    for a, at in enumerate((from1, from2)):
                        nc.gpsimd.tensor_copy(j_idx[:, a, slot:slot + 1], at[:, ds(n, 1)]).then_inc(j_cp, 1)
                    hold(pool, j_cp, 2 * n + 2)
                    for a in range(2):
                        nc.gpsimd.indirect_dma_start(
                            out=j_rows[a][:, slot, :], out_offset=None, in_=Y1,
                            in_offset=bass.IndirectOffsetOnAxis(ap=j_idx[:, a, slot:slot + 1].bitcast(u32), axis=0)).then_inc(j_in[a][slot], 16)
                walk_tiles(pool, (gather, 4))

            @block.vector
            def _(dve):
                def first_row(n, slot, use):
                    hold(dve, j_in[0][slot], 16 * (use + 1))
                    x = X[:, ds(n, 1), :]
                    nc.vector.scalar_tensor_tensor(x, j_rows[0][:, slot:slot + 1, :], keep1[:, ds(n, 1)], x, ALU.mult, ALU.add).then_inc(j_half, 1)

                def second_row(n, slot, use):
                    hold(dve, j_in[1][slot], 16 * (use + 1))
                    hold(dve, j_half, n + 1)
                    x = X[:, ds(n, 1), :]
                    nc.vector.scalar_tensor_tensor(x, j_rows[1][:, slot:slot + 1, :], keep2[:, ds(n, 1)], x, ALU.mult, ALU.add).then_inc(j_x, 1)
                walk_tiles(dve, (first_row, 1), (second_row, 0))

            @block.sync
            def _(sp):
                with sp.Fori(0, NT - 1) as n:
                    hold(sp, j_x, n + 5)
                    sp.dma_start(out[ds(n * P, P), :], X[:, ds(n, 1), :].rearrange("p o n -> p (o n)")).then_inc(j_out, 16)
                sp.wait_ge(j_x, NT + 4)
                sp.dma_start(out[(NT - 1) * P:NODES, :], X[0:TAIL, NT - 1, :]).then_inc(j_out, 16)
                sp.wait_ge(j_out, 16 * NT)

        with nc.Block() as block:
            combine(block)


WEIGHTS = ["L0_gnn_weight", "L0_ffn_gate_w", "L0_ffn_gate_b", "L0_ffn_w1", "L0_ffn_b1", "L0_ffn_w2", "L0_ffn_b2",
           "L1_gnn_eW1", "L1_gnn_eb1", "L1_gnn_eW2", "L1_gnn_eb2", "L1_gnn_nW1", "L1_gnn_nb1", "L1_gnn_nW2",
           "L1_gnn_nb2", "L1_gnn_ln_gamma", "L1_gnn_ln_beta", "L1_ffn_gamma", "L1_ffn_beta", "L1_ffn_Wr", "L1_ffn_br",
           "L1_ffn_W1", "L1_ffn_b1", "L1_ffn_W2", "L1_ffn_b2"]


def kernel(**inputs):
    import numpy as np
    import concourse.bacc as bacc
    from concourse.bass_utils import run_bass_kernel_spmd

    pad = EROW - EDGES
    src = np.concatenate([np.asarray(inputs["src"]), np.zeros(pad, np.int32)])
    dst = np.concatenate([np.asarray(inputs["dst"]), np.full(pad, NODES, np.int32)])
    w = np.concatenate([np.asarray(inputs["edge_weight"]), np.zeros(pad, np.float32)])
    attr = np.concatenate([np.asarray(inputs["edge_attr_64"]), np.zeros((pad, ED), np.float32)])
    arrays = {
        "x": np.asarray(inputs["x"]),
        "src_tiles": src[:ET * P].reshape(ETP, ETQ * P),
        "dst_tiles": dst[:ET * P].reshape(ETP, ETQ * P),
        "w_tiles": w[:ET * P].reshape(ETP, ETQ * P),
        "dst_row": dst,
        "attr_t": attr.T,
        "nb1_col": np.asarray(inputs["L1_gnn_nb1"]).reshape(DM // P, P).T,
        "b1_col": np.asarray(inputs["L0_ffn_b1"]).reshape(E * F0 // P, P).T,
    }
    for name in WEIGHTS:
        arrays[name] = np.asarray(inputs[name])
    arrays = {n: np.ascontiguousarray(a) for n, a in arrays.items()}
    nc = bacc.Bacc("TRN2", target_bir_lowering=False, num_devices=1)
    io = {n: nc.dram_tensor(f"in_{n}", a.shape, mybir.dt.from_np(a.dtype), kind="ExternalInput").ap()
          for n, a in arrays.items()}
    out = nc.dram_tensor("out_x", (NODES, D), f32, kind="ExternalOutput").ap()
    build(nc, io, out)
    r = run_bass_kernel_spmd(nc, [{f"in_{n}": a for n, a in arrays.items()}], core_ids=[0])
    return r.results[0]["out_x"]
```

```python
from contextlib import ExitStack

import concourse.bass as bass
from concourse import mybir

f32, i32, u32 = mybir.dt.float32, mybir.dt.int32, mybir.dt.uint32
ALU, ACT, AX = mybir.AluOpType, mybir.ActivationFunctionType, mybir.AxisListType
ENG = mybir.EngineType
ds = bass.ds

P = 128
NODES, D = 3125, 256
NT = -(-NODES // P)
NPAD = NT * P
TAIL = NODES - (NT - 1) * P
GRP = 5
NG = NT // GRP
WIN0, NWIN0 = P, NT
WIN = 64
NWIN = -(-NODES // WIN)
NWPAD = 2 * NT
EDGES = 53125
ET = -(-EDGES // P)
ETP, ETQ = 104, 4
EROW = (ET + 1) * P
CHUNK0 = ET + NWIN0 - 1
UN0 = 20
CHUNK1 = ET + NWIN - 1
UN1 = 16
LEAD, LAG = 3, 2
TABLE = CHUNK1 + UN1
MAXCHUNKS = -(-ET * NWIN // CHUNK1)
DM = 512
ED = 64
E = 8
CAP = -(-5 * NODES // (4 * E))
ESLOT = 512
F0 = 1024
TRASH0 = E * ESLOT
H1 = 512
T1 = (2 * NODES - E) // P + E
TRASH1 = T1 * P
BIGW = NWPAD * DM
EPS = 1e-5
assert ETP * ETQ == ET and CHUNK0 % UN0 == 0 and CHUNK1 % UN1 == 0 and TABLE >= CHUNK0 + UN0 and NT % GRP == 0 and ESLOT >= CAP


class Steps:

    def __init__(self, eng, sem, start=0):
        self.eng, self.sem, self.start, self.n = eng, sem, start, 0

    def __call__(self, instruction):
        instruction.then_inc(self.sem, 1)
        self.n += 1
        return instruction

    def wait(self):
        hold(self.eng, self.sem, self.start + self.n)


def hold(eng, sem, value):
    eng.wait_ge(sem, value)
    eng.nop(nofuse=True)


def build(nc, io, out):
    ctx = ExitStack()
    with ctx:
        sb = lambda name, shape, dt=f32: ctx.enter_context(nc.sbuf_tensor(name, shape, dt))
        sem = lambda name: ctx.enter_context(nc.semaphore(name))
        sems = lambda name, n: [sem(f"{name}{k}") for k in range(n)]
        of_phase = []

        def phase_sem(name):
            of_phase.append(nc.alloc_semaphore(name=name))
            return of_phase[-1]
        dram = lambda name, shape, dt=f32: nc.dram_tensor(name, shape, dt).ap()

        def load_regs(eng, ap, lo, hi):
            return nc.values_load_multi_w_load_instructions(
                ap, engines=[eng], min_val=lo, max_val=hi,
                skip_runtime_bounds_check_because="the table is built in range")[1]

        H0 = dram("h0_rows", (NPAD, D))
        BUF0 = dram("expert_in0", (TRASH0 + NPAD, D))
        Y0 = dram("expert_out0", (TRASH0, D))
        PROJ = dram("src_proj", (NPAD, DM))
        BUF1 = dram("expert_in1", (TRASH1 + 2 * NPAD, D))
        Y1 = dram("expert_out1", (TRASH1, D))

        ident = sb("ident", [P, P])
        before = sb("before", [P, P])
        upto = sb("upto", [P, P])
        ones = sb("ones", [P, P])
        zeros = sb("zeros", [P, 1024])
        iota = sb("iota", [P, TABLE])
        part = sb("part", [P, 1])
        X = sb("X", [P, NT, D])
        lo_dst, hi_dst = (sb(n, [ETP, ETQ], i32) for n in ("lo_dst", "hi_dst"))
        lo_win, hi_win = (sb(n, [ETP, ETQ], i32) for n in ("lo_win", "hi_win"))
        lo_f, n_f, incl, one4 = (sb(n, [ETP, ETQ]) for n in ("lo_f", "n_f", "incl", "one4"))
        ends, starts, first, tile_id = (sb(n, [ETP, ETQ]) for n in ("ends", "starts", "first", "tile_id"))
        chunk_hit = sb("chunk_hit", [1, MAXCHUNKS])
        chunks_f, chunks_i = sb("chunks_f", [1, 1]), sb("chunks_i", [1, 1], i32)
        tile_of = sb("tile_of", [1, TABLE], i32)
        win_of = sb("win_of", [1, LAG + TABLE], i32)
        src_items = sb("src_items", [P, TABLE], i32)
        dst_items = sb("dst_items", [P, TABLE])
        aux_items = sb("aux_items", [P, TABLE])
        CNT = sb("CNT", [P, NT])
        idx = sb("idx", [P, UN0], i32)
        BIG = sb("BIG", [P, BIGW])
        SCR = sb("SCR", [P, 10240])
        stats = sb("stats", [P, GRP, 6])
        mv = sb("mv", [P, GRP, 2])
        std = sb("std", [P, GRP])
        rstd = sb("rstd", [P, GRP])
        eps = sb("eps", [P, 1])
        scaled_ones = sb("scaled_ones", [1, 3, P])
        ones_of = lambda v: scaled_ones[0:1, (-WIN0, WIN, -WIN).index(v), :]
        SCR2 = sb("SCR2", [P, 2560])
        NIDT = sb("NIDT", [P, NT])
        expert8 = sb("expert8", [P, E])
        LG, OH1, OH2, RT, CUM = (SCR2[:, k * NT * E:(k + 1) * NT * E].rearrange("p (t e) -> p t e", e=E) for k in range(5))
        r_a, r_b, r_c, keep1, keep2 = (sb(n, [P, NT]) for n in ("r_a", "r_b", "r_c", "keep1", "keep2"))
        to1, to2, from1, from2 = (sb(n, [P, NT], i32) for n in ("to1", "to2", "from1", "from2"))
        weights_in = sem("weights_in")
        W0s = SCR2[:, 1024:1536].rearrange("p (c n) -> p c n", c=2)
        gate_ws = SCR2[:, 1536:1552].rearrange("p (c n) -> p c n", c=2)
        gate_bs = SCR2[:, 1552:1560]

        BANKS = [ctx.enter_context(nc.psum_tensor(f"bank{k}", [P, 512], f32)) for k in range(8)]

        acc0 = BIG[:, 0:NT * 257].rearrange("p (w n) -> p w n", n=257)
        HN = BIG[:, BIGW - NT * D:].rearrange("p (t d) -> p t d", d=D)
        zero_fill = sem("zero_fill")

        def ln_stats(dve, st, tiles):
            for k in range(GRP):
                st(nc.vector.bn_stats(stats[:, k, :], tiles[:, k, :]))
            st.wait()
            for k in range(GRP):
                st(nc.vector.bn_aggr(mv[:, k, :], stats[:, k, :]))

        def ln_apply(dve, st, tiles, to):
            st(nc.vector.reciprocal(rstd[:], std[:]))
            st.wait()
            for k in range(GRP):
                st(nc.vector.tensor_scalar(to[:, k, :], tiles[:, k, :], mv[:, k, 0:1], rstd[:, k:k + 1],
                                           ALU.subtract, ALU.mult))

        LN_A, LN_B = 2 * GRP, 1 + GRP

        def end_phase():
            with nc.Block() as block:
                clear(block, of_phase)
            for s in of_phase:
                nc.release_semaphore(s)
            of_phase.clear()

        def clear(block, which):
            @block.gpsimd
            def _(pool):
                for s in which:
                    pool.sem_clear(s)

        n_pe, n_st = sem("n_sums"), sem("n_st")

        def ranges_dve(dve, win, chunk):
            st = Steps(dve, n_st)
            shift = win.bit_length() - 1
            st(nc.vector.tensor_scalar(lo_win[:], lo_dst[:], shift, None, ALU.arith_shift_right))
            st(nc.vector.tensor_scalar(hi_win[:], hi_dst[:], shift, None, ALU.arith_shift_right))
            st.wait()
            st(nc.vector.tensor_copy(lo_f[:], lo_win[:]))
            st.wait()
            st(nc.vector.scalar_tensor_tensor(n_f[:], hi_win[:], 1.0, lo_f[:], ALU.add, ALU.subtract))
            st.wait()
            st(nc.vector.tensor_tensor_scan(incl[:], one4[:], n_f[:], 0.0, ALU.mult, ALU.add))
            st.wait()
            dve.sem_inc(n_pe, 1)
            dve.wait_ge(n_pe, 2)
            st(nc.vector.tensor_scalar(ends[:], incl[:], BANKS[0][0:ETP, 0:1], None, ALU.add))
            st(nc.vector.tensor_scalar(chunk_hit[:], iota[0:1, 0:MAXCHUNKS], float(chunk), BANKS[1][0:1, 0:1], ALU.mult, ALU.is_lt))
            st.wait()
            st(nc.vector.tensor_tensor(starts[:], ends[:], n_f[:], ALU.subtract))
            st(nc.vector.tensor_reduce(chunks_f[:], chunk_hit[:], AX.X, ALU.add))
            st.wait()
            st(nc.vector.tensor_tensor(first[:], lo_f[:], starts[:], ALU.subtract))
            st(nc.vector.tensor_copy(chunks_i[:], chunks_f[:]))

        def ranges_pe(pe):
            pe.wait_ge(n_pe, 1)
            nc.tensor.matmul(BANKS[0][0:ETP, 0:1], before[0:ETP, 0:ETP], incl[:, ETQ - 1:ETQ], start=True, stop=True)
            nc.tensor.matmul(BANKS[1][0:1, 0:1], ones[0:ETP, 0:1], incl[:, ETQ - 1:ETQ], start=True, stop=True).then_inc(n_pe, 1)

        x_in = [phase_sem(f"x_in{g}") for g in range(NG)]
        e_in, a_ready, a_stats, a_std, a_hn, a_st, a_const, a_mm = (
            phase_sem(n) for n in ("e_in", "a_tail", "a_stats", "a_std", "a_hn", "a_st", "a_const", "a_dst_range"))
        h0_out = phase_sem("h0_out")
        dt_i = SCR[0:ETP, 0:ETQ * P].bitcast(i32).rearrange("p (q e) -> p q e", q=ETQ)
        with nc.Block() as block:
            @block.sync
            def _(sp):
                sp.wait_ge(a_ready, 1)
                for g in range(NG - 1):
                    sp.dma_start(X[:, g * GRP:(g + 1) * GRP, :],
                                 io["x"][g * GRP * P:(g + 1) * GRP * P, :].rearrange("(t p) d -> p t d", p=P)).then_inc(x_in[g], 16)
                g = NG - 1
                sp.dma_start(X[:, g * GRP:NT - 1, :],
                             io["x"][g * GRP * P:(NT - 1) * P, :].rearrange("(t p) d -> p t d", p=P)).then_inc(x_in[g], 16)
                sp.dma_start(X[0:TAIL, NT - 1, :], io["x"][(NT - 1) * P:NODES, :]).then_inc(x_in[g], 16)
                sp.dma_start(W0s, io["L0_gnn_weight"].rearrange("(c p) n -> p c n", p=P)).then_inc(weights_in, 16)
                sp.dma_start(gate_ws, io["L0_ffn_gate_w"].rearrange("(c p) n -> p c n", p=P)).then_inc(weights_in, 16)
                sp.dma_start(gate_bs, io["L0_ffn_gate_b"].partition_broadcast(P)).then_inc(weights_in, 16)
                with sp.Fori(0, NG) as g:
                    sp.wait_ge(a_hn, g + 1)
                    sp.dma_start(H0.rearrange("(t p) d -> p t d", p=P)[:, ds(g * GRP, GRP), :],
                                 HN[:, ds(g * GRP, GRP), :]).then_inc(h0_out, 16)
                sp.wait_ge(h0_out, 16 * NG)

            @block.scalar
            def _(act):
                act.dma_start(dt_i, io["dst_tiles"].rearrange("p (q e) -> p q e", q=ETQ)).then_inc(e_in, 16)
                nc.scalar.preload_act_table(ACT.Sqrt)
                with act.Fori(0, NG) as g:
                    hold(act, a_stats, g + 1)
                    nc.scalar.activation(std[:], mv[:, :, 1], ACT.Sqrt, bias=eps[:, 0:1]).then_inc(a_std, 1)

            @block.gpsimd
            def _(pool):
                nc.gpsimd.iota(iota[:], [[1, TABLE]], base=0, channel_multiplier=0,
                               allow_small_or_imprecise_dtypes=True).then_inc(a_const, 1)
                nc.gpsimd.iota(part[:], [[1, 1]], base=0, channel_multiplier=1,
                               allow_small_or_imprecise_dtypes=True).then_inc(a_const, 1)
                nc.gpsimd.iota(tile_id[:], [[1, ETQ]], base=0, channel_multiplier=ETQ,
                               allow_small_or_imprecise_dtypes=True)
                pool.wait_ge(a_const, 2)
                nc.gpsimd.iota(NIDT[:], [[P, NT]], base=0, channel_multiplier=1,
                               allow_small_or_imprecise_dtypes=True)
                nc.gpsimd.iota(expert8[:], [[1, E]], base=-E, channel_multiplier=0,
                               allow_small_or_imprecise_dtypes=True)
                nc.gpsimd.memset(zeros[:], 0.0)
                nc.gpsimd.memset(BIG[:, 0:NT * 257], 0.0)

            @block.vector
            def _(dve):
                nc.vector.memset(eps[:], EPS)
                nc.vector.memset(X[:, NT - 1, :], 0.0).then_inc(a_ready, 1)
                nc.vector.memset(ones[:], 1.0)
                dve.wait_ge(a_const, 2)
                nc.vector.tensor_scalar(ident[:], iota[:, 0:P], part[:, 0:1], None, ALU.is_equal)
                nc.vector.tensor_scalar(before[:], iota[:, 0:P], part[:, 0:1], None, ALU.is_gt)
                nc.vector.tensor_scalar(upto[:], iota[:, 0:P], part[:, 0:1], None, ALU.is_ge)
                nc.vector.memset(one4[:], 1.0)
                nc.vector.memset(ones_of(-WIN0), -float(WIN0))
                nc.vector.memset(ones_of(WIN), float(WIN))
                nc.vector.memset(ones_of(-WIN), -float(WIN))
                nc.vector.memset(win_of[:, 0:LAG], float(NWPAD - 1))
                dve.wait_ge(e_in, 16)
                nc.vector.tensor_reduce(lo_dst[:], dt_i, AX.X, ALU.min).then_inc(a_mm, 1)
                nc.vector.tensor_reduce(hi_dst[:], dt_i, AX.X, ALU.max).then_inc(a_mm, 1)
                dve.wait_ge(a_mm, 2)
                ranges_dve(dve, WIN0, CHUNK0)
                for g in range(NG):
                    dve.wait_ge(x_in[g], 32 if g == NG - 1 else 16)
                    tiles = X[:, g * GRP:(g + 1) * GRP, :]
                    st = Steps(dve, a_st, g * (LN_A + LN_B))
                    ln_stats(dve, st, tiles)
                    st.wait()
                    dve.sem_inc(a_stats, 1)
                    dve.wait_ge(a_std, g + 1)
                    ln_apply(dve, st, tiles, HN[:, g * GRP:(g + 1) * GRP, :])
                    st.wait()
                    dve.sem_inc(a_hn, 1)

            @block.tensor
            def _(pe):
                ranges_pe(pe)

        end_phase()

        t_ld, t_conv, t_m, t_pe, t_win, t_rel, t_st = (
            sem("t_" + n) for n in ("tiles_in", "converted", "masks", "sums", "windows", "dst_and_nodes", "st"))
        table_sems = [n_pe, n_st, t_ld, t_conv, t_m, t_pe, t_win, t_rel, t_st]
        cols = lambda k: SCR[0:ETP, k * ETQ * TABLE:(k + 1) * ETQ * TABLE].rearrange("p (q j) -> p q j", q=ETQ)
        past_end, in_tile = cols(0), cols(2)
        tiles_at = lambda k: SCR[0:ETP, 3 * ETQ * TABLE + k * ETQ * P:3 * ETQ * TABLE + (k + 1) * ETQ * P]
        dst_t, src_t, w_t = (tiles_at(k).rearrange("p (q e) -> p q e", q=ETQ) for k in range(3))
        dst_ti, src_ti = (tiles_at(k).bitcast(i32) for k in (3, 4))
        win_f = SCR[0:1, 9216:9216 + TABLE]

        def load_chunks():
            return nc.values_load(chunks_i[0:1, 0:1], min_val=1, max_val=MAXCHUNKS,
                                  skip_runtime_bounds_check_because="counted up to MAXCHUNKS")

        def build_table(block, win, nwin, chunk, weights):
            @block.sync
            def _(sp):
                sp.dma_start(dst_ti, io["dst_tiles"]).then_inc(t_ld, 16)
                sp.dma_start(src_ti, io["src_tiles"]).then_inc(t_ld, 16)
                if weights:
                    sp.dma_start(tiles_at(2), io["w_tiles"]).then_inc(t_ld, 16)

            @block.scalar
            def _(act):
                nc.scalar.preload_act_table(ACT.Copy)
                act.wait_ge(t_ld, 48 if weights else 32)
                nc.scalar.activation(tiles_at(0), dst_ti, ACT.Copy).then_inc(t_conv, 1)
                nc.scalar.activation(tiles_at(1), src_ti, ACT.Copy).then_inc(t_conv, 1)
                act.wait_ge(t_pe, 1)
                nc.scalar.activation(src_items[:], BANKS[2][:, 0:TABLE], ACT.Copy)
                if weights:
                    act.wait_ge(t_pe, 2)
                    nc.scalar.activation(aux_items[:], BANKS[4][:, 0:TABLE], ACT.Copy)

            @block.vector
            def _(dve):
                for q in range(ETQ):
                    nc.vector.tensor_scalar(past_end[:, q, :], iota[0:ETP, 0:TABLE], ends[:, q:q + 1], None, ALU.is_ge).then_inc(t_m, 1)
                for q in range(ETQ):
                    dve.wait_ge(t_m, q + 1)
                    nc.vector.scalar_tensor_tensor(in_tile[:, q, :], iota[0:ETP, 0:TABLE], starts[:, q:q + 1], past_end[:, q, :],
                                                   ALU.is_ge, ALU.subtract).then_inc(t_m, 1)
                dve.wait_ge(t_win, 1)
                st = Steps(dve, t_st)
                st(nc.vector.tensor_tensor(win_f, BANKS[1][0:1, 0:TABLE], iota[0:1, 0:TABLE], ALU.add))
                if not weights:
                    nc.vector.tensor_copy(tile_of[:], BANKS[0][0:1, 0:TABLE])
                st.wait()
                st(nc.vector.tensor_scalar(win_f, win_f, float(nwin - 1), None, ALU.min))
                st.wait()
                dve.sem_inc(t_win, 1)
                nc.vector.tensor_copy(win_of[:, LAG:], win_f)
                for t, by in ((ends, -chunk), (starts, -chunk), (first, chunk)):
                    nc.vector.tensor_scalar(t[:], t[:], float(by), None, ALU.add)
                dve.wait_ge(t_rel, 1)
                nc.vector.tensor_copy(dst_items[:], BANKS[3][:, 0:TABLE])
                if not weights:
                    nc.vector.tensor_scalar(aux_items[0:win, :], BANKS[5][0:win, 0:TABLE], part[0:win, 0:1], None, ALU.add)

            @block.tensor
            def _(pe):
                for q in range(ETQ):
                    pe.wait_ge(t_m, ETQ + q + 1)
                    m = nc.tensor.matmul(BANKS[1][0:1, 0:TABLE], first[:, q:q + 1], in_tile[:, q, :], start=q == 0, stop=q == ETQ - 1)
                    if not weights:
                        m = nc.tensor.matmul(BANKS[0][0:1, 0:TABLE], tile_id[:, q:q + 1], in_tile[:, q, :], start=q == 0, stop=q == ETQ - 1)
                m.then_inc(t_win, 1)
                pe.wait_ge(t_conv, 2)
                for bank, tiles in ((2, src_t), (4, w_t)) if weights else ((2, src_t),):
                    for q in range(ETQ):
                        m = nc.tensor.matmul(BANKS[bank][:, 0:TABLE], tiles[:, q, :], in_tile[:, q, :], start=q == 0, stop=q == ETQ - 1)
                    m.then_inc(t_pe, 1)
                for q in range(ETQ):
                    nc.tensor.matmul(BANKS[3][:, 0:TABLE], dst_t[:, q, :], in_tile[:, q, :], start=q == 0, stop=False)
                pe.wait_ge(t_win, 2)
                m = nc.tensor.matmul(BANKS[3][:, 0:TABLE], ones_of(-win), win_f, start=False, stop=True)
                if not weights:
                    m = nc.tensor.matmul(BANKS[5][0:win, 0:TABLE], ones_of(win)[:, 0:win], win_f, start=True, stop=True)
                m.then_inc(t_rel, 1)

        R0 = UN0 // 2
        rows_in = sems("rows_in", R0)
        R1 = UN1 // 2
        rows_in1 = sems("rows1_in", R1)
        b_idx, b_scaled, b_S, b_pe, b_acc = (sem(n) for n in ("b_idx", "b_scaled", "b_onehot", "b_summed", "b_acc"))
        b_sems = [b_idx, b_scaled, b_S, b_pe, b_acc]
        rows0 = SCR[:, 0:R0 * D].rearrange("p (k n) -> p k n", n=D)
        msg0 = SCR[:, 2560:2560 + 4 * 257].rearrange("p (k n) -> p k n", n=257)
        S0 = SCR[:, 3600:3600 + 4 * WIN0].rearrange("p (k n) -> p k n", n=WIN0)

        def gather_items(pool, unroll, iters, ring, source, arrived, done):
            slots = unroll // 2
            with pool.Fori(0, iters) as i:
                for k in range(unroll):
                    hold(pool, done, i * unroll + (k + 1))
                    if k % slots == 0:
                        nc.gpsimd.tensor_copy(idx[:, k:k + slots], src_items[:, ds(i * unroll + k, slots)]).then_inc(b_idx, 1)
                        hold(pool, b_idx, i * 2 + (k // slots + 1))
                    nc.gpsimd.indirect_dma_start(
                        out=ring[:, k % slots, :], out_offset=None, in_=source,
                        in_offset=bass.IndirectOffsetOnAxis(ap=idx[:, k:k + 1].bitcast(u32), axis=0)).then_inc(arrived[k % slots], 16)

        def edge_sum0(block, chunk):
            ITERS = CHUNK0 // UN0

            @block.gpsimd
            def _(pool):
                gather_items(pool, UN0, ITERS, rows0, H0, rows_in, b_scaled)

            @block.scalar
            def _(act):
                act.sem_inc(b_scaled, R0)
                with act.Fori(0, ITERS) as i:
                    for k in range(UN0):
                        act.wait_ge(rows_in[k % R0], chunk * (ITERS * 32) + i * 32 + 16 * (k // R0 + 1))
                        act.nop(nofuse=True)
                        hold(act, b_pe, i * UN0 + (k + 1))
                        nc.scalar.activation(msg0[:, k % 4, 0:D], rows0[:, k % R0, :], ACT.Copy,
                                             scale=aux_items[:, ds(i * UN0 + k, 1)]).then_inc(b_scaled, 1)

            @block.vector
            def _(dve):
                nc.vector.memset(msg0[:, :, D:D + 1], 1.0).then_inc(b_S, 1)
                dve.sem_inc(b_acc, 4)
                with dve.Fori(0, ITERS) as i:
                    ws = load_regs(ENG.DVE, win_of[0:1, ds(i * UN0 + LAG, UN0)], 0, NWIN0 - 1)

                    def onehot(k):
                        hold(dve, b_pe, i * UN0 + (k + 1))
                        nc.vector.tensor_scalar(S0[:, k % 4, :], iota[:, 0:WIN0], dst_items[:, ds(i * UN0 + k, 1)],
                                                None, ALU.is_equal).then_inc(b_S, 1)
                    onehot(0)
                    onehot(1)
                    for k in range(UN0):
                        if k + 2 < UN0:
                            onehot(k + 2)
                        hold(dve, b_pe, i * UN0 + (k + 5))
                        hold(dve, b_acc, i * UN0 + (k + 4))
                        a = acc0[:, ds(ws[k], 1), :]
                        nc.vector.tensor_tensor(a, a, BANKS[k % 4][:, 0:257].rearrange("p (o n) -> p o n", o=1), ALU.add).then_inc(b_acc, 1)

            @block.tensor
            def _(pe):
                pe.sem_inc(b_pe, 4)
                with pe.Fori(0, ITERS) as i:
                    for k in range(UN0):
                        pe.wait_ge(b_S, i * UN0 + (k + 2))
                        pe.wait_ge(b_scaled, i * UN0 + (k + 1 + R0))
                        pe.wait_ge(b_acc, i * UN0 + (k + 1))
                        nc.tensor.matmul(BANKS[k % 4][:, 0:257], S0[:, k % 4, :], msg0[:, k % 4, :],
                                         start=True, stop=True).then_inc(b_pe, 1)

        n_chunks0 = load_chunks()
        with nc.Fori(0, n_chunks0) as chunk:
            with nc.Block() as block:
                build_table(block, WIN0, NWIN0, CHUNK0, weights=True)
            with nc.Block() as block:
                edge_sum0(block, chunk)
            with nc.Block() as block:
                clear(block, table_sems + b_sems)

        def walk_tiles(eng, *stages):
            most = max(lead for _, lead in stages)

            def turn(s):
                for step, lead in stages:
                    if 0 <= s + lead < NT:
                        step(s + lead, (s + lead) % 4, (s + lead) // 4)
            rounds = (NT - most) // 4
            for s in range(-most, 0):
                turn(s)
            with eng.Fori(0, rounds) as i:
                for k in range(4):
                    for step, lead in stages:
                        step(i * 4 + (k + lead), (k + lead) % 4, i + (k + lead) // 4)
            for s in range(4 * rounds, NT):
                turn(s)

        def tile_std(slot):
            return nc.scalar.activation(std[:, slot:slot + 1], mv[:, slot, 1:2], ACT.Sqrt, bias=eps[:, 0:1])

        def pe_transpose(bank, rows):
            nc.tensor.transpose(BANKS[bank][:, 0:P], rows[:, 0:P], ident[:])
            return nc.tensor.transpose(BANKS[bank][:, P:D], rows[:, P:D], ident[:])

        def ring4(at):
            return SCR[:, at:at + 4 * D].rearrange("p (s n) -> p s n", n=D)

        def halves(slot_tile):
            return slot_tile.rearrange("p (c n) -> p c n", c=2)

        stage_acc, xt1, h_rows, xt2 = ring4(0), ring4(1024), ring4(2048), ring4(3072)
        c_stage, c_T1, c_x1, c_O, c_stats, c_std, c_h, c_T2, c_x2, c_L, c_lg, c_hn, c_x, c_bn, c_rstd = (
            phase_sem("c_" + n) for n in ("stage", "sumsT", "sumsT_read", "out", "stats", "std", "norm", "normT", "normT_read",
                                          "logits", "logits_read", "copied", "updated", "bn_stats", "rstd"))
        def node_update0(block):
            @block.sync
            def _(sp):
                for buf, rows in ((BUF0, TRASH0), (BUF1, TRASH1)):
                    flat = buf[0:rows, :].rearrange("(p r) d -> p (r d)", p=P)
                    width = flat.shape[1]
                    for a in range(0, width, 1024):
                        sp.dma_start(flat[:, a:a + 1024], zeros[:]).then_inc(zero_fill, 16)

            @block.gpsimd
            def _(pool):
                def stage(n, slot, use):
                    hold(pool, c_T1, n + 1)
                    nc.gpsimd.tensor_copy(stage_acc[:, slot:slot + 1, :], acc0[:, ds(n, 1), 0:D]).then_inc(c_stage, 1)

                nc.gpsimd.tensor_copy(CNT[:], acc0[:, :, D])
                walk_tiles(pool, (stage, 6))

            @block.tensor
            def _(pe):
                pe.sem_inc(c_T1, 4)
                pe.sem_inc(c_O, 4)
                pe.sem_inc(c_T2, 4)
                pe.sem_inc(c_L, 4)
                pe.wait_ge(weights_in, 48)

                def turn_sums(n, slot, use):
                    pe.wait_ge(c_stage, n + 1)
                    pe.wait_ge(c_x1, n + 1)
                    pe_transpose(slot % 2, stage_acc[:, slot, :]).then_inc(c_T1, 1)

                def product(n, slot, use):
                    pe.wait_ge(c_x1, n + 3)
                    pe.wait_ge(c_x, n + 1)
                    for c in range(2):
                        m = nc.tensor.matmul(BANKS[2 + slot % 2][:, 0:D], halves(xt1[:, slot, :])[:, c, :], W0s[:, c, :], start=c == 0, stop=c == 1)
                    m.then_inc(c_O, 1)

                def turn_norm(n, slot, use):
                    pe.wait_ge(c_h, n + 1)
                    pe.wait_ge(c_x2, n + 1)
                    pe_transpose(4 + slot % 2, h_rows[:, slot, :]).then_inc(c_T2, 1)

                def logits(n, slot, use):
                    pe.wait_ge(c_x2, n + 3)
                    pe.wait_ge(c_lg, n + 1)
                    for c in range(2):
                        m = nc.tensor.matmul(BANKS[6 + slot % 2][:, 0:E], halves(xt2[:, slot, :])[:, c, :], gate_ws[:, c, :], start=c == 0, stop=c == 1)
                    m.then_inc(c_L, 1)
                walk_tiles(pe, (turn_sums, 6), (product, 5), (turn_norm, 1), (logits, 0))

            @block.scalar
            def _(act):
                act.sem_inc(c_x1, 2)
                act.sem_inc(c_x2, 2)
                act.sem_inc(c_hn, 4)
                nc.scalar.preload_act_table(ACT.Sqrt)

                def read_sums(n, slot, use):
                    hold(act, c_T1, n + 5)
                    hold(act, c_O, n + 1)
                    nc.scalar.activation(xt1[:, slot, :], BANKS[slot % 2][:, 0:D], ACT.Copy).then_inc(c_x1, 1)

                def deviation(n, slot, use):
                    hold(act, c_stats, n + 1)
                    tile_std(slot).then_inc(c_std, 1)

                def read_norm(n, slot, use):
                    hold(act, c_T2, n + 5)
                    hold(act, c_L, n + 1)
                    nc.scalar.activation(xt2[:, slot, :], BANKS[4 + slot % 2][:, 0:D], ACT.Copy).then_inc(c_x2, 1)

                def copy_norm(n, slot, use):
                    hold(act, c_h, n + 1)
                    nc.scalar.activation(HN[:, ds(n, 1), :], h_rows[:, slot:slot + 1, :], ACT.Copy).then_inc(c_hn, 1)
                walk_tiles(act, (read_sums, 6), (read_norm, 1), (copy_norm, 2), (deviation, 4))

            @block.vector
            def _(dve):
                dve.sem_inc(c_lg, 2)
                dve.sem_inc(c_x, 2)
                dve.wait_ge(weights_in, 48)

                def update(n, slot, use):
                    hold(dve, c_O, n + 5)
                    x = X[:, ds(n, 1), :]
                    nc.vector.scalar_tensor_tensor(x, BANKS[2 + slot % 2][:, 0:D].unsqueeze(1), 0.0, x, ALU.max, ALU.add).then_inc(c_x, 1)

                def invert(n, slot, use):
                    hold(dve, c_std, n + 1)
                    nc.vector.reciprocal(rstd[:, slot:slot + 1], std[:, slot:slot + 1]).then_inc(c_rstd, 1)

                def gather_stats(n, slot, use):
                    hold(dve, c_x, n + 3)
                    nc.vector.bn_stats(stats[:, slot, :], X[:, ds(n, 1), :].rearrange("p o n -> p (o n)")).then_inc(c_bn, 1)

                def norm(n, slot, use):
                    hold(dve, c_rstd, n + 1)
                    hold(dve, c_T2, n + 1)
                    hold(dve, c_hn, n + 1)
                    nc.vector.tensor_scalar(h_rows[:, slot:slot + 1, :], X[:, ds(n, 1), :], mv[:, slot, 0:1], rstd[:, slot:slot + 1],
                                            ALU.subtract, ALU.mult).then_inc(c_h, 1)

                def aggregate(n, slot, use):
                    hold(dve, c_bn, n + 1)
                    nc.vector.bn_aggr(mv[:, slot, :], stats[:, slot, :]).then_inc(c_stats, 1)

                def read_logits(n, slot, use):
                    hold(dve, c_L, n + 5)
                    nc.vector.tensor_tensor(LG[:, ds(n, 1), :], BANKS[6 + slot % 2][:, 0:E].unsqueeze(1),
                                            gate_bs.unsqueeze(1), ALU.add).then_inc(c_lg, 1)
                walk_tiles(dve, (update, 4), (invert, 3), (gather_stats, 4), (norm, 3), (aggregate, 4), (read_logits, 0))

        with nc.Block() as block:
            node_update0(block)

        def bce(t2):
            return t2[:].unsqueeze(2).to_broadcast([P, NT, E])

        def bct(row):
            return row.unsqueeze(1).to_broadcast([P, NT, E])

        def first_best(st, logits, best, onehot, scratch):
            st(nc.vector.tensor_reduce(best[:], logits[:], AX.X, ALU.max))
            st.wait()
            st(nc.vector.tensor_tensor(onehot[:], logits[:], bce(best), ALU.is_equal))
            st.wait()
            st(nc.vector.tensor_tensor(onehot[:], onehot[:], bct(expert8[:]), ALU.mult))
            st.wait()
            st(nc.vector.tensor_reduce(scratch[:], onehot[:], AX.X, ALU.min))
            st.wait()
            st(nc.vector.tensor_tensor(onehot[:], bct(expert8[:]), bce(scratch), ALU.is_equal))
            st.wait()

        def ranks(dve, st, counted, ready, summed, wait_value):
            st.wait()
            dve.sem_inc(ready, 1)
            dve.wait_ge(summed, wait_value)
            for e in range(E):
                st(nc.vector.tensor_tensor_scan(CUM[:, :, e], ones[:, 0:NT], BANKS[1][:, 0:NT * E].rearrange("p (t e) -> p t e", e=E)[:, :, e],
                                                0.0, ALU.mult, ALU.add))
            st(nc.vector.tensor_copy(RT[:], BANKS[1][:, 0:NT * E].rearrange("p (t e) -> p t e", e=E)))
            st.wait()
            st(nc.vector.tensor_tensor(RT[:], CUM[:], RT[:], ALU.subtract))
            st.wait()
            st(nc.vector.tensor_tensor(RT[:], RT[:], BANKS[0][:, 0:NT * E].rearrange("p (t e) -> p t e", e=E), ALU.add))
            st.wait()

        def pe_ranks(pe, counted, ready, summed, value):
            pe.wait_ge(ready, value)
            flat = counted[:].rearrange("p t e -> p (t e)")
            nc.tensor.matmul(BANKS[0][:, 0:NT * E], upto[:], flat, start=True, stop=True)
            nc.tensor.matmul(BANKS[1][:, 0:NT * E], ones[:], flat, start=True, stop=True).then_inc(summed, 1)

        r_st, r_ready, r_sum, r_exp = (phase_sem("r_" + n) for n in ("st", "ready", "summed", "exp"))
        r_done = sem("r_scattered")

        d_w, d_x = ([phase_sem(f"{n}{k}") for k in range(2)] for n in ("d_weights", "d_rows"))
        d_T, d_xT, d_h, d_hT, d_y, d_ys = (phase_sem("d_" + n) for n in ("transposed", "xT", "hidden", "relu", "y", "y_staged"))
        d_store, d_free = sem("d_store"), phase_sem("d_stage_free")
        w1s = [BIG[:, a * 4096:a * 4096 + 2048].rearrange("p (c f) -> p c f", c=2) for a in range(2)]
        w2s = [BIG[:, a * 4096 + 2048:a * 4096 + 4096].rearrange("p (f n) -> p f n", n=D) for a in range(2)]
        hT = [BIG[:, 8192 + a * 4096:8192 + (a + 1) * 4096].rearrange("p (f s) -> p f s", s=ESLOT) for a in range(2)]
        xin = [SCR[:, a * 1024:(a + 1) * 1024].rearrange("p (s n) -> p s n", n=D) for a in range(2)]
        xT = [SCR[:, 2048 + a * 1024:2048 + (a + 1) * 1024].rearrange("p (c s) -> p c s", c=2) for a in range(2)]
        ys = [SCR[:, 4096 + a * 1024:4096 + (a + 1) * 1024].rearrange("p (s n) -> p s n", n=D) for a in range(2)]
        b2s = SCR[:, 6144:6144 + E * D].rearrange("p (e n) -> p e n", e=E)
        b1s = SCR[:, 8192:8192 + 64]
        d_bias = phase_sem("d_bias")

        def route0(block):
            @block.sync
            def _(sp):
                for a in range(2):
                    sp.dma_start(w1s[a], io["L0_ffn_w1"][a, :, :].rearrange("(c p) f -> p c f", p=P)).then_inc(d_w[a], 16)
                    sp.dma_start(w2s[a], io["L0_ffn_w2"][a, :, :].rearrange("(f p) n -> p f n", p=P)).then_inc(d_w[a], 16)
                sp.dma_start(b1s, io["b1_col"]).then_inc(d_bias, 16)
                sp.dma_start(b2s, io["L0_ffn_b2"].rearrange("e n -> (e n)").partition_broadcast(P).rearrange("p (e n) -> p e n", e=E)).then_inc(d_bias, 16)

            @block.vector
            def _(dve):
                st = Steps(dve, r_st)
                first_best(st, LG, r_a, OH1, r_b)
                st(nc.vector.tensor_tensor(LG[:], LG[:], bce(r_a), ALU.subtract))
                st.wait()
                dve.sem_inc(r_exp, 1)
                ranks(dve, st, OH1, r_ready, r_sum, 1)
                st(nc.vector.tensor_tensor(RT[:], RT[:], OH1[:], ALU.mult))
                st.wait()
                st(nc.vector.tensor_reduce(r_c[:], RT[:], AX.X, ALU.add))
                st.wait()
                st(nc.vector.tensor_scalar(keep1[:], r_c[:], float(CAP), None, ALU.is_le))
                st(nc.vector.tensor_scalar(r_b[:], r_b[:], float(ESLOT), float(E * ESLOT - 1), ALU.mult, ALU.add))
                st(nc.vector.tensor_scalar(r_a[:], r_c[:], float(CAP), None, ALU.min))
                st.wait()
                st(nc.vector.tensor_tensor(r_a[:], r_a[:], r_b[:], ALU.add))
                st.wait()
                st(nc.vector.tensor_scalar(r_b[:], NIDT[:], float(TRASH0), None, ALU.add))
                st.wait()
                st(nc.vector.tensor_copy(from1[:], r_a[:]))
                st.wait()
                st(nc.vector.tensor_tensor(r_a[:], r_a[:], r_b[:], ALU.subtract))
                st.wait()
                st(nc.vector.tensor_tensor(r_a[:], r_a[:], keep1[:], ALU.mult))
                st.wait()
                st(nc.vector.tensor_tensor(r_a[:], r_a[:], r_b[:], ALU.add))
                st.wait()
                st(nc.vector.tensor_copy(to1[:], r_a[:]))
                st.wait()
                dve.sem_inc(r_ready, 1)
                dve.wait_ge(r_exp, 2)
                st(nc.vector.tensor_reduce(r_c[:], LG[:], AX.X, ALU.add))
                st.wait()
                st(nc.vector.reciprocal(r_c[:], r_c[:]))
                st.wait()
                st(nc.vector.tensor_tensor(keep1[:], keep1[:], r_c[:], ALU.mult))

            @block.scalar
            def _(act):
                act.wait_ge(r_exp, 1)
                nc.scalar.activation(LG[:], LG[:], ACT.Exp).then_inc(r_exp, 1)

            @block.tensor
            def _(pe):
                pe_ranks(pe, OH1, r_ready, r_sum, 1)

            @block.gpsimd
            def _(pool):
                pool.wait_ge(zero_fill, 16 * (TRASH0 + TRASH1) * D // (P * 1024))
                pool.wait_ge(r_ready, 2)
                for t in range(NT):
                    nc.gpsimd.indirect_dma_start(
                        out=BUF0, out_offset=bass.IndirectOffsetOnAxis(ap=to1[:, t:t + 1].bitcast(u32), axis=0),
                        in_=HN[:, t, :], in_offset=None).then_inc(r_done, 16)
                pool.wait_ge(r_done, 16 * NT)

        with nc.Block() as block:
            route0(block)

        eW1s = SCR2[:, 0:4 * DM].rearrange("p (c n) -> p c n", n=DM)
        eb1s = SCR2[:, 4 * DM:5 * DM]
        e_w = sem("e_weights")
        NF = F0 // P
        NS = ESLOT // P

        def experts0(block):
            @block.sync
            def _(sp):
                for a in range(2):
                    sp.dma_start(xin[a], BUF0[a * ESLOT:(a + 1) * ESLOT, :].rearrange("(s p) n -> p s n", p=P)).then_inc(d_x[a], 16)
                sp.dma_start(eW1s, io["L1_gnn_eW1"][0:4 * P, :].rearrange("(c p) n -> p c n", p=P)).then_inc(e_w, 16)
                sp.dma_start(eb1s, io["L1_gnn_eb1"].partition_broadcast(P)).then_inc(e_w, 16)
                with sp.Fori(0, E // 2 - 1) as i:
                    for a in range(2):
                        n = 2 * i + (2 + a)
                        hold(sp, d_y, NS * n + NS + 1)
                        sp.dma_start(xin[a], BUF0[ds(n * ESLOT, ESLOT), :].rearrange("(s p) n -> p s n", p=P)).then_inc(d_x[a], 16)
                        sp.dma_start(w1s[a], io["L0_ffn_w1"][ds(n, 1), :, :].rearrange("e (c p) f -> p (e c) f", p=P)).then_inc(d_w[a], 16)
                        sp.dma_start(w2s[a], io["L0_ffn_w2"][ds(n, 1), :, :].rearrange("e (f p) n -> p (e f) n", p=P)).then_inc(d_w[a], 16)

            @block.tensor
            def _(pe):
                pe.sem_inc(d_y, 2 * NS + 1)

                def turn_rows(a, n, use):
                    pe.wait_ge(d_x[a], 16 * (use + 1))
                    pe.wait_ge(d_xT, n + 1)
                    for s in range(NS):
                        for c in range(2):
                            m = nc.tensor.transpose(BANKS[c][:, s * P:(s + 1) * P], xin[a][:, s, c * P:(c + 1) * P], ident[:])
                    m.then_inc(d_T, 1)

                def pair(i, last):
                    for a in range(2):
                        n = 2 * i + a
                        pe.wait_ge(d_xT, n + 2)
                        pe.wait_ge(d_w[a], i * 32 + 32)
                        for f in range(NF):
                            pe.wait_ge(d_hT, n * NF + (f + 1))
                            for c in range(2):
                                m = nc.tensor.matmul(BANKS[2 + f % 4][:, 0:ESLOT], w1s[a][:, c, f * P:(f + 1) * P], xT[a][:, c, :],
                                                     start=c == 0, stop=c == 1)
                            m.then_inc(d_h, 1)
                        if not (last and a == 1):
                            turn_rows(1 - a, n + 1, i + a)
                        for s in range(NS):
                            pe.wait_ge(d_ys, n * NS + (s + 1))
                            for f in range(NF):
                                if s == 0:
                                    pe.wait_ge(d_hT, n * NF + (f + 5))
                                m = nc.tensor.matmul(BANKS[6 + s % 2][:, 0:D], hT[a][:, f, s * P:(s + 1) * P], w2s[a][:, f, :],
                                                     start=f == 0, stop=f == NF - 1)
                            m.then_inc(d_y, 1)
                turn_rows(0, 0, 0)
                with pe.Fori(0, E // 2 - 1) as i:
                    pair(i, False)
                pair(E // 2 - 1, True)

            @block.scalar
            def _(act):
                act.sem_inc(d_xT, 1)
                act.sem_inc(d_hT, 4)
                nc.scalar.preload_act_table(ACT.Relu)
                act.wait_ge(d_bias, 32)

                def read_rows(a, n):
                    hold(act, d_T, n + 1)
                    nc.scalar.activation(xT[a][:, 0, :], BANKS[0][:, :], ACT.Copy)
                    nc.scalar.activation(xT[a][:, 1, :], BANKS[1][:, :], ACT.Copy).then_inc(d_xT, 1)

                def pair(i, last):
                    for a in range(2):
                        n = 2 * i + a
                        for f in range(NF):
                            hold(act, d_h, n * NF + (f + 1))
                            nc.scalar.activation(hT[a][:, f, :], BANKS[2 + f % 4][:, 0:ESLOT], ACT.Relu,
                                                 bias=b1s[:, ds(n * NF + f, 1)]).then_inc(d_hT, 1)
                        if not (last and a == 1):
                            read_rows(1 - a, n + 1)
                read_rows(0, 0)
                with act.Fori(0, E // 2 - 1) as i:
                    pair(i, False)
                pair(E // 2 - 1, True)

            @block.vector
            def _(dve):
                dve.sem_inc(d_ys, 2)
                dve.wait_ge(d_bias, 32)
                with dve.Fori(0, E // 2) as i:
                    for a in range(2):
                        n = 2 * i + a
                        hold(dve, d_free, n + 1)
                        for s in range(NS):
                            hold(dve, d_y, n * NS + (s + 2 + 2 * NS))
                            nc.vector.tensor_tensor(ys[a][:, s:s + 1, :], BANKS[6 + s % 2][:, 0:D].unsqueeze(1), b2s[:, ds(n, 1), :],
                                                    ALU.add).then_inc(d_ys, 1)

            @block.gpsimd
            def _(pool):
                pool.sem_inc(d_free, 2)
                with pool.Fori(0, E // 2) as i:
                    for a in range(2):
                        n = 2 * i + a
                        hold(pool, d_ys, (n + 1) * NS + 2)
                        nc.gpsimd.dma_start(Y0[ds(n * ESLOT, ESLOT), :].rearrange("(s p) n -> p s n", p=P), ys[a]).then_inc(d_store, 16)
                        hold(pool, d_store, n * 16 + 16)
                        pool.sem_inc(d_free, 1)

        with nc.Block() as block:
            experts0(block)

        GY, finite_r, beyond_r, fill_r = ring4(0), ring4(1024), ring4(2048), ring4(3072)
        pstage = SCR[:, 6656:6656 + 4 * DM].rearrange("p (s n) -> p s n", n=DM)
        h_rows1, xt3 = ring4(8704), ring4(4096)
        Q = BIG[0:WIN, :].rearrange("p (w n) -> p w n", n=DM)
        acc1 = BIG[WIN:P, :].rearrange("p (w n) -> p w n", n=DM)
        e_gy = sems("e_rows", 4)
        e_store = [phase_sem(f"e_store{k}") for k in range(4)]
        (e_idx, e_y, e_over, e_stats, e_std, e_rstd, e_h, e_T, e_xt, e_pq, e_p, e_q, e_landed, e_x) = (
            phase_sem("e_" + n) for n in ("index", "scaled", "beyond", "stats", "std", "rstd", "norm", "transposed", "xt",
                                          "products", "src_read", "dst_read", "landed", "x_steps"))
        XS = 6

        def project(block):
            @block.sync
            def _(sp):
                def store(n, slot, use):
                    hold(sp, e_p, n + 3)
                    sp.dma_start(PROJ[ds(n * P, P), :], pstage[:, slot, :]).then_inc(e_store[slot], 16)

                def landed(n, slot, use):
                    hold(sp, e_store[slot], 16 * (use + 1))
                    sp.sem_inc(e_landed, 1)
                walk_tiles(sp, (store, 1), (landed, 0))

            @block.gpsimd
            def _(pool):
                def beyond(n, slot, use):
                    hold(pool, e_y, n + 1)
                    nc.gpsimd.tensor_scalar(beyond_r[:, slot, :], GY[:, slot, :], 0.0, 1e4, ALU.is_gt, ALU.mult).then_inc(e_over, 1)

                def gather(n, slot, use):
                    hold(pool, e_x, XS * n + 4)
                    nc.gpsimd.tensor_copy(idx[:, slot:slot + 1], from1[:, ds(n, 1)]).then_inc(e_idx, 1)
                    hold(pool, e_idx, n + 1)
                    nc.gpsimd.indirect_dma_start(
                        out=GY[:, slot, :], out_offset=None, in_=Y0,
                        in_offset=bass.IndirectOffsetOnAxis(ap=idx[:, slot:slot + 1].bitcast(u32), axis=0)).then_inc(e_gy[slot], 16)
                walk_tiles(pool, (gather, 6), (beyond, 4))

            @block.scalar
            def _(act):
                act.sem_inc(e_xt, 2)
                act.sem_inc(e_q, 4)
                nc.scalar.preload_act_table(ACT.Sqrt)

                def scale(n, slot, use):
                    hold(act, e_gy[slot], 16 * (use + 1))
                    nc.scalar.activation(GY[:, slot, :], GY[:, slot, :], ACT.Copy, scale=keep1[:, ds(n, 1)]).then_inc(e_y, 1)

                def deviation(n, slot, use):
                    hold(act, e_stats, n + 1)
                    tile_std(slot).then_inc(e_std, 1)

                def read_norm(n, slot, use):
                    hold(act, e_T, n + 5)
                    hold(act, e_pq, 2 * n + 2)
                    nc.scalar.activation(xt3[:, slot, :], BANKS[slot % 2][:, 0:D], ACT.Copy).then_inc(e_xt, 1)

                def read_q(n, slot, use):
                    hold(act, e_pq, 2 * n + 10)
                    for a in range(2):
                        nc.scalar.activation(Q[:, ds(n * 2 + a, 1), :], BANKS[5 + 2 * (slot % 2)][a * WIN:(a + 1) * WIN, :].unsqueeze(1),
                                             ACT.Copy).then_inc(e_q, 1)

                def clear_sums(n, slot, use):
                    nc.scalar.activation(acc1[:, ds(2 * n, 2), :], zeros[WIN:P, :].rearrange("p (w n) -> p w n", n=DM), ACT.Copy)
                walk_tiles(act, (read_norm, 1), (scale, 4), (deviation, 3), (read_q, 0), (clear_sums, 0))

            @block.tensor
            def _(pe):
                pe.sem_inc(e_T, 4)
                pe.sem_inc(e_pq, 8)
                pe.wait_ge(e_w, 32)

                def turn_norm(n, slot, use):
                    pe.wait_ge(e_h, n + 1)
                    pe.wait_ge(e_xt, n + 1)
                    pe_transpose(slot % 2, h_rows1[:, slot, :]).then_inc(e_T, 1)

                def products(n, slot, use):
                    pe.wait_ge(e_xt, n + 3)
                    pe.wait_ge(e_p, n + 1)
                    pe.wait_ge(e_q, 2 * n + 2)
                    for side in range(2):
                        for c in range(2):
                            m = nc.tensor.matmul(BANKS[4 + 2 * (slot % 2) + side][:, :], halves(xt3[:, slot, :])[:, c, :], eW1s[:, 2 * side + c, :],
                                                 start=c == 0, stop=c == 1)
                        m.then_inc(e_pq, 1)
                walk_tiles(pe, (turn_norm, 1), (products, 0))

            @block.vector
            def _(dve):
                dve.sem_inc(e_x, 4 * XS)
                dve.sem_inc(e_p, 2)
                dve.sem_inc(e_landed, 4)
                dve.wait_ge(e_w, 32)
                step = lambda n, k: XS * (n + 4) + k

                def masks(n, slot, use):
                    hold(dve, e_y, n + 1)
                    nc.vector.tensor_scalar(finite_r[:, slot, :].bitcast(i32), GY[:, slot, :], 0.0, 0.0, ALU.mult, ALU.is_equal).then_inc(e_x, 1)
                    nc.vector.tensor_scalar(fill_r[:, slot, :], GY[:, slot, :], 0.0, -1e4, ALU.is_lt, ALU.mult).then_inc(e_x, 1)

                def invert(n, slot, use):
                    hold(dve, e_std, n + 1)
                    nc.vector.reciprocal(rstd[:, slot:slot + 1], std[:, slot:slot + 1]).then_inc(e_rstd, 1)

                def fill(n, slot, use):
                    hold(dve, e_over, n + 1)
                    hold(dve, e_x, step(n, 2))
                    nc.vector.tensor_tensor(fill_r[:, slot, :], fill_r[:, slot, :], beyond_r[:, slot, :], ALU.add).then_inc(e_x, 1)

                def norm(n, slot, use):
                    hold(dve, e_rstd, n + 1)
                    hold(dve, e_T, n + 1)
                    nc.vector.tensor_scalar(h_rows1[:, slot:slot + 1, :], X[:, ds(n, 1), :], mv[:, slot, 0:1], rstd[:, slot:slot + 1],
                                            ALU.subtract, ALU.mult).then_inc(e_h, 1)

                def select(n, slot, use):
                    hold(dve, e_x, step(n, 3))
                    nc.vector.copy_predicated(fill_r[:, slot, :], finite_r[:, slot, :].bitcast(i32), GY[:, slot, :]).then_inc(e_x, 1)

                def add_bias(n, slot, use):
                    hold(dve, e_landed, n + 1)
                    hold(dve, e_pq, 2 * n + 9)
                    nc.vector.tensor_tensor(pstage[:, slot, :], BANKS[4 + 2 * (slot % 2)][:, :], eb1s, ALU.add).then_inc(e_p, 1)

                def update(n, slot, use):
                    hold(dve, e_x, step(n, 4))
                    nc.vector.tensor_tensor(X[:, ds(n, 1), :], X[:, ds(n, 1), :], fill_r[:, slot:slot + 1, :], ALU.add).then_inc(e_x, 1)
                    hold(dve, e_x, step(n, 5))
                    nc.vector.bn_stats(stats[:, slot, :], X[:, ds(n, 1), :].rearrange("p o n -> p (o n)")).then_inc(e_x, 1)
                    hold(dve, e_x, step(n, 6))
                    nc.vector.bn_aggr(mv[:, slot, :], stats[:, slot, :]).then_inc(e_stats, 1)
                walk_tiles(dve, (masks, 3), (invert, 2), (fill, 3), (norm, 2), (select, 3), (add_bias, 0), (update, 3))

        with nc.Block() as block:
            project(block)

        end_phase()

        f_rows = SCR[:, 0:R1 * DM].rearrange("p (k n) -> p k n", n=DM)
        f_rhs = SCR[:, 4096:4096 + 4 * DM].rearrange("p (k n) -> p k n", n=DM)
        f_msg = SCR[:, 6144:6144 + 4 * DM].rearrange("p (k n) -> p k n", n=DM)
        f_cat = SCR[:, 8192:8192 + 4 * P].rearrange("p (k n) -> p k n", n=P)
        f_dst = SCR[:, 8704:8704 + 4 * P].bitcast(i32).rearrange("p (k n) -> p k n", n=P)
        f_S = SCR[:, 9216:9216 + 4 * WIN].rearrange("p (k n) -> p k n", n=WIN)
        f_in = [phase_sem(f"f_edges{k}") for k in range(R1)]
        f_cats, f_qs, f_U, f_add, f_relu, f_onehot, f_seg, f_acc, f_w = (
            phase_sem("f_" + n) for n in ("cat", "rhs", "inputs", "added", "relu", "onehot", "summed", "acc", "weights"))
        f_sems = [b_idx, *f_in, f_cats, f_qs, f_U, f_add, f_relu, f_onehot, f_seg, f_acc, f_w]

        def edge_sum1(block, chunk):
            ITERS = CHUNK1 // UN1

            @block.gpsimd
            def _(pool):
                gather_items(pool, UN1, ITERS, f_rows, PROJ, rows_in1, f_add)

            @block.sync
            def _(sp):
                def load(slot, n, t):
                    sp.dma_start(f_cat[WIN:P, slot, :], io["attr_t"][:, ds(t * P, P)]).then_inc(f_in[n], 16)
                    sp.dma_start(f_dst[0:WIN, slot, :], io["dst_row"][ds(t * P, P)].partition_broadcast(WIN)).then_inc(f_in[n], 16)
                for k in range(4):
                    sp.dma_start(f_rhs[WIN:P, k, :], io["L1_gnn_eW1"][2 * D:2 * D + ED, :]).then_inc(f_w, 16)
                with sp.Fori(0, ITERS) as i:
                    ts = load_regs(ENG.SP, tile_of[0:1, ds(i * UN1, UN1)], 0, ET)
                    for k in range(UN1):
                        hold(sp, f_U, i * UN1 + (k + 1))
                        load(k % 4, k % R1, ts[k])
                ts = load_regs(ENG.SP, tile_of[0:1, CHUNK1:CHUNK1 + LEAD], 0, ET)
                for k in range(LEAD):
                    sp.wait_ge(f_U, CHUNK1 + k + 1)
                    load(k % 4, k, ts[k])
                for k in range(LEAD):
                    sp.wait_ge(f_in[k], 32 * (2 * ITERS + 1))

            @block.scalar
            def _(act):
                def copy_q(slot, w):
                    nc.scalar.activation(f_rhs[0:WIN, slot:slot + 1, :], Q[:, ds(w, 1), :], ACT.Copy).then_inc(f_qs, 1)
                nc.scalar.preload_act_table(ACT.Relu)
                for k, w in enumerate(load_regs(ENG.Activation, win_of[0:1, LAG:LAG + LEAD], 0, NWIN - 1)):
                    copy_q(k, w)
                with act.Fori(0, ITERS) as i:
                    ws = load_regs(ENG.Activation, win_of[0:1, ds(i * UN1 + LAG + LEAD, UN1)], 0, NWIN - 1)
                    for k in range(UN1):
                        hold(act, f_U, i * UN1 + (k + LEAD + 1))
                        copy_q((k + LEAD) % 4, ws[k])
                        hold(act, f_add, i * UN1 + (k + 1 + R1))
                        nc.scalar.activation(f_msg[:, k % 4, :], f_msg[:, k % 4, :], ACT.Relu).then_inc(f_relu, 1)

            @block.vector
            def _(dve):
                def cat(slot, item):
                    nc.vector.tensor_scalar(f_cat[0:WIN, slot, :], f_dst[0:WIN, slot, :], aux_items[0:WIN, item], None,
                                            ALU.is_equal).then_inc(f_cats, 1)

                def accumulate(slot, w, summed):
                    hold(dve, f_seg, summed)
                    hold(dve, f_acc, summed + 1)
                    a = acc1[:, ds(w, 1), :]
                    nc.vector.tensor_tensor(a, a, BANKS[4 + slot][WIN:P, :].unsqueeze(1), ALU.add).then_inc(f_acc, 1)
                dve.sem_inc(f_add, R1)
                dve.sem_inc(f_acc, 4)
                for slot in (2, 3):
                    nc.vector.memset(f_S[:, slot, :], 0.0).then_inc(f_onehot, 1)
                    nc.vector.memset(f_msg[:, slot, :], 0.0).then_inc(f_relu, 1)
                for k in range(LEAD):
                    dve.wait_ge(f_in[k], 32)
                    cat(k, slice(k, k + 1))
                with dve.Fori(0, ITERS) as i:
                    ws = load_regs(ENG.DVE, win_of[0:1, ds(i * UN1, UN1)], 0, NWPAD - 1)
                    for k in range(UN1):
                        n = i * UN1 + k
                        hold(dve, f_seg, n + 1)
                        hold(dve, f_U, n + 5)
                        dve.wait_ge(rows_in1[k % R1], chunk * (ITERS * 32) + i * 32 + 16 * (k // R1 + 1))
                        nc.vector.tensor_tensor(f_msg[:, k % 4, :], f_rows[:, k % R1, :], BANKS[k % 4][:, :], ALU.add).then_inc(f_add, 1)
                        nc.vector.tensor_scalar(f_S[:, k % 4, :], iota[:, 0:WIN], dst_items[:, ds(n, 1)],
                                                None, ALU.is_equal).then_inc(f_onehot, 1)
                        ahead = k + LEAD
                        hold(dve, f_in[ahead % R1], i * 64 + 32 * (ahead // R1 + 1))
                        cat(ahead % 4, ds(i * UN1 + ahead, 1))
                        accumulate((k - LAG) % 4, ws[k], n + 3)
                for k, w in enumerate(load_regs(ENG.DVE, win_of[0:1, CHUNK1:CHUNK1 + LAG], 0, NWPAD - 1)):
                    accumulate((k - LAG) % 4, w, CHUNK1 + k + 3)

            @block.tensor
            def _(pe):
                pe.sem_inc(f_U, 4)
                pe.sem_inc(f_seg, 2)

                def segment(slot, n):
                    pe.wait_ge(f_onehot, n + 1)
                    pe.wait_ge(f_relu, n + 1)
                    pe.wait_ge(f_acc, n + 1)
                    nc.tensor.matmul(BANKS[4 + slot][WIN:P, :], f_S[:, slot, :], f_msg[:, slot, :], start=True, stop=True).then_inc(f_seg, 1)
                pe.wait_ge(f_w, 64)
                with pe.Fori(0, ITERS) as i:
                    for k in range(UN1):
                        n = i * UN1 + k
                        pe.wait_ge(f_in[k % R1], i * 64 + 32 * (k // R1 + 1))
                        pe.wait_ge(f_cats, n + 1)
                        pe.wait_ge(f_qs, n + 1)
                        pe.wait_ge(f_add, n + (R1 - 3))
                        nc.tensor.matmul(BANKS[k % 4][:, :], f_cat[:, k % 4, :], f_rhs[:, k % 4, :], start=True, stop=True).then_inc(f_U, 1)
                        segment((k - LAG) % 4, n)
                for k in range(LAG):
                    segment((k - LAG) % 4, CHUNK1 + k)

        with nc.Block() as block:
            @block.vector
            def _(dve):
                ranges_dve(dve, WIN, CHUNK1)

            @block.tensor
            def _(pe):
                ranges_pe(pe)
        n_chunks1 = load_chunks()
        with nc.Fori(0, n_chunks1) as chunk:
            with nc.Block() as block:
                build_table(block, WIN, NWIN, CHUNK1, weights=False)
            with nc.Block() as block:
                edge_sum1(block, chunk)
            with nc.Block() as block:
                clear(block, table_sems + f_sems)

        GN = GRP * P
        HALF = GN // 2
        stage1 = BIG[0:WIN, 0:2 * GRP * DM].rearrange("p (w n) -> p w n", n=DM)
        diag = SCR[:, 9536:9536 + GN]
        AT = SCR[:, 0:4 * GN].rearrange("p (c n) -> p c n", n=GN)
        HID = AT
        GT = SCR[:, 2560:2560 + 2 * GN].rearrange("p (c n) -> p c n", n=GN)
        HT = SCR[:, 3840:3840 + 2 * GN].rearrange("p (c n) -> p c n", n=GN)
        HS = SCR[:, 5120:6400].rearrange("p (k n) -> p k n", n=D)
        eW2s = SCR[:, 6400:7424].rearrange("p (c n) -> p c n", n=D)
        nW2s = SCR[:, 7424:8448].rearrange("p (c n) -> p c n", n=D)
        eb2s, nb2s, gam, bet = (SCR[:, 8448 + k * D:8448 + (k + 1) * D] for k in range(4))
        nb1s = SCR[:, 9472:9476]
        gam1, bet1 = zeros[:, 0:D], zeros[:, D:2 * D]
        Wrs = zeros[:, 2 * D:2 * D + 2 * E].rearrange("p (c e) -> p c e", c=2)
        brs = zeros[:, 3 * D:3 * D + E]
        h_w = sem("h_weights")
        stats_n, mv_n = (SCR2[:, 2048 + 32 * k:2048 + 32 * k + w * GRP].rearrange("p (k n) -> p k n", n=w) for k, w in enumerate((6, 2)))
        std_n, rstd_n = SCR2[:, 2112:2112 + GRP], SCR2[:, 2120:2120 + GRP]
        nW1s = SCR2[:, 0:2048].rearrange("p (c n) -> p c n", n=DM)
        g_w = phase_sem("g_weights")
        (g_stage, g_T, g_hT, g_at, g_agg, g_gt, g_hid, g_relu, g_out, g_h, g_diag, g_stats, g_std, g_z, g_st) = (
            phase_sem("g_" + n) for n in ("stage", "sumsT", "rowsT", "evacuated", "agg", "agg_read", "hidden", "relu", "out", "rows",
                                    "diag", "stats", "std", "out_read", "st"))

        def rows_of(vec):
            return vec.unsqueeze(1).to_broadcast([P, GRP, D])

        O_PAIRS = ((0, 0, 2), (1, 2, 2), (2, 4, 1))

        def node_update1(block):
            @block.gpsimd
            def _(pool):
                with pool.Fori(0, NG - 1) as g:
                    hold(pool, g_T, (g + 1) * GRP + 1)
                    nc.gpsimd.tensor_copy(stage1, acc1[:, ds((g + 1) * 2 * GRP, 2 * GRP), :]).then_inc(g_stage, 1)

            @block.sync
            def _(sp):
                for to, name in ((eW2s, "L1_gnn_eW2"), (nW1s, "L1_gnn_nW1"), (nW2s, "L1_gnn_nW2")):
                    sp.dma_start(to, io[name].rearrange("(c p) n -> p c n", p=P)).then_inc(g_w, 16)
                for to, name in ((eb2s, "L1_gnn_eb2"), (nb2s, "L1_gnn_nb2"), (gam, "L1_gnn_ln_gamma"), (bet, "L1_gnn_ln_beta")):
                    sp.dma_start(to, io[name].partition_broadcast(P)).then_inc(g_w, 16)
                sp.dma_start(nb1s, io["nb1_col"]).then_inc(g_w, 16)
                sp.dma_start(gam1, io["L1_ffn_gamma"].partition_broadcast(P)).then_inc(h_w, 16)
                sp.dma_start(bet1, io["L1_ffn_beta"].partition_broadcast(P)).then_inc(h_w, 16)
                sp.dma_start(Wrs, io["L1_ffn_Wr"].rearrange("(c p) e -> p c e", p=P)).then_inc(h_w, 16)
                sp.dma_start(brs, io["L1_ffn_br"].partition_broadcast(P)).then_inc(h_w, 16)

            @block.scalar
            def _(act):
                nc.scalar.preload_act_table(ACT.Sqrt)
                nc.scalar.activation(stage1, acc1[:, 0:2 * GRP, :], ACT.Copy).then_inc(g_stage, 1)
                def deviation_next(count):
                    hold(act, g_stats, count)
                    nc.scalar.activation(std_n, mv_n[:, :, 1], ACT.Sqrt, bias=eps[:, 0:1]).then_inc(g_std, 1)

                def evacuate(g, last):
                    hold(act, g_out, 3 * g + 1)
                    for k in range(GRP):
                        hold(act, g_T, g * GRP + (k + 2))
                        nc.scalar.activation(AT[:, :, k * P:(k + 1) * P], BANKS[k][:, :].rearrange("p (c n) -> p c n", n=P),
                                             ACT.Copy).then_inc(g_at, 1)
                    for n in range(4):
                        hold(act, g_agg, 4 * g + (n + 1))
                        nc.scalar.activation(GT[:, n // 2, (n % 2) * HALF:(n % 2 + 1) * HALF], BANKS[n][:, 0:HALF], ACT.Copy).then_inc(g_gt, 1)
                    hold(act, g_hT, g + 1)
                    for q, (_, t0, n) in enumerate(O_PAIRS):
                        nc.scalar.activation(HT[:, :, t0 * P:(t0 + n) * P].rearrange("p c (k n) -> p k c n", n=P),
                                             BANKS[5 + q][:, 0:n * 256].rearrange("p (k c n) -> p k c n", k=n, c=2),
                                             ACT.Copy).then_inc(g_at, 1)
                    act.wait_ge(g_w, 128)
                    for n in range(8):
                        hold(act, g_hid, 8 * g + (n + 1))
                        nc.scalar.activation(HID[:, n // 2, (n % 2) * HALF:(n % 2 + 1) * HALF], BANKS[4 + n % 4][:, 0:HALF], ACT.Relu,
                                             bias=nb1s[:, n // 2:n // 2 + 1]).then_inc(g_relu, 1)
                    if not last:
                        deviation_next(2 * g + 2)
                    hold(act, g_stats, 2 * g + (2 if last else 3))
                    nc.scalar.activation(std[:], mv[:, :, 1], ACT.Sqrt, bias=eps[:, 0:1]).then_inc(g_std, 1)
                deviation_next(1)
                with act.Fori(0, NG - 1) as g:
                    evacuate(g, False)
                evacuate(NG - 1, True)

            @block.tensor
            def _(pe):
                pe.sem_inc(g_T, 1)
                pe.sem_inc(g_out, 1)
                with pe.Fori(0, NG) as g:
                    hold(pe, g_stage, g + 1)
                    hold(pe, g_z, 3 * g + 1)
                    for k in range(GRP):
                        for c in range(4):
                            for a in range(2):
                                m = nc.tensor.transpose(BANKS[k][:, c * P + a * WIN:c * P + (a + 1) * WIN],
                                                        stage1[:, 2 * k + a, c * P:(c + 1) * P], ident[0:WIN, 0:WIN])
                        m.then_inc(g_T, 1)
                    pe.wait_ge(g_w, 128)
                    pe.wait_ge(g_at, 8 * g + 5)
                    pe.wait_ge(g_diag, g + 1)
                    for n in range(4):
                        to = BANKS[n][:, 0:HALF]
                        cols = slice((n % 2) * HALF, (n % 2 + 1) * HALF)
                        for c in range(4):
                            nc.tensor.matmul(to, eW2s[:, c, (n // 2) * P:(n // 2 + 1) * P], AT[:, c, cols], start=c == 0, stop=False)
                        nc.tensor.matmul(to, eb2s[:, (n // 2) * P:(n // 2 + 1) * P], diag[:, cols], start=False, stop=True).then_inc(g_agg, 1)
                    pe.wait_ge(g_h, g + 1)
                    for k in range(GRP):
                        for c in range(2):
                            m = nc.tensor.transpose(BANKS[5 + k // 2][:, (k % 2) * 256 + c * P:(k % 2) * 256 + (c + 1) * P],
                                                    HS[:, k, c * P:(c + 1) * P], ident[:])
                    m.then_inc(g_hT, 1)
                    pe.wait_ge(g_at, 8 * g + 8)
                    pe.wait_ge(g_gt, 4 * g + 4)
                    for n in range(8):
                        pe.wait_ge(g_relu, 8 * g + (n + 1))
                        to = BANKS[4 + n % 4][:, 0:HALF]
                        cols = slice((n % 2) * HALF, (n % 2 + 1) * HALF)
                        f = slice((n // 2) * P, (n // 2 + 1) * P)
                        for c in range(4):
                            m = nc.tensor.matmul(to, nW1s[:, c, f], (HT if c < 2 else GT)[:, c % 2, cols], start=c == 0, stop=c == 3)
                        m.then_inc(g_hid, 1)
                    pe.wait_ge(g_relu, 8 * g + 8 + 4)
                    for q, (_, t0, n) in enumerate(O_PAIRS):
                        for k in range(t0, t0 + n):
                            for f in range(4):
                                m = nc.tensor.matmul(BANKS[q][:, (k - t0) * D:(k - t0 + 1) * D], HID[:, f, k * P:(k + 1) * P], nW2s[:, f, :],
                                                     start=f == 0, stop=f == 3)
                        m.then_inc(g_out, 1)

            @block.vector
            def _(dve):
                dve.sem_inc(g_z, 1)
                dve.sem_inc(g_relu, 4)
                xs = lambda g: X[:, ds(g * GRP, GRP), :]

                def diagonals(g):
                    nc.vector.tensor_tensor(diag.rearrange("p (k n) -> p k n", n=P),
                                            ident[:].unsqueeze(1).to_broadcast([P, GRP, P]),
                                            CNT[:, ds(g * GRP, GRP)].unsqueeze(2).to_broadcast([P, GRP, P]),
                                            ALU.mult).then_inc(g_diag, 1)

                def next_stats(st, g, count):
                    for k in range(GRP):
                        st(nc.vector.bn_stats(stats_n[:, k, :], xs(g)[:, k, :]))
                    st.wait()
                    for k in range(GRP):
                        st(nc.vector.bn_aggr(mv_n[:, k, :], stats_n[:, k, :]))
                    st.wait()
                    dve.sem_inc(g_stats, 1)
                    hold(dve, g_std, count)
                    st(nc.vector.reciprocal(rstd_n, std_n))
                    st.wait()

                def update(g, last):
                    st = Steps(dve, g_st, HEAD + g * STEPS)
                    for k in range(GRP):
                        st(nc.vector.tensor_scalar(HS[:, k, :], xs(g)[:, k, :], mv_n[:, k, 0:1], rstd_n[:, k:k + 1],
                                                   ALU.subtract, ALU.mult))
                    st.wait()
                    dve.sem_inc(g_h, 1)
                    hold(dve, g_hT, g + 1)
                    st(nc.vector.tensor_tensor(HS, HS, rows_of(nb2s), ALU.add))
                    if not last:
                        diagonals(g + 1)
                        next_stats(st, g + 1, 2 * g + 2)
                    st.wait()
                    for q, (_, t0, n) in enumerate(O_PAIRS):
                        hold(dve, g_out, 3 * g + (q + 2))
                        st(nc.vector.tensor_tensor(HS[:, t0:t0 + n, :], HS[:, t0:t0 + n, :],
                                                   BANKS[q][:, 0:n * D].rearrange("p (k n) -> p k n", n=D), ALU.add))
                    st.wait()
                    dve.sem_inc(g_z, 3)
                    ln_stats(dve, st, HS)
                    st.wait()
                    dve.sem_inc(g_stats, 1)
                    hold(dve, g_std, 2 * g + (2 if last else 3))
                    ln_apply(dve, st, HS, HS)
                    st.wait()
                    st(nc.vector.tensor_tensor(HS, HS, rows_of(gam), ALU.mult))
                    st.wait()
                    st(nc.vector.tensor_tensor(HS, HS, rows_of(bet), ALU.add))
                    st.wait()
                    st(nc.vector.tensor_tensor(xs(g), xs(g), HS, ALU.add))
                    st.wait()
                    return st.n
                HEAD, STEPS = LN_A + 1, GRP + 1 + (LN_A + 1) + len(O_PAIRS) + LN_A + LN_B + 3
                diagonals(0)
                next_stats(Steps(dve, g_st), 0, 1)
                dve.wait_ge(g_w, 128)
                with dve.Fori(0, NG - 1) as g:
                    assert update(g, False) == STEPS
                update(NG - 1, True)

        with nc.Block() as block:
            node_update1(block)

        end_phase()

        XN = BIG[:, 0:NT * D].rearrange("p (t n) -> p t n", n=D)
        W1s = BIG[:, 6400:6400 + E * 2 * H1].rearrange("p (e c h) -> p e c h", e=E, c=2)
        W2s = BIG[:, 14592:14592 + E * 4 * D].rearrange("p (e f n) -> p e f n", e=E, f=4)
        b2r = BIG[:, 22784:22784 + E * D].rearrange("p (e n) -> p e n", e=E)
        b1r = SCR[:, 6144:6144 + E * H1].rearrange("p (e h) -> p e h", e=E)
        pre_r, z_rows, xt4 = ring4(0), ring4(1024), ring4(2048)
        stats2 = SCR[:, 5664:5688].rearrange("p (s n) -> p s n", n=6)
        mv2 = SCR[:, 5696:5704].rearrange("p (s n) -> p s n", n=2)
        std2, rstd2 = SCR[:, 5712:5716], SCR[:, 5720:5724]
        tile_expert = sb("tile_expert", [1, T1], i32)
        (h_big, h_T, h_xt, h_stats, h_std, h_stats2, h_std2, h_x, h_pre, h_y, h_z, h_L, h_lg, h_copied) = (
            phase_sem("h_" + n) for n in ("expert_weights", "transposed", "xt", "stats", "std", "stats2", "std2", "first_steps",
                                          "normed", "second_steps", "rows", "logits", "logits_read", "copied"))
        h_g, h_rstd, h_rstd2, h_pre2 = (phase_sem("h_" + n) for n in ("gamma", "rstd", "rstd2", "normed2"))

        def router1(block):
            @block.sync
            def _(sp):
                for e in range(E):
                    sp.dma_start(W1s[:, e, :, :], io["L1_ffn_W1"][e, :, :].rearrange("(c p) h -> p c h", p=P)).then_inc(h_big, 16)
                    sp.dma_start(W2s[:, e, :, :], io["L1_ffn_W2"][e, :, :].rearrange("(f p) n -> p f n", p=P)).then_inc(h_big, 16)
                sp.dma_start(b1r, io["L1_ffn_b1"].rearrange("e h -> (e h)").partition_broadcast(P).rearrange("p (e h) -> p e h", e=E)).then_inc(h_big, 16)
                sp.dma_start(b2r, io["L1_ffn_b2"].rearrange("e h -> (e h)").partition_broadcast(P).rearrange("p (e h) -> p e h", e=E)).then_inc(h_big, 16)

            @block.scalar
            def _(act):
                act.sem_inc(h_xt, 2)
                act.sem_inc(h_copied, 4)
                nc.scalar.preload_act_table(ACT.Sqrt)

                def deviation(n, slot, use):
                    hold(act, h_stats, n + 1)
                    tile_std(slot).then_inc(h_std, 1)

                def deviation2(n, slot, use):
                    hold(act, h_stats2, n + 1)
                    nc.scalar.activation(std2[:, slot:slot + 1], mv2[:, slot, 1:2], ACT.Sqrt, bias=eps[:, 0:1]).then_inc(h_std2, 1)

                def copy_rows(n, slot, use):
                    hold(act, h_z, n + 1)
                    nc.scalar.activation(XN[:, ds(n, 1), :], z_rows[:, slot:slot + 1, :], ACT.Copy).then_inc(h_copied, 1)

                def read_rows(n, slot, use):
                    hold(act, h_T, n + 5)
                    hold(act, h_L, n + 1)
                    nc.scalar.activation(xt4[:, slot, :], BANKS[slot % 2][:, 0:D], ACT.Copy).then_inc(h_xt, 1)
                walk_tiles(act, (read_rows, 1), (copy_rows, 1), (deviation2, 4), (deviation, 6))

            @block.tensor
            def _(pe):
                pe.sem_inc(h_T, 4)
                pe.sem_inc(h_L, 4)
                pe.wait_ge(h_w, 64)

                def turn_rows(n, slot, use):
                    pe.wait_ge(h_z, n + 1)
                    pe.wait_ge(h_xt, n + 1)
                    pe_transpose(slot % 2, z_rows[:, slot, :]).then_inc(h_T, 1)

                def logits(n, slot, use):
                    pe.wait_ge(h_xt, n + 3)
                    pe.wait_ge(h_lg, n + 1)
                    for c in range(2):
                        m = nc.tensor.matmul(BANKS[2 + slot % 2][:, 0:E], halves(xt4[:, slot, :])[:, c, :], Wrs[:, c, :], start=c == 0, stop=c == 1)
                    m.then_inc(h_L, 1)
                walk_tiles(pe, (turn_rows, 1), (logits, 0))

            @block.vector
            def _(dve):
                dve.sem_inc(h_lg, 2)
                dve.wait_ge(h_w, 64)

                def stats_first(n, slot, use):
                    nc.vector.bn_stats(stats[:, slot, :], X[:, ds(n, 1), :].rearrange("p o n -> p (o n)")).then_inc(h_x, 1)

                def aggregate_first(n, slot, use):
                    hold(dve, h_x, n + 1)
                    nc.vector.bn_aggr(mv[:, slot, :], stats[:, slot, :]).then_inc(h_stats, 1)

                def invert_first(n, slot, use):
                    hold(dve, h_std, n + 1)
                    nc.vector.reciprocal(rstd[:, slot:slot + 1], std[:, slot:slot + 1]).then_inc(h_rstd, 1)

                def norm_first(n, slot, use):
                    hold(dve, h_rstd, n + 1)
                    hold(dve, h_g, n + 1)
                    nc.vector.tensor_scalar(pre_r[:, slot:slot + 1, :], X[:, ds(n, 1), :], mv[:, slot, 0:1], rstd[:, slot:slot + 1],
                                            ALU.subtract, ALU.mult).then_inc(h_pre, 1)

                def stats_second(n, slot, use):
                    hold(dve, h_pre, n + 1)
                    nc.vector.bn_stats(stats2[:, slot, :], pre_r[:, slot, :]).then_inc(h_y, 1)

                def aggregate_second(n, slot, use):
                    hold(dve, h_y, n + 1)
                    nc.vector.bn_aggr(mv2[:, slot, :], stats2[:, slot, :]).then_inc(h_stats2, 1)

                def invert_second(n, slot, use):
                    hold(dve, h_std2, n + 1)
                    nc.vector.reciprocal(rstd2[:, slot:slot + 1], std2[:, slot:slot + 1]).then_inc(h_rstd2, 1)

                def norm_second(n, slot, use):
                    hold(dve, h_rstd2, n + 1)
                    nc.vector.tensor_scalar(pre_r[:, slot, :], pre_r[:, slot, :], mv2[:, slot, 0:1], rstd2[:, slot:slot + 1],
                                            ALU.subtract, ALU.mult).then_inc(h_pre2, 1)

                def read_logits(n, slot, use):
                    hold(dve, h_L, n + 5)
                    nc.vector.tensor_tensor(LG[:, ds(n, 1), :], BANKS[2 + slot % 2][:, 0:E].unsqueeze(1), brs.unsqueeze(1),
                                            ALU.add).then_inc(h_lg, 1)
                walk_tiles(dve, (stats_first, 6), (stats_second, 4), (invert_second, 3), (invert_first, 5), (aggregate_first, 6),
                           (aggregate_second, 4), (norm_second, 3), (norm_first, 5), (read_logits, 0))

            @block.gpsimd
            def _(pool):
                pool.sem_inc(h_g, 4)

                def affine(n, slot, use):
                    hold(pool, h_pre2, n + 1)
                    hold(pool, h_T, n + 1)
                    hold(pool, h_copied, n + 1)
                    nc.gpsimd.tensor_tensor(z_rows[:, slot, :], pre_r[:, slot, :], gam1, ALU.mult).then_inc(h_g, 1)
                    hold(pool, h_g, n + 5)
                    nc.gpsimd.tensor_tensor(z_rows[:, slot, :], z_rows[:, slot, :], bet1, ALU.add).then_inc(h_z, 1)
                walk_tiles(pool, (affine, 3))

        with nc.Block() as block:
            router1(block)

        q_st, q_ready, q_sum, q_exp = (phase_sem("q_" + n) for n in ("st", "ready", "summed", "exp"))
        q_done = sem("q_scattered")
        tiles_i = SCR[:, 8:8 + E].bitcast(i32)
        tiles_f, tiles_end, first_slot = (SCR[:, 16 + 8 * k:24 + 8 * k] for k in range(3))
        past = SCR[0:1, 64:64 + T1 * E].rearrange("p (t e) -> p t e", e=E)
        te_f = SCR[0:1, 640:640 + T1]
        valid = r_c

        def route1(block):
            @block.vector
            def _(dve):
                st = Steps(dve, q_st)
                first_best(st, LG, r_a, OH1, r_b)
                st(nc.vector.scalar_tensor_tensor(LG[:], OH1[:], -3e38, LG[:], ALU.mult, ALU.add))
                st.wait()
                first_best(st, LG, r_c, OH2, r_b)
                st(nc.vector.tensor_tensor(keep2[:], r_c[:], r_a[:], ALU.subtract))
                st.wait()
                dve.sem_inc(q_exp, 1)
                st(nc.vector.tensor_scalar(valid[:], NIDT[:], float(NODES), None, ALU.is_lt))
                st.wait()
                st(nc.vector.tensor_tensor(OH1[:], OH1[:], bce(valid), ALU.mult))
                st(nc.vector.tensor_tensor(OH2[:], OH2[:], bce(valid), ALU.mult))
                st.wait()
                st(nc.vector.tensor_tensor(LG[:], OH1[:], OH2[:], ALU.add))
                ranks(dve, st, LG, q_ready, q_sum, 1)
                members = CUM[:, NT - 1, :]
                st(nc.vector.tensor_scalar(tiles_i, members, float(P - 1), None, ALU.add))
                st.wait()
                st(nc.vector.tensor_scalar(tiles_i, tiles_i, P.bit_length() - 1, None, ALU.arith_shift_right))
                st.wait()
                st(nc.vector.tensor_copy(tiles_f, tiles_i))
                st.wait()
                st(nc.vector.tensor_tensor_scan(tiles_end, ones[:, 0:E], tiles_f, 0.0, ALU.mult, ALU.add))
                st.wait()
                st(nc.vector.tensor_tensor(first_slot, tiles_end, tiles_f, ALU.subtract))
                st(nc.vector.tensor_tensor(past, iota[0:1, 0:T1].unsqueeze(2).to_broadcast([1, T1, E]),
                                           tiles_end[0:1, :].unsqueeze(1).to_broadcast([1, T1, E]), ALU.is_ge))
                st.wait()
                st(nc.vector.tensor_scalar(first_slot, first_slot, float(P), -1.0, ALU.mult, ALU.add))
                st(nc.vector.tensor_reduce(te_f, past, AX.X, ALU.add))
                st.wait()
                st(nc.vector.tensor_scalar(tile_expert[:], te_f, float(E - 1), None, ALU.min))
                st(nc.vector.tensor_tensor(RT[:], RT[:], bct(first_slot), ALU.add))
                st.wait()
                for a, (oh, to, frm) in enumerate(((OH1, to1, from1), (OH2, to2, from2))):
                    st(nc.vector.tensor_tensor(CUM[:], RT[:], oh[:], ALU.mult))
                    st.wait()
                    st(nc.vector.tensor_reduce(r_a[:], CUM[:], AX.X, ALU.add))
                    st.wait()
                    st(nc.vector.tensor_copy(frm[:], r_a[:]))
                    st(nc.vector.tensor_scalar(r_b[:], NIDT[:], float(TRASH1 + a * NPAD), None, ALU.add))
                    st.wait()
                    st(nc.vector.tensor_tensor(r_a[:], r_a[:], r_b[:], ALU.subtract))
                    st.wait()
                    st(nc.vector.tensor_tensor(r_a[:], r_a[:], valid[:], ALU.mult))
                    st.wait()
                    st(nc.vector.tensor_tensor(r_a[:], r_a[:], r_b[:], ALU.add))
                    st.wait()
                    st(nc.vector.tensor_copy(to[:], r_a[:]))
                    st.wait()
                    dve.sem_inc(q_ready, 1)
                dve.wait_ge(q_exp, 2)
                st(nc.vector.tensor_scalar(keep1[:], keep2[:], 1.0, None, ALU.add))
                st.wait()
                st(nc.vector.reciprocal(keep1[:], keep1[:]))
                st.wait()
                st(nc.vector.tensor_tensor(keep2[:], keep2[:], keep1[:], ALU.mult))

            @block.scalar
            def _(act):
                act.wait_ge(q_exp, 1)
                nc.scalar.activation(keep2[:], keep2[:], ACT.Exp).then_inc(q_exp, 1)

            @block.tensor
            def _(pe):
                pe_ranks(pe, LG, q_ready, q_sum, 1)

            @block.gpsimd
            def _(pool):
                for a, to in enumerate((to1, to2)):
                    pool.wait_ge(q_ready, 2 + a)
                    for t in range(NT):
                        nc.gpsimd.indirect_dma_start(
                            out=BUF1, out_offset=bass.IndirectOffsetOnAxis(ap=to[:, t:t + 1].bitcast(u32), axis=0),
                            in_=XN[:, t, :], in_offset=None).then_inc(q_done, 16)
                pool.wait_ge(q_done, 32 * NT)
                pool.wait_ge(h_big, 16 * (2 * E + 2))

        with nc.Block() as block:
            route1(block)

        end_phase()

        i_rows = [BIG[:, k * D:(k + 1) * D] for k in range(4)]
        i_xT = [BIG[:, 1024 + k * D:1024 + (k + 1) * D].rearrange("p (c n) -> p c n", c=2) for k in range(4)]
        i_h = [BIG[:, 2048 + k * H1:2048 + (k + 1) * H1] for k in range(4)]
        i_hT = [BIG[:, 4096 + k * H1:4096 + (k + 1) * H1].rearrange("p (f n) -> p f n", n=P) for k in range(2)]
        i_y = [BIG[:, 5120 + k * D:5120 + (k + 1) * D] for k in range(4)]
        i_in, i_out = [phase_sem(f"i_in{k}") for k in range(4)], sems("i_out", 4)
        i_T, i_x, i_m1, i_b1, i_gelu, i_Th, i_hTs, i_m2, i_ys, i_stored = (
            phase_sem("i_" + n) for n in ("rowsT", "xT", "hidden", "biased", "gelu", "hiddenT", "hT", "out", "y", "stored"))
        UT = 28

        def experts1(block):
            @block.sync
            def _(sp):
                with sp.Fori(0, T1 // UT) as i:
                    for k in range(UT):
                        n = i * UT + k
                        hold(sp, i_T, n + 1)
                        sp.dma_start(i_rows[k % 4], BUF1[ds(n * P, P), :]).then_inc(i_in[k % 4], 16)

            @block.tensor
            def _(pe):
                pe.sem_inc(i_T, 4)
                pe.sem_inc(i_m2, 2)
                with pe.Fori(0, T1 // UT) as i:
                    es = load_regs(ENG.PE, tile_expert[0:1, ds(i * UT, UT)], 0, E - 1)

                    def turn_rows(k):
                        n = i * UT + k
                        pe.wait_ge(i_in[k % 4], i * (4 * UT) + 16 * (k // 4 + 1))
                        pe.wait_ge(i_x, n + 1)
                        for c in range(2):
                            m = nc.tensor.transpose(BANKS[7 * (k % 2)][:, c * P:(c + 1) * P], i_rows[k % 4][:, c * P:(c + 1) * P], ident[:])
                        m.then_inc(i_T, 1)

                    def first(k):
                        n = i * UT + k
                        pe.wait_ge(i_x, n + 3)
                        pe.wait_ge(i_b1, n + 1)
                        for c in range(2):
                            m = nc.tensor.matmul(BANKS[1 + k % 2][:, 0:H1], i_xT[k % 4][:, c, :],
                                                 W1s[:, ds(es[k], 1), c, :].rearrange("p e h -> p (e h)"), start=c == 0, stop=c == 1)
                        m.then_inc(i_m1, 1)

                    def turn(k):
                        n = i * UT + k
                        pe.wait_ge(i_gelu, n + 1)
                        pe.wait_ge(i_hTs, n + 1)
                        for f in range(4):
                            m = nc.tensor.transpose(BANKS[3 + k % 2][:, f * P:(f + 1) * P], i_h[k % 4][:, f * P:(f + 1) * P], ident[:])
                        m.then_inc(i_Th, 1)

                    def second(k):
                        n = i * UT + k
                        pe.wait_ge(i_hTs, n + 3)
                        pe.wait_ge(i_ys, n + 1)
                        for f in range(4):
                            m = nc.tensor.matmul(BANKS[5 + k % 2][:, 0:D], i_hT[k % 2][:, f, :],
                                                 W2s[:, ds(es[k], 1), f, :].rearrange("p e n -> p (e n)"), start=f == 0, stop=f == 3)
                        m.then_inc(i_m2, 1)
                    turn_rows(0)
                    turn_rows(1)
                    first(0)
                    for k in range(UT):
                        if k + 2 < UT:
                            turn_rows(k + 2)
                        if k + 1 < UT:
                            first(k + 1)
                        turn(k)
                        if k:
                            second(k - 1)
                    second(UT - 1)

            @block.scalar
            def _(act):
                act.sem_inc(i_x, 2)
                nc.scalar.preload_act_table(ACT.Gelu)
                with act.Fori(0, T1 // UT) as i:
                    def rows(k):
                        hold(act, i_T, i * UT + (k + 5))
                        nc.scalar.activation(i_xT[k % 4].rearrange("p c n -> p (c n)"), BANKS[7 * (k % 2)][:, 0:D], ACT.Copy).then_inc(i_x, 1)
                    rows(0)
                    rows(1)
                    for k in range(UT):
                        if k + 2 < UT:
                            rows(k + 2)
                        hold(act, i_b1, i * UT + (k + 3))
                        nc.scalar.activation(i_h[k % 4], i_h[k % 4], ACT.Gelu).then_inc(i_gelu, 1)

            @block.vector
            def _(dve):
                dve.sem_inc(i_b1, 2)
                dve.sem_inc(i_hTs, 2)
                dve.sem_inc(i_ys, 2)
                with dve.Fori(0, T1 // UT) as i:
                    es = load_regs(ENG.DVE, tile_expert[0:1, ds(i * UT, UT)], 0, E - 1)

                    def bias(k):
                        n = i * UT + k
                        hold(dve, i_m1, n + 1)
                        nc.vector.tensor_tensor(i_h[k % 4].unsqueeze(1), BANKS[1 + k % 2][:, 0:H1].unsqueeze(1), b1r[:, ds(es[k], 1), :],
                                                ALU.add).then_inc(i_b1, 1)

                    def turn(k):
                        n = i * UT + k
                        hold(dve, i_Th, n + 1)
                        hold(dve, i_m2, n + 1)
                        nc.vector.tensor_copy(i_hT[k % 2].rearrange("p f n -> p (f n)"), BANKS[3 + k % 2][:, :]).then_inc(i_hTs, 1)

                    def finish(k):
                        n = i * UT + k
                        hold(dve, i_m2, n + 3)
                        hold(dve, i_stored, n + 1)
                        nc.vector.tensor_tensor(i_y[k % 4].unsqueeze(1), BANKS[5 + k % 2][:, 0:D].unsqueeze(1), b2r[:, ds(es[k], 1), :],
                                                ALU.add).then_inc(i_ys, 1)
                    bias(0)
                    for k in range(UT):
                        if k + 1 < UT:
                            bias(k + 1)
                        turn(k)
                        if k:
                            finish(k - 1)
                    finish(UT - 1)

            @block.gpsimd
            def _(pool):
                pool.sem_inc(i_stored, 4)
                with pool.Fori(0, T1 // UT) as i:
                    for k in range(UT):
                        n = i * UT + k
                        hold(pool, i_ys, n + 3)
                        nc.gpsimd.dma_start(Y1[ds(n * P, P), :], i_y[k % 4]).then_inc(i_out[k % 4], 16)
                        hold(pool, i_out[k % 4], i * (4 * UT) + 16 * (k // 4 + 1))
                        pool.sem_inc(i_stored, 1)

        with nc.Block() as block:
            experts1(block)

        j_rows = [ring4(a * 4 * D) for a in range(2)]
        j_in = [sems(f"j_in{a}_", 4) for a in range(2)]
        j_half, j_x, j_out = (sem("j_" + n) for n in ("first_added", "added", "out"))

        def combine(block):
            @block.gpsimd
            def _(pool):
                pool.sem_inc(j_x, 4)

                for n in range(NT):
                    pool.wait_ge(j_x, n + 1)
                    for a, at in enumerate((from1, from2)):
                        nc.gpsimd.indirect_dma_start(
                            out=j_rows[a][:, n % 4, :], out_offset=None, in_=Y1,
                            in_offset=bass.IndirectOffsetOnAxis(ap=at[:, n:n + 1].bitcast(u32), axis=0)).then_inc(j_in[a][n % 4], 16)

            @block.vector
            def _(dve):
                def first_row(n, slot, use):
                    hold(dve, j_in[0][slot], 16 * (use + 1))
                    x = X[:, ds(n, 1), :]
                    nc.vector.scalar_tensor_tensor(x, j_rows[0][:, slot:slot + 1, :], keep1[:, ds(n, 1)], x, ALU.mult, ALU.add).then_inc(j_half, 1)

                def second_row(n, slot, use):
                    hold(dve, j_in[1][slot], 16 * (use + 1))
                    hold(dve, j_half, n + 1)
                    x = X[:, ds(n, 1), :]
                    nc.vector.scalar_tensor_tensor(x, j_rows[1][:, slot:slot + 1, :], keep2[:, ds(n, 1)], x, ALU.mult, ALU.add).then_inc(j_x, 1)
                walk_tiles(dve, (first_row, 1), (second_row, 0))

            @block.sync
            def _(sp):
                with sp.Fori(0, NT - 1) as n:
                    hold(sp, j_x, n + 5)
                    sp.dma_start(out[ds(n * P, P), :], X[:, ds(n, 1), :].rearrange("p o n -> p (o n)")).then_inc(j_out, 16)
                sp.wait_ge(j_x, NT + 4)
                sp.dma_start(out[(NT - 1) * P:NODES, :], X[0:TAIL, NT - 1, :]).then_inc(j_out, 16)
                sp.wait_ge(j_out, 16 * NT)

        with nc.Block() as block:
            combine(block)


WEIGHTS = ["L0_gnn_weight", "L0_ffn_gate_w", "L0_ffn_gate_b", "L0_ffn_w1", "L0_ffn_b1", "L0_ffn_w2", "L0_ffn_b2",
           "L1_gnn_eW1", "L1_gnn_eb1", "L1_gnn_eW2", "L1_gnn_eb2", "L1_gnn_nW1", "L1_gnn_nb1", "L1_gnn_nW2",
           "L1_gnn_nb2", "L1_gnn_ln_gamma", "L1_gnn_ln_beta", "L1_ffn_gamma", "L1_ffn_beta", "L1_ffn_Wr", "L1_ffn_br",
           "L1_ffn_W1", "L1_ffn_b1", "L1_ffn_W2", "L1_ffn_b2"]


def kernel(**inputs):
    import numpy as np
    import concourse.bacc as bacc
    from concourse.bass_utils import run_bass_kernel_spmd

    pad = EROW - EDGES
    src = np.concatenate([np.asarray(inputs["src"]), np.zeros(pad, np.int32)])
    dst = np.concatenate([np.asarray(inputs["dst"]), np.full(pad, NODES, np.int32)])
    w = np.concatenate([np.asarray(inputs["edge_weight"]), np.zeros(pad, np.float32)])
    attr = np.concatenate([np.asarray(inputs["edge_attr_64"]), np.zeros((pad, ED), np.float32)])
    arrays = {
        "x": np.asarray(inputs["x"]),
        "src_tiles": src[:ET * P].reshape(ETP, ETQ * P),
        "dst_tiles": dst[:ET * P].reshape(ETP, ETQ * P),
        "w_tiles": w[:ET * P].reshape(ETP, ETQ * P),
        "dst_row": dst,
        "attr_t": attr.T,
        "nb1_col": np.asarray(inputs["L1_gnn_nb1"]).reshape(DM // P, P).T,
        "b1_col": np.asarray(inputs["L0_ffn_b1"]).reshape(E * F0 // P, P).T,
    }
    for name in WEIGHTS:
        arrays[name] = np.asarray(inputs[name])
    arrays = {n: np.ascontiguousarray(a) for n, a in arrays.items()}
    nc = bacc.Bacc("TRN2", target_bir_lowering=False, num_devices=1)
    io = {n: nc.dram_tensor(f"in_{n}", a.shape, mybir.dt.from_np(a.dtype), kind="ExternalInput").ap()
          for n, a in arrays.items()}
    out = nc.dram_tensor("out_x", (NODES, D), f32, kind="ExternalOutput").ap()
    build(nc, io, out)
    r = run_bass_kernel_spmd(nc, [{f"in_{n}": a for n, a in arrays.items()}], core_ids=[0])
    return r.results[0]["out_x"]
```
